# Optimizing a Trainium2 kernel written in Bass

```python
import numpy as np
import jax
import jax.numpy as jnp

def _softmax(x, axis=-1):
    return jax.nn.softmax(x, axis=axis)

def _gelu(x):
    return jax.nn.gelu(x, approximate=True)

def _silu(x):
    return jax.nn.silu(x)

def _sigmoid(x):
    return jax.nn.sigmoid(x)

def _layernorm(x, axis=-1, eps=1e-05):
    m = jnp.mean(x, axis=axis, keepdims=True)
    v = jnp.var(x, axis=axis, keepdims=True)
    return (x - m) / jnp.sqrt(v + eps)

def _scatter_add(tgt, idx, src, axis=0):
    return tgt.at[idx].add(src)

def _segment_sum(src, seg, n):
    return jax.ops.segment_sum(src, seg, n)
kernel_name = 'mk_adj_ffn_d2_adj_r2_9de5f5'

def setup_inputs(seed: int=0):
    np.random.seed(seed)
    _w = jnp.asarray

    def _rec_inputs():
        import jax
        import jax.numpy as jnp
        _gk = jax.random.key(seed)
        x = -0.0005207 + 1.001 * jax.random.normal(jax.random.fold_in(_gk, 1), (64, 128, 128), jnp.float32)
        _a = jax.random.bernoulli(jax.random.fold_in(_gk, 2), 0.125, (64, 128, 128))
        _a = jnp.logical_or(_a, jnp.swapaxes(_a, -1, -2))
        _a = jnp.logical_or(_a, jnp.eye(128, dtype=bool))
        adj = _a.astype(jnp.int32)
        return (x, adj)
    x, adj = _rec_inputs()

    def _L0_gnn_setup():
        import jax, jax.numpy as jnp
        import numpy as np
        B, N, IN_F, OUT_F, H, NUM_EDGE_TYPES = (16, 256, 128, 128, 8, 50)
        HEAD_DIM = OUT_F // H
        LN_EPS = 1e-05
        key = jax.random.key(seed)
        ks = jax.random.split(key, 8)
        x = jax.random.normal(ks[0], (B, N, IN_F), dtype=jnp.float32)
        adj = jax.random.randint(ks[1], (B, N, N), 0, 2, dtype=jnp.int32)
        edge_types = jax.random.randint(ks[2], (B, N, N), 0, NUM_EDGE_TYPES, dtype=jnp.int32)
        W = jax.random.normal(ks[3], (IN_F, OUT_F), dtype=jnp.float32) / np.sqrt(IN_F)
        a1 = jax.random.normal(ks[4], (HEAD_DIM,), dtype=jnp.float32) / np.sqrt(HEAD_DIM)
        a2 = jax.random.normal(ks[5], (HEAD_DIM,), dtype=jnp.float32) / np.sqrt(HEAD_DIM)
        edge_emb = jax.random.normal(ks[6], (NUM_EDGE_TYPES, H), dtype=jnp.float32) * 0.02
        edge_emb = edge_emb.at[0].set(0.0)
        ln_gamma = jnp.ones((OUT_F,), dtype=jnp.float32)
        ln_beta = jnp.zeros((OUT_F,), dtype=jnp.float32)
        return {'x': x, 'adj': adj, 'edge_types': edge_types, 'W': W, 'a1': a1, 'a2': a2, 'edge_emb': edge_emb, 'ln_gamma': ln_gamma, 'ln_beta': ln_beta}
    _L0_gnn_all = _L0_gnn_setup()
    _L0_gnn_in = {k: v for k, v in _L0_gnn_all.items() if k in ('W', 'a1', 'a2', 'edge_emb', 'ln_gamma', 'ln_beta')}
    del _L0_gnn_all

    def _L0_ffn_setup():
        import jax, jax.numpy as jnp
        import numpy as np
        D_MODEL = 128
        N_EXPERTS = 16
        HIDDEN = 256
        SCALE = 0.02
        key = jax.random.key(seed)
        ks = jax.random.split(key, 5)
        x = jax.random.normal(ks[0], (4, 4096, D_MODEL), dtype=jnp.float32)
        gate_w = jax.random.normal(ks[1], (D_MODEL, N_EXPERTS), dtype=jnp.float32) * SCALE
        gate_b = jnp.zeros((N_EXPERTS,), dtype=jnp.float32)
        w1 = jax.random.normal(ks[2], (N_EXPERTS, D_MODEL, HIDDEN), dtype=jnp.float32) * SCALE
        w2 = jax.random.normal(ks[3], (N_EXPERTS, D_MODEL, HIDDEN), dtype=jnp.float32) * SCALE
        w3 = jax.random.normal(ks[4], (N_EXPERTS, HIDDEN, D_MODEL), dtype=jnp.float32) * SCALE
        return {'x': x, 'gate_w': gate_w, 'gate_b': gate_b, 'w1': w1, 'w2': w2, 'w3': w3}
    _L0_ffn_all = _L0_ffn_setup()
    _L0_ffn_in = {k: v for k, v in _L0_ffn_all.items() if k in ('gate_w', 'gate_b', 'w1', 'w2', 'w3')}
    del _L0_ffn_all

    def _L1_gnn_setup():
        import jax, jax.numpy as jnp
        import numpy as np
        OUT = 128
        NUM_LAYERS = 3

        def _gru_cell(inp, h, w_ih, w_hh, b_ih, b_hh):
            gi = inp @ w_ih.T + b_ih
            gh = h @ w_hh.T + b_hh
            i_r, i_z, i_n = jnp.split(gi, 3, axis=-1)
            h_r, h_z, h_n = jnp.split(gh, 3, axis=-1)
            r = jax.nn.sigmoid(i_r + h_r)
            z = jax.nn.sigmoid(i_z + h_z)
            n = jnp.tanh(i_n + r * h_n)
            return (1.0 - z) * n + z * h
        key = jax.random.key(seed)
        ks = jax.random.split(key, 8)
        B, N, D = (32, 256, 128)
        x = jax.random.normal(ks[0], (B, N, D), dtype=jnp.float32)
        adj = jax.random.randint(ks[1], (B, N, N), 0, 2, dtype=jnp.int32)
        s = 1.0 / np.sqrt(OUT)
        weight = jax.random.uniform(ks[2], (NUM_LAYERS, OUT, OUT), jnp.float32, -s, s)
        w_ih = jax.random.uniform(ks[3], (3 * OUT, OUT), jnp.float32, -s, s)
        w_hh = jax.random.uniform(ks[4], (3 * OUT, OUT), jnp.float32, -s, s)
        b_ih = jax.random.uniform(ks[5], (3 * OUT,), jnp.float32, -s, s)
        b_hh = jax.random.uniform(ks[6], (3 * OUT,), jnp.float32, -s, s)
        return {'x': x, 'adj': adj, 'weight': weight, 'w_ih': w_ih, 'w_hh': w_hh, 'b_ih': b_ih, 'b_hh': b_hh}
    _L1_gnn_all = _L1_gnn_setup()
    _L1_gnn_in = {k: v for k, v in _L1_gnn_all.items() if k in ('weight', 'w_ih', 'w_hh', 'b_ih', 'b_hh')}
    del _L1_gnn_all

    def _L1_ffn_setup():
        import jax, jax.numpy as jnp
        import numpy as np
        TOP_K = 2
        key = jax.random.key(seed)
        ks = jax.random.split(key, 4)
        B, L, D, H, E = (8, 2048, 128, 512, 8)
        s = 0.02
        return {'x': jax.random.normal(ks[0], (B, L, D), jnp.float32), 'Wg': jax.random.normal(ks[1], (D, E), jnp.float32) * s, 'bg': jnp.zeros((E,), jnp.float32), 'W1': jax.random.normal(ks[2], (E, D, H), jnp.float32) * s, 'b1': jnp.zeros((E, H), jnp.float32), 'W2': jax.random.normal(ks[3], (E, H, D), jnp.float32) * s, 'b2': jnp.zeros((E, D), jnp.float32)}
    _L1_ffn_all = _L1_ffn_setup()
    _L1_ffn_in = {k: v for k, v in _L1_ffn_all.items() if k in ('Wg', 'bg', 'W1', 'b1', 'W2', 'b2')}
    del _L1_ffn_all
    return {'x': x, 'adj': adj, 'L0_gnn_W': _L0_gnn_in['W'], 'L0_gnn_a1': _L0_gnn_in['a1'], 'L0_gnn_a2': _L0_gnn_in['a2'], 'L0_gnn_edge_emb': _L0_gnn_in['edge_emb'], 'L0_gnn_ln_gamma': _L0_gnn_in['ln_gamma'], 'L0_gnn_ln_beta': _L0_gnn_in['ln_beta'], 'L0_ffn_gate_w': _L0_ffn_in['gate_w'], 'L0_ffn_gate_b': _L0_ffn_in['gate_b'], 'L0_ffn_w1': _L0_ffn_in['w1'], 'L0_ffn_w2': _L0_ffn_in['w2'], 'L0_ffn_w3': _L0_ffn_in['w3'], 'L1_gnn_weight': _L1_gnn_in['weight'], 'L1_gnn_w_ih': _L1_gnn_in['w_ih'], 'L1_gnn_w_hh': _L1_gnn_in['w_hh'], 'L1_gnn_b_ih': _L1_gnn_in['b_ih'], 'L1_gnn_b_hh': _L1_gnn_in['b_hh'], 'L1_ffn_Wg': _L1_ffn_in['Wg'], 'L1_ffn_bg': _L1_ffn_in['bg'], 'L1_ffn_W1': _L1_ffn_in['W1'], 'L1_ffn_b1': _L1_ffn_in['b1'], 'L1_ffn_W2': _L1_ffn_in['W2'], 'L1_ffn_b2': _L1_ffn_in['b2']}

def reference(x, adj, L0_gnn_W, L0_gnn_a1, L0_gnn_a2, L0_gnn_edge_emb, L0_gnn_ln_gamma, L0_gnn_ln_beta, L0_ffn_gate_w, L0_ffn_gate_b, L0_ffn_w1, L0_ffn_w2, L0_ffn_w3, L1_gnn_weight, L1_gnn_w_ih, L1_gnn_w_hh, L1_gnn_b_ih, L1_gnn_b_hh, L1_ffn_Wg, L1_ffn_bg, L1_ffn_W1, L1_ffn_b1, L1_ffn_W2, L1_ffn_b2):
    import jax
    import jax.numpy as jnp

    def _L0_gnn_ref(x, adj, edge_types, W, a1, a2, edge_emb, ln_gamma, ln_beta):
        import jax, jax.numpy as jnp
        import numpy as np
        B, N, IN_F, OUT_F, H, NUM_EDGE_TYPES = (16, 256, 128, 128, 8, 50)
        HEAD_DIM = OUT_F // H
        LN_EPS = 1e-05
        Bx, Nx, _ = x.shape
        Wh = (x @ W).reshape(Bx, Nx, H, HEAD_DIM)
        s1 = jnp.einsum('bnhd,d->bnh', Wh, a1)
        s2 = jnp.einsum('bnhd,d->bnh', Wh, a2)
        e = s1[:, :, None, :] + s2[:, None, :, :] + edge_emb[edge_types]
        e = jnp.where(e > 0, e, 0.2 * e)
        e = jnp.where((adj == 0)[..., None], jnp.float32(-1000000000.0), e)
        alpha = jax.nn.softmax(e, axis=2)
        h = jnp.einsum('bijh,bjhd->bihd', alpha, Wh).reshape(Bx, Nx, OUT_F)
        mu = jnp.mean(h, axis=-1, keepdims=True)
        var = jnp.mean(jnp.square(h - mu), axis=-1, keepdims=True)
        hn = (h - mu) * jax.lax.rsqrt(var + LN_EPS) * ln_gamma + ln_beta
        return jax.nn.elu(hn)

    def _L0_ffn_ref(x, gate_w, gate_b, w1, w2, w3):
        import jax, jax.numpy as jnp
        import numpy as np
        D_MODEL = 128
        N_EXPERTS = 16
        HIDDEN = 256
        SCALE = 0.02
        n_experts = w1.shape[0]
        logits = jnp.einsum('bsd,de->bse', x, gate_w) + gate_b
        probs = jax.nn.softmax(logits, axis=-1)
        top_probs, top_idx = jax.lax.top_k(probs, 2)
        top_probs = top_probs / jnp.sum(top_probs, axis=-1, keepdims=True)
        dispatch = jnp.sum(jax.nn.one_hot(top_idx, n_experts, dtype=x.dtype) * top_probs[..., None], axis=-2)
        h1 = jnp.einsum('bsd,edh->bseh', x, w1)
        h2 = jnp.einsum('bsd,edh->bseh', x, w2)
        hidden = jax.nn.silu(h1) * h2
        expert_out = jnp.einsum('bseh,eho->bseo', hidden, w3)
        return jnp.einsum('bseo,bse->bso', expert_out, dispatch)

    def _L1_gnn_ref(x, adj, weight, w_ih, w_hh, b_ih, b_hh):
        import jax, jax.numpy as jnp
        import numpy as np
        OUT = 128
        NUM_LAYERS = 3

        def _gru_cell(inp, h, w_ih, w_hh, b_ih, b_hh):
            gi = inp @ w_ih.T + b_ih
            gh = h @ w_hh.T + b_hh
            i_r, i_z, i_n = jnp.split(gi, 3, axis=-1)
            h_r, h_z, h_n = jnp.split(gh, 3, axis=-1)
            r = jax.nn.sigmoid(i_r + h_r)
            z = jax.nn.sigmoid(i_z + h_z)
            n = jnp.tanh(i_n + r * h_n)
            return (1.0 - z) * n + z * h
        A = (adj != 0).astype(x.dtype)
        h = x
        L = weight.shape[0]
        for i in range(L):
            m = jnp.einsum('bnd,de->bne', h, weight[i])
            aggr = jnp.einsum('bst,bsd->btd', A, m)
            h = _gru_cell(aggr, h, w_ih, w_hh, b_ih, b_hh)
        return h

    def _L1_ffn_ref(x, Wg, bg, W1, b1, W2, b2):
        import jax, jax.numpy as jnp
        import numpy as np
        TOP_K = 2
        B, L, D = x.shape
        E = W1.shape[0]
        xf = x.reshape(-1, D)
        gate_logits = xf @ Wg + bg
        top_w, top_i = jax.lax.top_k(gate_logits, TOP_K)
        top_w = jax.nn.softmax(top_w, axis=-1)
        w_dense = jnp.sum(jax.nn.one_hot(top_i, E, dtype=xf.dtype) * top_w[..., None], axis=1)
        out = jnp.zeros_like(xf)
        for e in range(E):
            h = jax.nn.gelu(xf @ W1[e] + b1[e], approximate=False)
            out = out + w_dense[:, e:e + 1] * (h @ W2[e] + b2[e])
        return out.reshape(B, L, D)
    x = x + _L0_gnn_ref(_layernorm(x, axis=-1), adj, adj, L0_gnn_W, L0_gnn_a1, L0_gnn_a2, L0_gnn_edge_emb, L0_gnn_ln_gamma, L0_gnn_ln_beta)
    x = x + _L0_ffn_ref(_layernorm(x, axis=-1), L0_ffn_gate_w, L0_ffn_gate_b, L0_ffn_w1, L0_ffn_w2, L0_ffn_w3)
    x = x + _L1_gnn_ref(_layernorm(x, axis=-1), adj, L1_gnn_weight, L1_gnn_w_ih, L1_gnn_w_hh, L1_gnn_b_ih, L1_gnn_b_hh)
    x = x + _L1_ffn_ref(_layernorm(x, axis=-1), L1_ffn_Wg, L1_ffn_bg, L1_ffn_W1, L1_ffn_b1, L1_ffn_W2, L1_ffn_b2)
    return x

_drawn_inputs = setup_inputs


def setup_inputs(seed=0):
    import zlib

    import numpy as np

    out = dict(_drawn_inputs(seed))
    spreads = {'L0_gnn_ln_gamma': (1.0, 0.2),
     'L0_gnn_ln_beta': (0.0, 0.1),
     'L0_ffn_gate_b': (0.0, 0.8),
     'L1_ffn_bg': (0.0, 0.35),
     'L1_ffn_b1': (0.0, 0.751),
     'L1_ffn_b2': (0.0, 0.522)}
    factors = {'L0_gnn_edge_emb': 4.082,
     'L0_ffn_gate_w': 8.0,
     'L0_ffn_w1': 8.0,
     'L0_ffn_w2': 8.0,
     'L0_ffn_w3': 8.0,
     'L1_gnn_b_ih': 3.67,
     'L1_gnn_b_hh': 5.628,
     'L1_ffn_W1': 5.741}
    for name, (base, spread) in spreads.items():
        noise = np.random.default_rng([zlib.crc32(name.encode()), seed]).standard_normal(out[name].shape)
        drawn = base * np.exp(spread * noise) if base else spread * noise
        out[name] = jnp.asarray(drawn.astype(out[name].dtype))
    for name, factor in factors.items():
        out[name] = (out[name] * factor).astype(out[name].dtype)
    return out
```

```python
import concourse.bass as bass
from concourse import mybir
from contextlib import ExitStack

F32 = mybir.dt.float32
BF16 = mybir.dt.bfloat16
I32 = mybir.dt.int32
U32 = mybir.dt.uint32
ALU = mybir.AluOpType
ACT = mybir.ActivationFunctionType
AX = mybir.AxisListType

P = 128
B = 64
N = 128
D = 128
Q = 4
NG = B // Q
QN = Q * N
H = 8
HD = D // H
PARTS = 3
KP = 32 * (PARTS - 1) + 2 * H
EPS = 1e-5
MASKED = -1e9
LAYERS = 3

E0, H0 = 16, 256
E1, H1 = 8, 512
PAIRS = 2 * B * N
CAP = B * N + P
T0 = PAIRS // P + E0
T1 = PAIRS // P + E1


class Group:

    def __init__(self, u, b):
        self.u, self.b, self.g = u, b, u * 2 + b

    def prev(self):
        return Group(self.u, 0) if self.b else Group(self.u - 1, 1)


class Tile:

    def __init__(self, i, off):
        self.i, self.off, self.g, self.m = i, off, i * 8 + off, off % 8

    def back(self, n, T):
        if isinstance(self.g, int) and not 0 <= self.g - n < T:
            return None
        return Tile(self.i, self.off - n)

    def uses(self, n):
        return self.i * (8 // n) + self.off // n + 1


def early(G, n):
    return isinstance(G.g, int) and G.g < n


class Chain:

    def __init__(self, eng, sem, n, g):
        self.eng, self.sem, self.n, self.g, self.k = eng, sem, n, g, 0

    def step(self, ins, apart=None):
        self.k += 1
        ins.then_inc(self.sem, 1)
        self.eng.wait_ge(self.sem, self.g * self.n + self.k)
        if apart:
            apart(self.eng)

    def end(self):
        assert self.k == self.n, (self.sem, self.k, self.n)


def two_layers(nc, x, adj, gat_w, gat_a1, gat_a2, gat_emb, gat_gamma, gat_beta, gate0_w, gate0_b, w1, w2, w3,
               gru_w, w_ih, w_hh, b_ih, b_hh, gate1_w, gate1_b, v1, c1, v2, c2, out):
    with ExitStack() as ctx:
        def sb(name, shape, dt=F32):
            return ctx.enter_context(nc.sbuf_tensor(name, shape, dt))

        def ps(name, shape, dt=F32):
            return ctx.enter_context(nc.psum_tensor(name, shape, dt))

        def sem(name):
            return ctx.enter_context(nc.semaphore(name))

        ident = sb("ident", [P, P])
        identb = sb("identb", [P, P], BF16)
        before = sb("before", [P, P], BF16)
        onesb = sb("onesb", [P, P], BF16)
        sel = sb("sel", [KP, 2 * H, P], BF16)
        rev = sb("rev", [P, E0])
        base = sb("base", [P, E0])
        not_hi = sb("not_hi", [KP, 1])
        is_lo = sb("is_lo", [KP, 1])
        slope = sb("slope", [KP, 1])
        minus_half = sb("minus_half", [P, Q])
        lane = sb("lane", [P, 1])
        zeros = sb("zeros", [P, D])
        tile_no = sb("tile_no", [1, T0])

        gat_w_sb = sb("gat_w_sb", [P, D])
        a_rows = sb("a_rows", [P, 2, HD])
        wa = sb("wa", [P, 2, H])
        prod = sb("prod", [P, D])
        wa_dup = sb("wa_dup", [P, 2, KP])
        emb = sb("emb", [KP, 1])
        gamma = sb("gamma", [P, D])
        beta = sb("beta", [P, D])
        gate0_sb = sb("gate0_sb", [P, E0])
        gate0_bias = sb("gate0_bias", [P, E0])
        gate1_sb = sb("gate1_sb", [P, E1])
        gate1_bias = sb("gate1_bias", [P, E1])

        xs = sb("xs", [P, B, D])
        edges = sb("edges", [P, B, N], BF16)
        slot_all = sb("slot_all", [P, B, 2])
        gate_all = sb("gate_all", [P, B, 2])

        adj_in = sb("adj_in", [P, 2, Q, N], I32)
        mask = sb("mask", [P, 2, Q, N], BF16)
        stats = sb("stats", [P, Q, 6])
        moments = sb("moments", [P, Q, 2])
        var_eps = sb("var_eps", [P, Q])
        rstd = sb("rstd", [P, Q])
        stats3 = sb("stats3", [P, Q, 6])
        moments3 = sb("moments3", [P, Q, 2])
        var_eps3 = sb("var_eps3", [P, Q])
        rstd3 = sb("rstd3", [P, Q])
        wide = sb("wide", [P, 20, QN])

        def one(k):
            return wide[:, k, :]

        def pair(k):
            return wide[:, k:k + 2, :]

        def by_graph(t):
            return t.rearrange("p (q d) -> p q d", q=Q)

        y, yT = by_graph(one(0)), one(1)
        values = sb("values", [P, 2, Q, H, HD + 1])
        s1, s2, top, part_b = (wide[0:KP, k, :] for k in (2, 3, 4, 5))
        part_a = sb("part_a", [KP, QN], BF16)
        part_c = sb("part_c", [KP, QN], BF16)
        s2_parts = sb("s2_parts", [KP, 2, QN], BF16)
        s1_parts = sb("s1_parts", [KP, QN], BF16)
        rowmax = sb("rowmax", [P, Q, H])
        rowmax_dup = sb("rowmax_dup", [P, Q, KP])
        exp1, exp2, probs = pair(6), pair(8), pair(10)
        rden = sb("rden", [P, 2, Q // 2 * H])
        hn, hneg, hexp, ygT = by_graph(one(12)), by_graph(one(13)), by_graph(one(14)), one(15)
        yg = sb("yg", [P, 2, Q, D])
        lg = sb("lg", [P, Q, E0])
        lg2 = sb("lg2", [P, Q, E0])
        score = sb("score", [P, Q, E0])
        first = sb("first", [P, Q, E0])
        second = sb("second", [P, Q, E0])
        peak = sb("peak", [P, Q, 2])
        rmax = sb("rmax", [P, Q])
        gap = sb("gap", [P, Q])
        egap = sb("egap", [P, Q])
        chosen = sb("chosen", [P, Q, E0], BF16)
        seen = sb("seen", [P, Q + 1, E0], BF16)
        rank = sb("rank", [P, Q, E0])
        slot_f = sb("slot_f", [P, Q, 2])
        slot_u = sb("slot_u", [P, 2, Q, 2], U32)
        wgt = sb("wgt", [P, Q, 2])

        x_tile = one(0).rearrange("p (k d) -> p k d", k=4)
        xT_tile = one(1).rearrange("p (k d) -> p k d", k=4)
        silu, hid, hidT = pair(2), pair(4), pair(6)
        y_tile = one(8).rearrange("p (k d) -> p k d", k=4)
        counts = sb("counts", [P, E0])
        pad_f = sb("pad_f", [P, E0])
        pad_u = sb("pad_u", [P, E0], U32)
        tiles_i = sb("tiles_i", [P, 2, E0], I32)
        tiles_f = sb("tiles_f", [P, E0])
        ends = sb("ends", [P, 2, E0])
        closer = sb("closer", [P, E0])
        moved = sb("moved", [P, 2 * B])
        expert_f = sb("expert_f", [1, T0])
        start_f = sb("start_f", [1, T0])
        tile_row = sb("tile_row", [1, T0], I32)
        tile_expert = sb("tile_expert", [1, T0], I32)
        w12_sb = sb("w12_sb", [P, E0, 2 * H0])
        w3_sb = sb("w3_sb", [P, E0, H0 // P, D])
        v1_sb = w12_sb[:, 0:E1, :]
        v2_sb = w12_sb[:, E1:2 * E1, :].rearrange("p e (c d) -> p e c d", d=D)
        bias_rows = wide[0:KP, 12:20, :].rearrange("p k n -> p (k n)")
        c1_parts = sb("c1_parts", [KP, E1 * H1], BF16)
        c2_parts = sb("c2_parts", [KP, E1 * D], BF16)

        hT, msg, agg, adj32, gate_r, gate_z, cand = (pair(k) for k in (0, 2, 4, 6, 8, 10, 12))
        got = wide[:, 16:20, :].rearrange("p (b k) n -> p b (k n)", b=2).rearrange("p b (q k d) -> p b q k d", q=Q, k=2)
        near = sb("near", [P, 2, 2 * Q], U32)
        from_u = sb("from_u", [P, 2 * B], U32)
        gru_w_sb = sb("gru_w_sb", [P, LAYERS, D])
        gru_in = sb("gru_in", [P, 2, 3, D])
        gru_wT = sb("gru_wT", [P, 2, 3, D])
        gru_b = sb("gru_b", [P, 2, 3])
        bias_rz = sb("bias_rz", [P, 2])

        ring = ps("ring", [P, 3, QN])
        tp = ps("tp", [P, QN])
        tp3 = ps("tp3", [P, QN])
        heads = ps("heads", [P, 2, QN])
        small = ps("small", [P, QN])

        rows0 = nc.dram_tensor("rows0", (E0 * CAP + E0 * P, D), F32, kind="Internal").ap()
        outs0 = nc.dram_tensor("outs0", (T0 * P, D), F32, kind="Internal").ap()
        rows1 = nc.dram_tensor("rows1", (E1 * CAP + E1 * P, D), F32, kind="Internal").ap()
        outs1 = nc.dram_tensor("outs1", (T1 * P, D), F32, kind="Internal").ap()

        c_passed, c_consts, c_small, c_wa = sem("c_passed"), sem("c_consts"), sem("c_small"), sem("c_wa")
        x_in = [sem("x_in0"), sem("x_in1")]
        adj_read = sem("adj_read")
        a_chain, s_chain, v_chain, f_chain, f_chain2 = (sem(f"{n}_chain") for n in ("ln", "split", "max", "fin", "gate"))
        a_var, a_rstd, a_y, a_yTp, a_yT, a_whp, a_wh = (
            sem(n) for n in ("a_var", "a_rstd", "a_y", "a_yTp", "a_yT", "a_whp", "a_wh"))
        a_s2p, a_s1p, a_s2, a_s1, a_s2parts, a_s1parts = (
            sem(n) for n in ("a_s2p", "a_s1p", "a_s2", "a_s1", "a_s2parts", "a_s1parts"))
        a_maximg, a_rowmax, a_dup, a_maxT = (sem(n) for n in ("a_maximg", "a_rowmax", "a_dup", "a_maxT"))
        p_img1, p_img2, p_exp1, p_exp2, p_probs, p_heads = (
            sem(n) for n in ("p_img1", "p_img2", "p_exp1", "p_exp2", "p_probs", "p_heads"))
        f_var, f_rstd, f_neg, f_exp, f_y, f_yTp, f_yT, f_lgp = (
            sem(n) for n in ("f_var", "f_rstd", "f_neg", "f_exp", "f_y", "f_yTp", "f_yT", "f_lgp"))
        g_gap, g_egap, g_chosen, g_rankp, g_slot = (
            sem(n) for n in ("g_gap", "g_egap", "g_chosen", "g_rankp", "g_slot"))
        sent = [sem("sent0"), sem("sent1")]
        stored = sem("stored")
        i_chain, m_from, r_near = sem("i_chain"), sem("m_from"), sem("r_near")
        c_zero, b_chain = sem("c_zero"), sem("b_chain")
        c_weights1 = sem("c_weights1")
        c_weights, c_gru, c_gruT, c_bias = sem("c_weights"), sem("c_gru"), sem("c_gruT"), sem("c_bias")
        m_count, m_pad, m_padded, m_table, m_chain = (
            sem(n) for n in ("m_count", "m_pad", "m_padded", "m_table", "m_chain"))
        T_SEMS = ("xTp", "xT", "hp", "act", "hid", "hidTp", "hidT", "yp", "y")
        tiles = [{n: sem(f"t{k}_{n}") for n in T_SEMS} for k in range(2)]
        for k in range(2):
            tiles[k]["in"] = [sem(f"t{k}_in{j}") for j in range(4)]
            tiles[k]["out"] = [sem(f"t{k}_out{j}") for j in range(4)]
        r_combined, r_yTp, r_h0, r_adj, r_mp, r_m, r_aggp, r_agg, r_rz, r_sig, r_t, r_n, r_backp = (
            sem(f"r_{n}") for n in ("combined", "yTp", "h0", "adj", "mp", "m", "aggp", "agg", "rz", "sig", "t",
                                    "n", "backp"))
        r_h = [sem("r_hA"), sem("r_hB")]
        r_chain, r_chain2, r_xn, r_back = (sem(f"r_{n}") for n in ("chain", "chain2", "xn", "back"))
        got_in = [sem("got_in0"), sem("got_in1")]
        last_in = [sem("last_in0"), sem("last_in1")]
        last_done, last_chain = sem("last_done"), sem("last_chain")
        GATE = ("chain", "var", "rstd", "y", "yTp", "yT", "lgp", "gap", "egap", "chosen", "rankp", "slot")
        gates = [dict(zip(GATE, (f_chain2, f_var, f_rstd, f_y, f_yTp, f_yT, f_lgp, g_gap, g_egap, g_chosen, g_rankp,
                                 g_slot))),
                 {n: sem(f"g1_{n}") for n in GATE}]
        sents = [sent, [sem("sent2"), sem("sent3")]]
        rows, results = [rows0, rows1], [outs0, outs1]
        mixtures = [(E0, H0, T0), (E1, H1, T1)]

        block = ctx.enter_context(nc.Block())

        def attention_steps(eng, work):
            work(Group(0, 0), True, False)
            work(Group(0, 1), True, True)
            with eng.Fori(1, NG // 2) as u:
                work(Group(u, 0), True, True)
                work(Group(u, 1), True, True)
            work(Group(NG // 2, 0), False, True)

        def tile_steps(eng, T, work):
            for s in range(8):
                work(Tile(0, s), T)
            with eng.Fori(1, T // 8) as i:
                for c in range(8):
                    work(Tile(i, c), T)
            for s in range(T, T + 6):
                work(Tile(0, s), T)

        def recurrence_steps(eng, work):
            work(0, True)
            with eng.Fori(1, NG // 2 - 1) as u:
                work(u, True)
            work(NG // 2 - 1, False)

        def turn(G, l):
            return G.u * (2 * LAYERS) + (2 * l + G.b + 1)

        def norm(G, layer, n):
            return G.g * 2 + n if layer == 0 else G.u * 4 + (2 * (n - 1) + G.b + 1)

        def last_steps(eng, work):
            work(Group(0, 0))
            work(Group(0, 1))
            with eng.Fori(1, NG // 2) as u:
                work(Group(u, 0))
                work(Group(u, 1))

        def apart(eng):
            eng.sem_inc(c_passed, 1)

        def graphs(t, g):
            return t[:, bass.ds(g * Q, Q)]

        @block.sync
        def _(sp):
            for dst, src in (
                    (gat_w_sb[:, :], gat_w), (gate0_sb[:, :], gate0_w), (gate1_sb[:, :], gate1_w),
                    (a_rows[:, 0, :], gat_a1.partition_broadcast(P)), (a_rows[:, 1, :], gat_a2.partition_broadcast(P)),
                    (gamma[:, :], gat_gamma.partition_broadcast(P)), (beta[:, :], gat_beta.partition_broadcast(P)),
                    (gate0_bias[:, :], gate0_b.partition_broadcast(P)),
                    (gate1_bias[:, :], gate1_b.partition_broadcast(P))):
                sp.dma_start(dst, src).then_inc(c_small, 16)
            sp.wait_ge(c_zero, 1)
            for c in range(PARTS):
                sp.dma_start(wide[32 * c:32 * c + 1, 8:8 + E1 * D // QN, :].rearrange("p k n -> p (k n)"),
                             c2.rearrange("(a e) d -> a (e d)", a=1)).then_inc(c_bias, 16)
                sp.dma_start(bias_rows[32 * c:32 * c + 1, :], c1.rearrange("(a e) h -> a (e h)", a=1)).then_inc(c_bias, 16)
            sp.wait_ge(c_consts, 1)
            for c in range(PARTS):
                for k in range(2):
                    r = 32 * c + H * k
                    sp.dma_start(emb[r:r + H, :], gat_emb[1:2, :].rearrange("a h -> h a"),
                                 allow_slow_non_contiguous=True).then_inc(c_small, 16)

            def load(G, prepare, attend):
                if prepare:
                    if not early(G, 2):
                        sp.wait_ge(adj_read, G.g - 1)
                    sp.dma_start(graphs(xs, G.g), x[bass.ds(G.g * Q, Q)].rearrange("q n f -> n q f")).then_inc(
                        x_in[G.b], 16)
                    sp.dma_start(adj_in[:, G.b], adj[bass.ds(G.g * Q, Q)].rearrange("q i j -> i q j")).then_inc(
                        x_in[G.b], 16)

            attention_steps(sp, load)

            def mixture(k):
                E, HID, T = mixtures[k]
                t_ = tiles[k]
                sp.wait_ge(m_table, k + 1)
                for b in range(2):
                    sp.wait_ge(sents[k][b], NG // 2 * 2 * Q * 16)
                sp.wait_ge(m_padded, 16 * (E0 + (E1 if k else 0) + 2))

                def work(t, T):
                    a = t.back(0, T)
                    if a:
                        if not early(a, 4):
                            sp.wait_ge(t_["xTp"], a.g - 3)
                        row = sp.value_load(tile_row[0:1, bass.ds(a.g, 1)], min_val=0, max_val=E * CAP + (E - 1) * P)
                        sp.dma_start(x_tile[:, a.m % 4, :], rows[k][bass.ds(row, P), :]).then_inc(
                            t_["in"][a.m % 4], 16)
                    a = t.back(5, T)
                    if a:
                        sp.wait_ge(t_["y"], a.g + 1)
                        sp.dma_start(results[k][bass.ds(a.g * P, P), :], y_tile[:, a.m % 4, :]).then_inc(
                            t_["out"][a.m % 4], 16)

                tile_steps(sp, T, work)

            mixture(0)
            mixture(1)

            def store(G):
                sp.wait_ge(last_done, G.g + 1)
                apart(sp)
                sp.dma_start(out[bass.ds(G.g * Q, Q)].rearrange("q n f -> n q f"), graphs(xs, G.g)).then_inc(
                    stored, 16)

            last_steps(sp, store)
            sp.wait_ge(stored, NG * 16)

        @block.gpsimd
        def _(pool):
            pool.memset(emb[:, :], 0.0).then_inc(c_consts, 1)
            k = [1]

            def after(ins):
                k[0] += 1
                ins.then_inc(c_consts, 1)
                pool.wait_ge(c_consts, k[0])

            def choose(t, pattern, base_, mult, op, fill):
                after(pool.affine_select(out=t, in_=t, pattern=pattern, compare_op=op, fill=fill, base=base_,
                                         channel_multiplier=mult))

            after(pool.memset(ident[:, :], 0.0))
            choose(ident[:, :], [[-1, P]], 0, 1, ALU.not_equal, 1.0)
            after(pool.tensor_copy(identb[:, :], ident[:, :]))
            after(pool.memset(before[:, :], 0.0))
            choose(before[:, :], [[-1, P]], 0, 1, ALU.is_ge, 1.0)
            after(pool.memset(onesb[:, :], 1.0))
            after(pool.memset(sel[:, :, :], 0.0))
            for c in range(PARTS):
                choose(sel[:, :, :], [[-1, 2 * H], [0, P]], -32 * c, 1, ALU.not_equal, 1.0)
            after(pool.iota(rev[:, :], [[-1, E0]], base=E0, channel_multiplier=0, allow_small_or_imprecise_dtypes=True))
            after(pool.iota(base[:, :], [[CAP, E0]], base=0, channel_multiplier=0, allow_small_or_imprecise_dtypes=True))
            after(pool.iota(lane[:, :], [[0, 1]], base=0, channel_multiplier=1, allow_small_or_imprecise_dtypes=True))
            after(pool.iota(tile_no[:, :], [[1, T0]], base=0, channel_multiplier=0, allow_small_or_imprecise_dtypes=True))
            after(pool.memset(not_hi[:, :], -1.0))
            choose(not_hi[:, :], [[0, 1]], -32, 1, ALU.is_ge, 0.0)
            after(pool.memset(is_lo[:, :], -1.0))
            choose(is_lo[:, :], [[0, 1]], -64, 1, ALU.is_ge, 0.0)
            after(pool.memset(slope[:, :], 1.0))
            for c in range(PARTS):
                choose(slope[:, :], [[0, 1]], 32 * c + H, -1, ALU.is_gt, 0.2)
                choose(slope[:, :], [[0, 1]], 32 * c + 32, -1, ALU.is_gt, 1.0)
            after(pool.memset(minus_half[:, :], -0.5))
            after(pool.memset(zeros[:, :], 0.0))
            after(pool.memset(wa_dup[:, :, :], 0.0))
            after(pool.memset(rowmax_dup[:, :, :], 0.0))
            after(pool.memset(seen[:, 0, :], 0.0))
            after(pool.memset(values[:, :, :, :, :], 1.0))
            assert k[0] == CONSTS, k[0]

            def work(G, prepare, attend):
                if prepare:
                    pool.wait_ge(a_var, G.g + 1)
                    pool.tensor_tensor(rstd[:, :], var_eps[:, :], minus_half[:, :], ALU.pow).then_inc(a_rstd, 1)
                if attend:
                    G = G.prev()
                    for k in (1, 2):
                        power(G, 0, k)
                    send(G, 0)

            def power(G, k, n):
                pool.wait_ge(gates[k]["var"], norm(G, k, n))
                pool.tensor_tensor(rstd3[:, :], var_eps3[:, :], minus_half[:, :], ALU.pow).then_inc(
                    gates[k]["rstd"], 1)

            def send(G, layer):
                pool.wait_ge(gates[layer]["slot"], G.g + 1)
                apart(pool)
                for q in range(Q):
                    for k in range(2):
                        pool.indirect_dma_start(
                            rows[layer], bass.IndirectOffsetOnAxis(ap=slot_u[:, G.b, q, k:k + 1], axis=0),
                            yg[:, G.b, q, :], None).then_inc(sents[layer][G.b], 16)

            def fetch(G, layer, combined, sems):
                if not early(G, 2):
                    pool.wait_ge(combined, G.g - 1)
                    apart(pool)
                pool.tensor_copy(near[:, G.b], from_u[:, bass.ds(G.g * (2 * Q), 2 * Q)]).then_inc(
                    r_near, 1)
                pool.wait_ge(r_near, G.g + (layer * NG + 1))
                apart(pool)
                for q in range(Q):
                    for k in range(2):
                        pool.indirect_dma_start(
                            got[:, G.b, q, k, :], None, results[layer],
                            bass.IndirectOffsetOnAxis(ap=near[:, G.b, 2 * q + k:2 * q + k + 1], axis=0)).then_inc(sems[G.b], 16)

            def pad(k):
                pool.wait_ge(m_pad, k + 1)
                for e in range(mixtures[k][0]):
                    pool.indirect_dma_start(rows[k], bass.IndirectOffsetOnAxis(ap=pad_u[:, e:e + 1], axis=0),
                                            zeros[:, :], None).then_inc(m_padded, 16)

            def results_stored(k):
                T = mixtures[k][2]
                pool.wait_ge(m_from, k + 1)
                for j in range(4):
                    pool.wait_ge(tiles[k]["out"][j], T // 4 * 16)

            for k in range(2):
                E = mixtures[k][0]
                pool.dma_start(rows[k][E * CAP:, :].rearrange("(e p) d -> p e d", p=P),
                               zeros[:, :].rearrange("p (e d) -> p e d", e=1).broadcast_to([P, E, D])).then_inc(
                    m_padded, 16)
            attention_steps(pool, work)
            pad(0)
            results_stored(0)
            def recurrence(u, more):
                if isinstance(u, int) and u == 0:
                    for b in range(2):
                        fetch(Group(u, b), 0, r_combined, got_in)
                for b in range(2):
                    power(Group(u, b), 1, 1)
                if more:
                    for b in range(2):
                        fetch(Group(u + 1, b), 0, r_combined, got_in)
                for b in range(2):
                    power(Group(u, b), 1, 2)
                    send(Group(u, b), 1)

            recurrence_steps(pool, recurrence)
            for b in range(2):
                pool.wait_ge(sents[1][b], NG // 2 * 2 * Q * 16)
            pad(1)
            results_stored(1)
            last_steps(pool, lambda G: fetch(G, 1, last_done, last_in))

        @block.tensor
        def _(pe):
            pe.wait_ge(c_consts, CONSTS)
            pe.wait_ge(c_wa, 8)

            def prepare_a(G):
                pe.wait_ge(a_y, G.g + 1)
                if not early(G, 1):
                    pe.wait_ge(a_wh, G.g)
                for q in range(Q):
                    ins = pe.transpose(tp[:, q * P:(q + 1) * P], y[:, q, :], ident[:, :])
                ins.then_inc(a_yTp, 1)
                pe.wait_ge(a_yT, G.g + 1)
                if not early(G, 2):
                    pe.wait_ge(p_exp1, H * (G.g - 1))
                pe.matmul(ring[0:KP, 0, :], wa_dup[:, 1, :], yT[:, :], start=True, stop=True).then_inc(a_s2p, 1)
                if not early(G, 2):
                    pe.wait_ge(p_exp2, H * (G.g - 1))
                pe.matmul(ring[0:KP, 1, :], wa_dup[:, 0, :], yT[:, :], start=True, stop=True).then_inc(a_s1p, 1)
                for q in range(Q):
                    ins = pe.matmul(tp[:, q * P:(q + 1) * P], yT[:, q * P:(q + 1) * P], gat_w_sb[:, :],
                                    start=True, stop=True)
                ins.then_inc(a_whp, 1)

            def max_image(G, h):
                if h == 0:
                    pe.wait_ge(a_s2parts, G.g + 1)
                    if not early(G, 1):
                        pe.wait_ge(a_s1parts, G.g)
                else:
                    pe.wait_ge(a_rowmax, H * G.g + h)
                pe.matmul(ring[:, 2, :], sel[:, h, :], s2_parts[:, G.b, :], start=True, stop=False)
                pe.matmul(ring[:, 2, :], identb[:, :], mask[:, G.b].rearrange("p q n -> p (q n)"),
                          start=False, stop=True).then_inc(a_maximg, 1)

            def image(G, h, k):
                bank = ring[:, k, :]
                row = sel[:, H * k + h, :]
                if h > 0:
                    pe.wait_ge((p_exp1, p_exp2)[k], H * G.g + h)
                pe.matmul(bank, row, s1_parts[:, :], start=True, stop=False)
                for q in range(Q):
                    cols = slice(q * P, (q + 1) * P)
                    pe.matmul(bank[:, cols], s2_parts[:, G.b, cols], row, start=False, stop=False)
                    ins = pe.matmul(bank[:, cols], mask[:, G.b, q, :], identb[:, :], start=False, stop=(q == Q - 1))
                ins.then_inc((p_img1, p_img2)[k], 1)

            def attend_head(G, h):
                pe.wait_ge(p_probs, H * G.g + h + 1)
                for q in range(Q):
                    c = (q % 2) * H * (HD + 1) + h * (HD + 1)
                    ins = pe.matmul(heads[:, q // 2, c:c + HD + 1], probs[:, h % 2, q * P:(q + 1) * P],
                                    values[:, G.b, q, h, :], start=True, stop=True, skip_group_check=True)
                ins.then_inc(p_heads, 1)

            def finish(G, k):
                E = mixtures[k][0]
                gs = gates[k]
                gate_w = (gate0_sb, gate1_sb)[k]
                pe.wait_ge(gs["y"], G.g + 1)
                for q in range(Q):
                    ins = pe.transpose(tp3[:, q * P:(q + 1) * P], yg[:, G.b, q, :], ident[:, :])
                ins.then_inc(gs["yTp"], 1)
                pe.wait_ge(gs["yT"], G.g + 1)
                for q in range(Q):
                    ins = pe.matmul(small[:, q * E:(q + 1) * E], ygT[:, q * P:(q + 1) * P], gate_w[:, :],
                                    start=True, stop=True)
                ins.then_inc(gs["lgp"], 1)
                pe.wait_ge(gs["chosen"], G.g + 1)
                pe.matmul(small[:, 0:Q * E], before[:, :], chosen[:, :, 0:E], start=True, stop=False)
                pe.matmul(small[:, 0:Q * E], onesb[:, :], seen[:, 0:Q, 0:E], start=False, stop=True).then_inc(
                    gs["rankp"], 1)

            def work(G, prepare, attend):
                if prepare:
                    prepare_a(G)
                L = G.prev() if attend else None
                if attend:
                    pe.wait_ge(a_s1parts, L.g + 1)
                    if prepare:
                        pe.wait_ge(a_s2, G.g + 1)
                        pe.wait_ge(a_s1, G.g + 1)
                for h in range(H):
                    if attend:
                        image(L, h, 0)
                        image(L, h, 1)
                    if prepare:
                        max_image(G, h)
                    if attend and h > 0:
                        attend_head(L, h - 1)
                if attend:
                    attend_head(L, H - 1)
                if prepare:
                    pe.wait_ge(a_dup, G.g + 1)
                    for q in range(Q):
                        ins = pe.transpose(ring[0:KP, 2, q * P:(q + 1) * P], rowmax_dup[:, q, :], ident[:, :])
                    ins.then_inc(a_maxT, 1)
                if attend:
                    finish(L, 0)

            def count(k):
                E = mixtures[k][0]
                pe.wait_ge(gates[k]["slot"], NG)
                pe.matmul(small[:, 0:E], onesb[:, :], seen[:, Q, 0:E], start=True, stop=True).then_inc(m_count, 1)

            def mixture(k):
                E, HID, T = mixtures[k]
                C = HID // P
                t_ = tiles[k]
                w_in, w_out = ((w12_sb, w3_sb), (v1_sb, v2_sb))[k]
                pe.wait_ge(m_table, k + 1)
                pe.wait_ge(*((c_weights, WEIGHTS), (c_weights1, WEIGHTS1))[k])
                xT_banks, h_banks, hT_banks, y_banks = (tp, tp3), (ring[:, 0], ring[:, 1]), (ring[:, 2], small), (
                    heads[:, 0], heads[:, 1])

                experts = {}

                def expert(a):
                    key = (id(a.i), a.off)
                    if key not in experts:
                        experts[key] = pe.value_load(tile_expert[0:1, bass.ds(a.g, 1)], min_val=0, max_val=E - 1)
                    return experts[key]

                def work(t, T):
                    a = t.back(2, T)
                    if a:
                        expert(a)
                    a = t.back(1, T)
                    if a:
                        pe.wait_ge(t_["in"][a.m % 4], 16 * a.uses(4))
                        if not early(a, 2):
                            pe.wait_ge(t_["xT"], a.g - 1)
                        pe.transpose(xT_banks[a.m % 2][:, 0:P], x_tile[:, a.m % 4, :], ident[:, :]).then_inc(
                            t_["xTp"], 1)
                    a = t.back(2, T)
                    if a:
                        e = expert(a)
                        bank = h_banks[a.m % 2]
                        pe.wait_ge(t_["xT"], a.g + 1)
                        if not early(a, 2):
                            pe.wait_ge(t_["hid"], a.g - 1)
                        ins = pe.matmul(bank, xT_tile[:, a.m % 4, :], w_in[:, bass.ds(e, 1), :], start=True,
                                        stop=(k == 0))
                        if k:
                            ins = pe.matmul(bank, onesb[0:KP, :], c1_parts[:, bass.ds(e * H1, H1)], start=False,
                                            stop=True)
                        ins.then_inc(t_["hp"], 1)
                    a = t.back(3, T)
                    if a:
                        pe.wait_ge(t_["hid"], a.g + 1)
                        if not early(a, 2):
                            pe.wait_ge(t_["hidT"], a.g - 1)
                        for c in range(C):
                            ins = pe.transpose(hT_banks[a.m % 2][:, c * P:(c + 1) * P],
                                               hid[:, a.m % 2, c * P:(c + 1) * P], ident[:, :])
                        ins.then_inc(t_["hidTp"], 1)
                    a = t.back(4, T)
                    if a:
                        e = expert(a)
                        bank = y_banks[a.m % 2][:, 0:D]
                        pe.wait_ge(t_["hidT"], a.g + 1)
                        if not early(a, 2):
                            pe.wait_ge(t_["y"], a.g - 1)
                        for c in range(C):
                            ins = pe.matmul(bank, hidT[:, a.m % 2, c * P:(c + 1) * P],
                                            w_out[:, bass.ds(e, 1), c, :], start=(c == 0),
                                            stop=(k == 0 and c == C - 1))
                        if k:
                            ins = pe.matmul(bank, onesb[0:KP, :], c2_parts[:, bass.ds(e * D, D)], start=False,
                                            stop=True)
                        ins.then_inc(t_["yp"], 1)

                tile_steps(pe, T, work)

            def recurrence(u, more):
                groups = [Group(u, b) for b in range(2)]
                for G in groups:
                    pe.wait_ge(r_xn, G.g + 1)
                    for q in range(Q):
                        ins = pe.transpose(tp[:, q * P:(q + 1) * P], yg[:, G.b, q, :], ident[:, :])
                    ins.then_inc(r_yTp, 1)
                    pe.wait_ge(r_h0, G.g + 1)
                for l in range(LAYERS):
                    for G in groups:
                        n = turn(G, l)
                        bank = heads[:, G.b, :]
                        state = hT[:, G.b, :]
                        if l:
                            pe.wait_ge(r_h[G.b], G.u * LAYERS + l)
                        for q in range(Q):
                            ins = pe.matmul(bank[:, q * P:(q + 1) * P], state[:, q * P:(q + 1) * P], gru_w_sb[:, l, :],
                                            start=True, stop=True)
                        ins.then_inc(r_mp, 1)
                        if not (isinstance(n, int) and n == 1):
                            pe.wait_ge(r_t, n - 1)
                        pe.matmul(ring[:, 0, :], gru_wT[:, 1, 0, :], state, start=True, stop=False)
                        pe.matmul(ring[:, 1, :], gru_wT[:, 1, 1, :], state, start=True, stop=False)
                        pe.matmul(small[:, :], gru_wT[:, 1, 2, :], state, start=True, stop=True)
                        pe.wait_ge(r_m, turn(G, l))
                        for q in range(Q):
                            ins = pe.matmul(bank[:, q * P:(q + 1) * P], msg[:, G.b, q * P:(q + 1) * P],
                                            adj32[:, G.b, q * P:(q + 1) * P], start=True, stop=True)
                        ins.then_inc(r_aggp, 1)
                        pe.wait_ge(r_agg, turn(G, l))
                        pe.matmul(ring[:, 0, :], gru_wT[:, 0, 0, :], agg[:, G.b, :], start=False, stop=True)
                        pe.matmul(ring[:, 1, :], gru_wT[:, 0, 1, :], agg[:, G.b, :], start=False, stop=True)
                        pe.matmul(ring[:, 2, :], gru_wT[:, 0, 2, :], agg[:, G.b, :], start=True, stop=True).then_inc(
                            r_rz, 1)
                for G in groups:
                    pe.wait_ge(r_h[G.b], (G.u + 1) * LAYERS)
                    for q in range(Q):
                        ins = pe.transpose(tp[:, q * P:(q + 1) * P], hT[:, G.b, q * P:(q + 1) * P], ident[:, :])
                    ins.then_inc(r_backp, 1)
                    finish(G, 1)

            pe.wait_ge(c_gru, GRU)
            for k in range(2):
                for c in range(3):
                    ins = pe.transpose((tp, tp3)[k][:, c * P:(c + 1) * P], gru_in[:, k, c, :], ident[:, :])
            ins.then_inc(c_gruT, 1)
            pe.wait_ge(c_gruT, 3)
            attention_steps(pe, work)
            count(0)
            mixture(0)
            recurrence_steps(pe, recurrence)
            count(1)
            mixture(1)

        @block.scalar
        def _(act):
            act.wait_ge(c_consts, CONSTS)
            act.wait_ge(c_small, SMALL)

            def work(G, prepare, attend):
                if prepare:
                    act.wait_ge(a_yTp, G.g + 1)
                    act.copy(yT[:, :], tp[:, :]).then_inc(a_yT, 1)
                    act.wait_ge(a_s1p, G.g + 1)
                    act.activation(s1[:, :], ring[0:KP, 1, :], ACT.Identity, bias=emb[:, 0:1]).then_inc(a_s1, 1)
                    act.wait_ge(a_whp, G.g + 1)
                    act.copy(values[:, G.b, :, :, 0:HD].rearrange("p q h d -> p (q h) d"),
                             tp[:, :].rearrange("p (a d) -> p a d", d=HD)).then_inc(a_wh, 1)
                if not attend:
                    return
                L = G.prev()
                for h in range(H):
                    if not (early(L, 1) and h < 2):
                        act.wait_ge(p_probs, H * L.g + h - 1)
                    act.wait_ge(p_img1, H * L.g + h + 1)
                    act.activation(exp1[:, h % 2, :], ring[:, 0, :], ACT.Exp).then_inc(p_exp1, 1)
                    act.wait_ge(p_img2, H * L.g + h + 1)
                    act.activation(exp2[:, h % 2, :], ring[:, 1, :], ACT.Exp).then_inc(p_exp2, 1)
                act.wait_ge(f_neg, L.g + 1)
                act.activation(hexp[:, :, :], hneg[:, :, :], ACT.Exp).then_inc(f_exp, 1)
                gate(L, 0)

            def gate(G, k):
                gs = gates[k]
                act.wait_ge(gs["yTp"], G.g + 1)
                act.copy(ygT[:, :], tp3[:, :]).then_inc(gs["yT"], 1)
                act.wait_ge(gs["gap"], G.g + 1)
                act.activation(egap[:, :], gap[:, :], (ACT.Exp, ACT.Sigmoid)[k]).then_inc(gs["egap"], 1)

            def mixture(k):
                t_ = tiles[k]
                HID, T = mixtures[k][1:]

                def work(t, T):
                    a = t.back(2, T)
                    if a:
                        act.wait_ge(t_["hp"], a.g + 1)
                        bank = ring[:, a.m % 2, :]
                        if k == 0:
                            if not early(a, 2):
                                act.wait_ge(t_["hid"], a.g - 1)
                            act.activation(silu[:, a.m % 2, 0:H0], bank[:, 0:H0], ACT.Silu).then_inc(t_["act"], 1)
                        else:
                            if not early(a, 2):
                                act.wait_ge(t_["hidTp"], a.g - 1)
                            act.activation(hid[:, a.m % 2, :], bank, ACT.Gelu).then_inc(t_["hid"], 1)
                    a = t.back(3, T)
                    if a and k == 0:
                        act.wait_ge(t_["hidTp"], a.g + 1)
                        if not early(a, 2):
                            act.wait_ge(t_["yp"], a.g - 1)
                        act.copy(hidT[:, a.m % 2, 0:HID], (ring[:, 2, :], small)[a.m % 2][:, 0:HID]).then_inc(
                            t_["hidT"], 1)

                tile_steps(act, T, work)

            def recurrence(u, more):
                groups = [Group(u, b) for b in range(2)]
                for G in groups:
                    act.wait_ge(r_yTp, G.g + 1)
                    act.copy(hT[:, G.b, :], tp[:, :]).then_inc(r_h0, 1)
                for l in range(LAYERS):
                    for G in groups:
                        n = turn(G, l)
                        act.wait_ge(r_mp, n)
                        act.copy(msg[:, G.b, :], heads[:, G.b, :]).then_inc(r_m, 1)
                        act.wait_ge(r_aggp, n)
                        act.copy(agg[:, G.b, :], heads[:, G.b, :]).then_inc(r_agg, 1)
                        act.wait_ge(r_rz, n)
                        act.activation(gate_r[:, G.b, :], ring[:, 0, :], ACT.Sigmoid, bias=bias_rz[:, 0:1]).then_inc(
                            r_sig, 1)
                        act.activation(gate_z[:, G.b, :], ring[:, 1, :], ACT.Sigmoid, bias=bias_rz[:, 1:2]).then_inc(
                            r_sig, 1)
                        act.wait_ge(r_t, n)
                        act.activation(cand[:, G.b, :], cand[:, G.b, :], ACT.Tanh, bias=gru_b[:, 0, 2:3]).then_inc(
                            r_n, 1)
                for G in groups:
                    gate(G, 1)

            act.dma_start(gru_w_sb[:, :, :], gru_w.rearrange("l d e -> d l e")).then_inc(c_gru, 16)
            for k, w in enumerate((w_ih, w_hh)):
                act.dma_start(gru_in[:, k], w.rearrange("(c e) d -> e c d", c=3)).then_inc(c_gru, 16)
            for k, w in enumerate((b_ih, b_hh)):
                act.dma_start(gru_b[:, k, :], w.rearrange("(c e) -> e c", c=3),
                              allow_slow_non_contiguous=True).then_inc(c_gru, 16)
            act.dma_start(w12_sb[:, :, 0:H0], w1.rearrange("e d h -> d e h")).then_inc(c_weights, 16)
            act.dma_start(w12_sb[:, :, H0:2 * H0], w2.rearrange("e d h -> d e h")).then_inc(c_weights, 16)
            for c in range(H0 // P):
                act.dma_start(w3_sb[:, :, c, :], w3[:, c * P:(c + 1) * P, :].rearrange("e k o -> k e o")).then_inc(
                    c_weights, 16)
            act.wait_ge(c_gruT, 1)
            for k in range(2):
                act.copy(gru_wT[:, k].rearrange("p c e -> p (c e)"), (tp, tp3)[k][:, 0:3 * P]).then_inc(c_gruT, 1)
            attention_steps(act, work)
            mixture(0)
            act.wait_ge(tiles[0]["yp"], T0)
            act.dma_start(v1_sb, v1.rearrange("e d h -> d e h")).then_inc(c_weights1, 16)
            for c in range(H1 // P):
                act.dma_start(v2_sb[:, :, c, :], v2[:, c * P:(c + 1) * P, :].rearrange("e k o -> k e o")).then_inc(
                    c_weights1, 16)
            recurrence_steps(act, recurrence)
            mixture(1)

        @block.vector
        def _(dve):
            dve.memset(wide[0:KP, 8:20, :], 0.0).then_inc(c_zero, 1)
            dve.wait_ge(c_consts, CONSTS)
            dve.wait_ge(c_small, SMALL)
            for k in range(2):
                dve.tensor_tensor(prod[:, :].rearrange("p (h d) -> p h d", d=HD),
                                  gat_w_sb[:, :].rearrange("p (h d) -> p h d", d=HD),
                                  a_rows[:, k:k + 1, :].broadcast_to([P, H, HD]), ALU.mult).then_inc(c_wa, 1)
                dve.wait_ge(c_wa, 2 * k + 1)
                dve.tensor_reduce(wa[:, k, :], prod[:, :].rearrange("p (h d) -> p h d", d=HD), AX.X,
                                  ALU.add).then_inc(c_wa, 1)
                dve.wait_ge(c_wa, 2 * k + 2)
            for k in range(2):
                for c in range(2):
                    view = wa_dup[:, k, H * c:H * c + H]
                    dst = bass.AP(view.tensor, view.offset, [view.ap[0], [32, PARTS], [1, H]])
                    dve.tensor_copy(dst, wa[:, k:k + 1, :].broadcast_to([P, PARTS, H])).then_inc(c_wa, 1)

            def features(G):
                if isinstance(G.g, int):
                    return lambda q: xs[:, G.g * Q + q, :]
                return lambda q: xs[:, bass.ds(G.g * Q + q, 1), :].rearrange("p a f -> p (a f)")

            def moments_of(ch, src, stats_, moments_):
                for q in range(Q):
                    ins = dve.bn_stats(stats_[:, q, :], src(q))
                ch.step(ins, apart)
                for q in range(Q):
                    ins = dve.bn_aggr(moments_[:, q, :], stats_[:, q, :])
                ch.step(ins)

            def split(ch, src, dst):
                ch.step(dve.tensor_copy(part_a[:, :], src))
                ch.step(dve.scalar_tensor_tensor(part_b[:, :], part_a[:, :], not_hi[:, 0:1], src, ALU.mult, ALU.add))
                ch.step(dve.tensor_copy(part_c[:, :], part_b[:, :]))
                return dve.scalar_tensor_tensor(dst, part_c[:, :], is_lo[:, 0:1], part_b[:, :], ALU.mult, ALU.add)

            def prepare_a(G):
                ch = Chain(dve, a_chain, 2, G.g)
                dve.wait_ge(x_in[G.b], 32 * G.u + 32)
                apart(dve)
                src = features(G)
                moments_of(ch, src, stats, moments)
                ch.end()
                dve.tensor_scalar(var_eps[:, :], moments[:, :, 1], EPS, None, ALU.add).then_inc(a_var, 1)
                dve.tensor_scalar(mask[:, G.b], adj_in[:, G.b], 0.0, MASKED, ALU.is_equal, ALU.mult)
                dve.tensor_scalar(graphs(edges, G.g), adj_in[:, G.b], 0.0, None, ALU.not_equal).then_inc(adj_read, 1)
                dve.wait_ge(a_rstd, G.g + 1)
                for q in range(Q):
                    ins = dve.tensor_scalar(y[:, q, :], src(q), moments[:, q, 0:1], rstd[:, q:q + 1], ALU.subtract,
                                            ALU.mult)
                ins.then_inc(a_y, 1)
                sc = Chain(dve, s_chain, 3, G.g)
                dve.wait_ge(a_s2p, G.g + 1)
                dve.tensor_scalar(s2[:, :], ring[0:KP, 0, :], slope[:, 0:1], None, ALU.mult).then_inc(a_s2, 1)
                dve.wait_ge(a_s2, G.g + 1)
                split(sc, s2[:, :], s2_parts[:, G.b, :]).then_inc(a_s2parts, 1)
                sc.end()

            def prepare_c(G):
                for c in range(PARTS):
                    view = rowmax_dup[:, :, 32 * c:32 * c + 2 * H].rearrange("p q (k h) -> p q k h", k=2)
                    ins = dve.tensor_copy(view, rowmax[:, :, :].rearrange("p q (k h) -> p q k h", k=1).broadcast_to(
                        [P, Q, 2, H]))
                ins.then_inc(a_dup, 1)
                ch = Chain(dve, v_chain, 6, G.g)
                dve.wait_ge(a_maxT, G.g + 1)
                dve.wait_ge(a_s1, G.g + 1)
                ch.step(dve.tensor_tensor(top[:, :], s1[:, :], ring[0:KP, 2, :], ALU.add))
                ch.step(dve.scalar_tensor_tensor(top[:, :], top[:, :], 0.2, top[:, :], ALU.mult, ALU.max))
                ch.step(dve.scalar_tensor_tensor(top[:, :], s1[:, :], slope[:, 0:1], top[:, :], ALU.mult,
                                                 ALU.subtract))
                split(ch, top[:, :], s1_parts[:, :]).then_inc(a_s1parts, 1)
                ch.end()

            def finish(G):
                ch = Chain(dve, f_chain, FIN, G.g)
                dve.wait_ge(p_heads, H * (G.g + 1))
                view = heads[:, :, 0:2 * H * (HD + 1)].rearrange("p a (h d) -> p a h d", d=HD + 1)
                ch.step(dve.reciprocal(rden[:, :, :], view[:, :, :, HD]))
                ch.step(dve.tensor_tensor(hn[:, :, :].rearrange("p (a b) (h d) -> p a (b h) d", a=2, d=HD),
                                          view[:, :, :, 0:HD],
                                          rden[:, :, :].rearrange("p a (h d) -> p a h d", d=1).broadcast_to(
                                              [P, 2, 2 * H, HD]), ALU.mult), apart)
                moments_of(ch, lambda q: hn[:, q, :], stats3, moments3)
                dve.tensor_scalar(var_eps3[:, :], moments3[:, :, 1], EPS, None, ALU.add).then_inc(f_var, 1)
                dve.wait_ge(f_rstd, norm(G, 0, 1))
                for q in range(Q):
                    ins = dve.tensor_scalar(hn[:, q, :], hn[:, q, :], moments3[:, q, 0:1], rstd3[:, q:q + 1],
                                            ALU.subtract, ALU.mult)
                ch.step(ins)
                ch.step(dve.tensor_tensor(hn[:, :, :], hn[:, :, :], gamma[:, :].rearrange("p (a f) -> p a f", a=1)
                                          .broadcast_to([P, Q, D]), ALU.mult))
                ch.step(dve.tensor_tensor(hn[:, :, :], hn[:, :, :], beta[:, :].rearrange("p (a f) -> p a f", a=1)
                                          .broadcast_to([P, Q, D]), ALU.add))
                dve.tensor_scalar(hneg[:, :, :], hn[:, :, :], 0.0, None, ALU.min).then_inc(f_neg, 1)
                dve.wait_ge(f_exp, G.g + 1)
                ch.step(dve.scalar_tensor_tensor(hn[:, :, :], hn[:, :, :], 0.0, hexp[:, :, :], ALU.max, ALU.add))
                ch.step(dve.scalar_tensor_tensor(graphs(xs, G.g), hn[:, :, :], -1.0, graphs(xs, G.g), ALU.add,
                                                 ALU.add), apart)
                ch.end()
                normalise_and_gate(G, 0)

            def normalise_and_gate(G, layer):
                gs, E, bias, sent = gates[layer], mixtures[layer][0], (gate0_bias, gate1_bias)[layer], sents[layer]
                ch = Chain(dve, gs["chain"], FIN2, G.g)
                src = features(G)
                moments_of(ch, src, stats3, moments3)
                dve.tensor_scalar(var_eps3[:, :], moments3[:, :, 1], EPS, None, ALU.add).then_inc(gs["var"], 1)
                if not early(G, 2):
                    dve.wait_ge(sent[G.b], G.u * (2 * Q * 16))
                dve.wait_ge(gs["rstd"], norm(G, layer, 2))
                for q in range(Q):
                    ins = dve.tensor_scalar(yg[:, G.b, q, :], src(q), moments3[:, q, 0:1], rstd3[:, q:q + 1],
                                            ALU.subtract, ALU.mult)
                ins.then_inc(gs["y"], 1)

                def wide(t):
                    return t.rearrange("p (q a) -> p q a", a=1).broadcast_to([P, Q, E])

                L, S, F1, F2 = lg[:, :, 0:E], score[:, :, 0:E], first[:, :, 0:E], second[:, :, 0:E]
                revs = rev[:, 0:E].rearrange("p (a e) -> p a e", a=1).broadcast_to([P, Q, E])
                dve.wait_ge(gs["lgp"], G.g + 1)
                ch.step(dve.tensor_tensor(L, small[:, 0:Q * E].rearrange("p (q e) -> p q e", e=E),
                                          bias[:, 0:E].rearrange("p (a e) -> p a e", a=1).broadcast_to([P, Q, E]),
                                          ALU.add))
                for k, (src_, one) in enumerate(((L, F1), (lg2[:, :, 0:E], F2))):
                    ch.step(dve.tensor_reduce(peak[:, :, k], src_, AX.X, ALU.max))
                    ch.step(dve.tensor_tensor(S, src_, peak[:, :, k:k + 1].broadcast_to([P, Q, E]), ALU.is_equal))
                    ch.step(dve.tensor_tensor(S, S, revs, ALU.mult))
                    ch.step(dve.tensor_reduce(rmax[:, :], S, AX.X, ALU.max))
                    ch.step(dve.tensor_tensor(one, S, wide(rmax[:, :]), ALU.is_equal))
                    if k == 0:
                        ch.step(dve.scalar_tensor_tensor(lg2[:, :, 0:E], one, -3e38, L, ALU.mult, ALU.add))
                dve.tensor_tensor(gap[:, :], peak[:, :, 1], peak[:, :, 0], ALU.subtract).then_inc(gs["gap"], 1)
                ch.step(dve.tensor_tensor(chosen[:, :, 0:E], F1, F2, ALU.add))
                if not early(G, 1):
                    ch.step(dve.tensor_copy(seen[:, 0, 0:E], seen[:, Q, 0:E]))
                else:
                    ch.step(dve.memset(seen[:, 0, 0:E], 0.0))
                for q in range(Q):
                    ins = dve.tensor_tensor(seen[:, q + 1, 0:E], seen[:, q, 0:E], chosen[:, q, 0:E], ALU.add)
                    if q < Q - 1:
                        ch.step(ins)
                ins.then_inc(gs["chosen"], 1)
                dve.wait_ge(gs["egap"], G.g + 1)
                if layer == 0:
                    ch.step(dve.tensor_scalar(rmax[:, :], egap[:, :], 1.0, None, ALU.add))
                    ch.step(dve.reciprocal(wgt[:, :, 0], rmax[:, :]))
                    ch.step(dve.tensor_tensor(wgt[:, :, 1], wgt[:, :, 0], egap[:, :], ALU.mult))
                else:
                    ch.step(dve.tensor_copy(wgt[:, :, 1], egap[:, :]))
                    ch.step(dve.tensor_scalar(wgt[:, :, 0], egap[:, :], -1.0, 1.0, ALU.mult, ALU.add))
                    ch.step(dve.tensor_copy(rmax[:, :], wgt[:, :, 0]))
                dve.tensor_scalar(graphs(gate_all, G.g), wgt[:, :, :], 1.0, None, ALU.mult)
                dve.wait_ge(gs["rankp"], G.g + 1)
                ch.step(dve.tensor_tensor(rank[:, :, 0:E], small[:, 0:Q * E].rearrange("p (q e) -> p q e", e=E),
                                          base[:, 0:E].rearrange("p (a e) -> p a e", a=1).broadcast_to([P, Q, E]),
                                          ALU.add))
                for k, one in enumerate((F1, F2)):
                    ch.step(dve.tensor_tensor(S, one, rank[:, :, 0:E], ALU.mult))
                    ch.step(dve.tensor_reduce(slot_f[:, :, k], S, AX.X, ALU.add))
                ch.step(dve.tensor_scalar(graphs(slot_all, G.g), slot_f[:, :, :], 1.0, None, ALU.mult))
                dve.tensor_copy(slot_u[:, G.b], slot_f[:, :, :]).then_inc(gs["slot"], 1)
                ch.end()

            def work(G, prepare, attend):
                if prepare:
                    prepare_a(G)
                L = G.prev() if attend else None
                for h in range(H):
                    if prepare:
                        dve.wait_ge(a_maximg, H * G.g + h + 1)
                        dve.tensor_reduce(rowmax[:, :, h], ring[:, 2, :].rearrange("p (q n) -> p q n", q=Q), AX.X,
                                          ALU.max).then_inc(a_rowmax, 1)
                    if attend:
                        if not (early(L, 1) and h < 2):
                            dve.wait_ge(p_heads, H * L.g + h - 1)
                        dve.wait_ge(p_exp2, H * L.g + h + 1)
                        dve.tensor_tensor(probs[:, h % 2, :], exp1[:, h % 2, :], exp2[:, h % 2, :],
                                          ALU.max).then_inc(p_probs, 1)
                if prepare:
                    dve.wait_ge(a_rowmax, H * G.g + H)
                    prepare_c(G)
                if attend:
                    finish(L)

            def plan(k):
                E, HID, T = mixtures[k]
                ch = Chain(dve, m_chain, PLAN, 0)
                ch.k = PLAN if k else 0
                dve.wait_ge(m_count, k + 1)
                if k:
                    dve.wait_ge(m_padded, 16 * (E0 + 2))
                ch.step(dve.tensor_copy(counts[:, 0:E], small[:, 0:E]))
                ch.step(dve.tensor_tensor(pad_f[:, 0:E], counts[:, 0:E], base[:, 0:E], ALU.add))
                dve.tensor_scalar(pad_u[:, 0:E], pad_f[:, 0:E], lane[:, 0:1], None, ALU.add).then_inc(m_pad, 1)
                ch.step(dve.tensor_scalar(tiles_i[:, 0, 0:E], counts[:, 0:E], float(P - 1), None, ALU.add))
                ch.step(dve.tensor_scalar(tiles_i[:, 1, 0:E], tiles_i[:, 0, 0:E], P.bit_length() - 1, None,
                                          ALU.logical_shift_right))
                ch.step(dve.tensor_copy(tiles_f[:, 0:E], tiles_i[:, 1, 0:E]))
                ch.step(dve.tensor_copy(ends[:, 0, 0:E], tiles_f[:, 0:E]))
                dve.memset(closer[:, 0:1], 0.0)
                dve.tensor_scalar(closer[:, 1:E], tiles_f[:, 0:E - 1], float(P), -float(CAP), ALU.mult, ALU.add)
                src, step = 0, 1
                while step < E:
                    dve.tensor_copy(ends[:, 1 - src, 0:step], ends[:, src, 0:step])
                    ch.step(dve.tensor_tensor(ends[:, 1 - src, step:E], ends[:, src, step:E],
                                              ends[:, src, 0:E - step], ALU.add))
                    src, step = 1 - src, 2 * step
                flat = wide[0:1, :, :].rearrange("p k n -> p (k n)")
                past = flat[:, 0:T * E].rearrange("p (t e) -> p t e", e=E)
                held = flat[:, T0 * E0:T0 * E0 + T * E].rearrange("p (t e) -> p t e", e=E)

                def per_tile(t):
                    return t.rearrange("p (a e) -> p a e", a=1).broadcast_to([1, T, E])

                ch.step(dve.tensor_tensor(past, tile_no[:, 0:T].rearrange("p (t a) -> p t a", a=1).broadcast_to(
                    [1, T, E]), per_tile(ends[0:1, src, 0:E]), ALU.is_ge))
                ch.step(dve.tensor_tensor(held, past, per_tile(tiles_f[0:1, 0:E]), ALU.mult))
                ch.step(dve.tensor_reduce(expert_f[:, 0:T], past, AX.X, ALU.add))
                ch.step(dve.tensor_reduce(start_f[:, 0:T], held, AX.X, ALU.add))
                ch.step(dve.tensor_tensor(start_f[:, 0:T], tile_no[:, 0:T], start_f[:, 0:T], ALU.subtract))
                ch.step(dve.tensor_scalar(start_f[:, 0:T], start_f[:, 0:T], float(P), None, ALU.mult))
                ch.step(dve.tensor_scalar(tile_expert[:, 0:T], expert_f[:, 0:T], float(E - 1), None, ALU.min))
                ch.step(dve.tensor_scalar(expert_f[:, 0:T], expert_f[:, 0:T], float(CAP), None, ALU.mult))
                dve.tensor_tensor(tile_row[:, 0:T], expert_f[:, 0:T], start_f[:, 0:T], ALU.add).then_inc(m_table, 1)

            def mixture(k):
                t_ = tiles[k]
                HID, T = mixtures[k][1:]

                def work(t, T):
                    a = t.back(1, T)
                    if a:
                        dve.wait_ge(t_["xTp"], a.g + 1)
                        if not early(a, 4):
                            dve.wait_ge(t_["hp"], a.g - 3)
                        dve.tensor_copy(xT_tile[:, a.m % 4, :], (tp, tp3)[a.m % 2][:, 0:P]).then_inc(t_["xT"], 1)
                    a = t.back(2, T)
                    if a and k == 0:
                        dve.wait_ge(t_["act"], a.g + 1)
                        if not early(a, 2):
                            dve.wait_ge(t_["hidTp"], a.g - 1)
                        dve.tensor_tensor(hid[:, a.m % 2, 0:H0], silu[:, a.m % 2, 0:H0],
                                          ring[:, a.m % 2, H0:2 * H0], ALU.mult).then_inc(t_["hid"], 1)
                    a = t.back(3, T)
                    if a and k == 1:
                        dve.wait_ge(t_["hidTp"], a.g + 1)
                        if not early(a, 2):
                            dve.wait_ge(t_["yp"], a.g - 1)
                        dve.tensor_copy(hidT[:, a.m % 2, :], (ring[:, 2, :], small)[a.m % 2][:, 0:HID]).then_inc(
                            t_["hidT"], 1)
                    a = t.back(4, T)
                    if a:
                        dve.wait_ge(t_["yp"], a.g + 1)
                        if not early(a, 4):
                            dve.wait_ge(t_["out"][a.m % 4], 16 * (a.uses(4) - 1))
                        dve.tensor_copy(y_tile[:, a.m % 4, :], heads[:, a.m % 2, 0:D]).then_inc(t_["y"], 1)

                tile_steps(dve, T, work)

            def index(k):
                E = mixtures[k][0]
                ch = Chain(dve, i_chain, 3, k)
                slots = slot_all[:, :, :].rearrange("p g k -> p (g k)")
                cmp = wide[:, 12:12 + 2 * B * E // QN, :].rearrange("p k n -> p (k n)").rearrange("p (g e) -> p g e", e=E)

                def every(t):
                    return t[:, 0:E].rearrange("p (a e) -> p a e", a=1).broadcast_to([P, 2 * B, E])

                ch.step(dve.tensor_tensor(cmp, slots.rearrange("p (g a) -> p g a", a=1).broadcast_to([P, 2 * B, E]),
                                          every(base), ALU.is_ge))
                ch.step(dve.tensor_tensor(cmp, cmp, every(closer), ALU.mult))
                ch.step(dve.tensor_reduce(moved[:, :], cmp, AX.X, ALU.add))
                ch.end()
                dve.tensor_tensor(from_u[:, :], slots, moved[:, :], ALU.add).then_inc(m_from, 1)

            def weight(G, q, k):
                return gate_all[:, bass.ds(G.g * Q + q, 1), k:k + 1].rearrange("p a c -> p (a c)")

            def combine(G, ch, sems):
                dve.wait_ge(sems[G.b], G.u * (2 * Q * 16) + 2 * Q * 16)
                x_of = features(G)
                for k in range(2):
                    for q in range(Q):
                        ins = dve.scalar_tensor_tensor(x_of(q), got[:, G.b, q, k, :], weight(G, q, k), x_of(q), ALU.mult,
                                                       ALU.add)
                    if k == 0:
                        ch.step(ins)
                return ins

            def recurrence(u, more):
                groups = [Group(u, b) for b in range(2)]
                for G in groups:
                    ch = Chain(dve, r_chain, 3, G.g)
                    combine(G, ch, got_in).then_inc(r_combined, 1)
                    dve.wait_ge(r_combined, G.g + 1)
                    apart(dve)
                    moments_of(ch, features(G), stats3, moments3)
                    ch.end()
                    dve.tensor_scalar(var_eps3[:, :], moments3[:, :, 1], EPS, None, ALU.add).then_inc(
                        gates[1]["var"], 1)
                    dve.tensor_scalar(by_graph(adj32[:, G.b, :]), graphs(edges, G.g), 1.0, None, ALU.mult)
                    dve.wait_ge(gates[1]["rstd"], norm(G, 1, 1))
                    if not early(G, 2):
                        dve.wait_ge(sents[1][G.b], G.u * (2 * Q * 16))
                    for q in range(Q):
                        ins = dve.tensor_scalar(yg[:, G.b, q, :], features(G)(q), moments3[:, q, 0:1], rstd3[:, q:q + 1],
                                                ALU.subtract, ALU.mult)
                    ins.then_inc(r_xn, 1)
                for l in range(LAYERS):
                    for G in groups:
                        n = turn(G, l)
                        state, c, z = hT[:, G.b, :], cand[:, G.b, :], gate_z[:, G.b, :]
                        ch = Chain(dve, r_chain2, 3, n - 1)
                        dve.wait_ge(r_sig, 2 * n)
                        ch.step(dve.scalar_tensor_tensor(c, small[:, :], gru_b[:, 1, 2:3], gate_r[:, G.b, :], ALU.add,
                                                         ALU.mult))
                        dve.tensor_tensor(c, c, ring[:, 2, :], ALU.add).then_inc(r_t, 1)
                        dve.wait_ge(r_n, n)
                        ch.step(dve.tensor_tensor(state, state, c, ALU.subtract))
                        ch.step(dve.tensor_tensor(state, state, z, ALU.mult))
                        ch.end()
                        dve.tensor_tensor(state, state, c, ALU.add).then_inc(r_h[G.b], 1)
                for G in groups:
                    dve.wait_ge(r_backp, G.g + 1)
                    dve.tensor_tensor(graphs(xs, G.g), graphs(xs, G.g), by_graph(tp[:, :]), ALU.add).then_inc(r_back, 1)
                    dve.wait_ge(r_back, G.g + 1)
                    apart(dve)
                    normalise_and_gate(G, 1)

            dve.wait_ge(c_bias, 16 * 2 * PARTS)
            bc = Chain(dve, b_chain, 4 * BIAS_STEPS, 0)
            for j in range(E1 * H1 // QN):
                bc.step(split(bc, wide[0:KP, 12 + j, :], c1_parts[:, j * QN:(j + 1) * QN]))
            for j in range(E1 * D // QN):
                bc.step(split(bc, wide[0:KP, 8 + j, :], c2_parts[:, j * QN:(j + 1) * QN]))
            bc.end()
            dve.wait_ge(c_gru, GRU)
            dve.tensor_tensor(bias_rz[:, :], gru_b[:, 0, 0:2], gru_b[:, 1, 0:2], ALU.add)
            attention_steps(dve, work)
            plan(0)
            index(0)
            mixture(0)
            recurrence_steps(dve, recurrence)
            plan(1)
            index(1)
            mixture(1)

            def last(G):
                ch = Chain(dve, last_chain, 1, G.g)
                combine(G, ch, last_in).then_inc(last_done, 1)
            last_steps(dve, last)


PLAN = 18
BIAS_STEPS = E1 * (H1 + D) // QN

WEIGHTS = 16 * (2 + H0 // P)
WEIGHTS1 = 16 * (1 + H1 // P)
GRU = 16 * 5
CONSTS = 32
FIN = 9
FIN2 = 28
SMALL = 16 * (9 + 2 * PARTS)

_INS = ['x', 'adj', 'L0_gnn_W', 'L0_gnn_a1', 'L0_gnn_a2', 'L0_gnn_edge_emb', 'L0_gnn_ln_gamma', 'L0_gnn_ln_beta',
        'L0_ffn_gate_w', 'L0_ffn_gate_b', 'L0_ffn_w1', 'L0_ffn_w2', 'L0_ffn_w3', 'L1_gnn_weight', 'L1_gnn_w_ih',
        'L1_gnn_w_hh', 'L1_gnn_b_ih', 'L1_gnn_b_hh', 'L1_ffn_Wg', 'L1_ffn_bg', 'L1_ffn_W1', 'L1_ffn_b1', 'L1_ffn_W2',
        'L1_ffn_b2']
_OUTS = [((64, 128, 128), 'float32')]


def kernel(**inputs):
    import numpy as _np
    import concourse.bacc as _bacc
    from concourse import mybir as _mybir
    from concourse.bass_utils import run_bass_kernel_spmd as _run

    nc = _bacc.Bacc("TRN2", target_bir_lowering=False, num_devices=1)
    arrays, args = {}, []
    for name in _INS:
        a = _np.ascontiguousarray(inputs[name])
        arrays[f"in_{name}_dram"] = a
        args.append(nc.dram_tensor(f"in_{name}_dram", a.shape, _mybir.dt.from_np(a.dtype), kind="ExternalInput").ap())
    for i, (shape, dtype) in enumerate(_OUTS):
        dt = _mybir.dt.from_np(_np.dtype(dtype))
        args.append(nc.dram_tensor(f"out_{i}_dram", shape, dt, kind="ExternalOutput").ap())
    two_layers(nc, *args)
    r = _run(nc, [arrays], core_ids=[0])
    return r.results[0]["out_0_dram"]
```

```python
import concourse.bass as bass
from concourse import mybir
from contextlib import ExitStack

F32 = mybir.dt.float32
BF16 = mybir.dt.bfloat16
I32 = mybir.dt.int32
U32 = mybir.dt.uint32
ALU = mybir.AluOpType
ACT = mybir.ActivationFunctionType
AX = mybir.AxisListType

P = 128
B = 64
N = 128
D = 128
Q = 4
NG = B // Q
QN = Q * N
H = 8
HD = D // H
PARTS = 3
KP = 32 * (PARTS - 1) + 2 * H
EPS = 1e-5
MASKED = -1e9
LAYERS = 3

E0, H0 = 16, 256
E1, H1 = 8, 512
PAIRS = 2 * B * N
CAP = B * N + P
T0 = PAIRS // P + E0
T1 = PAIRS // P + E1


class Group:

    def __init__(self, u, b):
        self.u, self.b, self.g = u, b, u * 2 + b

    def prev(self):
        return Group(self.u, 0) if self.b else Group(self.u - 1, 1)


class Tile:

    def __init__(self, i, off):
        self.i, self.off, self.g, self.m = i, off, i * 8 + off, off % 8

    def back(self, n, T):
        if isinstance(self.g, int) and not 0 <= self.g - n < T:
            return None
        return Tile(self.i, self.off - n)

    def uses(self, n):
        return self.i * (8 // n) + self.off // n + 1


def early(G, n):
    return isinstance(G.g, int) and G.g < n


class Chain:

    def __init__(self, eng, sem, n, g):
        self.eng, self.sem, self.n, self.g, self.k = eng, sem, n, g, 0

    def step(self, ins, apart=None):
        self.k += 1
        ins.then_inc(self.sem, 1)
        self.eng.wait_ge(self.sem, self.g * self.n + self.k)
        if apart:
            apart(self.eng)

    def end(self):
        assert self.k == self.n, (self.sem, self.k, self.n)


def two_layers(nc, x, adj, gat_w, gat_a1, gat_a2, gat_emb, gat_gamma, gat_beta, gate0_w, gate0_b, w1, w2, w3,
               gru_w, w_ih, w_hh, b_ih, b_hh, gate1_w, gate1_b, v1, c1, v2, c2, out):
    with ExitStack() as ctx:
        def sb(name, shape, dt=F32):
            return ctx.enter_context(nc.sbuf_tensor(name, shape, dt))

        def ps(name, shape, dt=F32):
            return ctx.enter_context(nc.psum_tensor(name, shape, dt))

        def sem(name):
            return ctx.enter_context(nc.semaphore(name))

        ident = sb("ident", [P, P])
        identb = sb("identb", [P, P], BF16)
        before = sb("before", [P, P], BF16)
        onesb = sb("onesb", [P, P], BF16)
        sel = sb("sel", [KP, 2 * H, P], BF16)
        rev = sb("rev", [P, E0])
        base = sb("base", [P, E0])
        not_hi = sb("not_hi", [KP, 1])
        is_lo = sb("is_lo", [KP, 1])
        slope = sb("slope", [KP, 1])
        minus_half = sb("minus_half", [P, Q])
        lane = sb("lane", [P, 1])
        zeros = sb("zeros", [P, D])
        tile_no = sb("tile_no", [1, T0])

        gat_w_sb = sb("gat_w_sb", [P, D])
        a_rows = sb("a_rows", [P, 2, HD])
        wa = sb("wa", [P, 2, H])
        prod = sb("prod", [P, D])
        wa_dup = sb("wa_dup", [P, 2, KP])
        emb = sb("emb", [KP, 1])
        gamma = sb("gamma", [P, D])
        beta = sb("beta", [P, D])
        gate0_sb = sb("gate0_sb", [P, E0])
        gate0_bias = sb("gate0_bias", [P, E0])
        gate1_sb = sb("gate1_sb", [P, E1])
        gate1_bias = sb("gate1_bias", [P, E1])

        xs = sb("xs", [P, B, D])
        edges = sb("edges", [P, B, N], BF16)
        slot_all = sb("slot_all", [P, B, 2])
        gate_all = sb("gate_all", [P, B, 2])

        adj_in = sb("adj_in", [P, 2, Q, N], I32)
        mask = sb("mask", [P, 2, Q, N], BF16)
        stats = sb("stats", [P, Q, 6])
        moments = sb("moments", [P, Q, 2])
        var_eps = sb("var_eps", [P, Q])
        rstd = sb("rstd", [P, Q])
        stats3 = sb("stats3", [P, Q, 6])
        moments3 = sb("moments3", [P, Q, 2])
        var_eps3 = sb("var_eps3", [P, Q])
        rstd3 = sb("rstd3", [P, Q])
        wide = sb("wide", [P, 20, QN])

        def one(k):
            return wide[:, k, :]

        def pair(k):
            return wide[:, k:k + 2, :]

        def by_graph(t):
            return t.rearrange("p (q d) -> p q d", q=Q)

        y, yT = by_graph(one(0)), one(1)
        values = sb("values", [P, 2, Q, H, HD + 1])
        s2, top, part_b = (wide[0:KP, k, :] for k in (3, 4, 5))
        s1 = [wide[0:KP, k, :] for k in (2, 16)]
        part_a = sb("part_a", [KP, QN], BF16)
        part_c = sb("part_c", [KP, QN], BF16)
        s2_parts = sb("s2_parts", [KP, 2, QN], BF16)
        s1_parts = sb("s1_parts", [KP, QN], BF16)
        rowmax = sb("rowmax", [P, Q, H])
        rowmax_dup = sb("rowmax_dup", [P, Q, KP])
        exp1, exp2, probs = pair(6), pair(8), pair(10)
        rden = sb("rden", [P, 2, Q // 2 * H])
        hn, hneg, hexp, ygT = by_graph(one(12)), by_graph(one(13)), by_graph(one(14)), one(15)
        yg = sb("yg", [P, 2, Q, D])
        lg = sb("lg", [P, Q, E0])
        lg2 = sb("lg2", [P, Q, E0])
        score = sb("score", [P, Q, E0])
        first = sb("first", [P, Q, E0])
        second = sb("second", [P, Q, E0])
        peak = sb("peak", [P, Q, 2])
        rmax = sb("rmax", [P, Q])
        gap = sb("gap", [P, Q])
        egap = sb("egap", [P, Q])
        chosen = sb("chosen", [P, Q, E0], BF16)
        seen = sb("seen", [P, Q + 1, E0], BF16)
        rank = sb("rank", [P, Q, E0])
        slot_f = sb("slot_f", [P, Q, 2])
        slot_u = sb("slot_u", [P, 2, Q, 2], U32)
        wgt = sb("wgt", [P, Q, 2])

        x_tile = one(0).rearrange("p (k d) -> p k d", k=4)
        xT_tile = one(1).rearrange("p (k d) -> p k d", k=4)
        silu, hid, hidT = pair(2), pair(4), pair(6)
        y_tile = one(8).rearrange("p (k d) -> p k d", k=4)
        counts = sb("counts", [P, E0])
        pad_f = sb("pad_f", [P, E0])
        pad_u = sb("pad_u", [P, E0], U32)
        tiles_i = sb("tiles_i", [P, 2, E0], I32)
        tiles_f = sb("tiles_f", [P, E0])
        ends = sb("ends", [P, 2, E0])
        closer = sb("closer", [P, E0])
        moved = sb("moved", [P, 2 * B])
        expert_f = sb("expert_f", [1, T0])
        start_f = sb("start_f", [1, T0])
        tile_row = sb("tile_row", [1, T0], I32)
        tile_expert = sb("tile_expert", [1, T0], I32)
        w12_sb = sb("w12_sb", [P, E0, 2 * H0])
        w3_sb = sb("w3_sb", [P, E0, H0 // P, D])
        v1_sb = w12_sb[:, 0:E1, :]
        v2_sb = w12_sb[:, E1:2 * E1, :].rearrange("p e (c d) -> p e c d", d=D)
        bias_rows = wide[0:KP, 12:20, :].rearrange("p k n -> p (k n)")
        c1_parts = sb("c1_parts", [KP, E1 * H1], BF16)
        c2_parts = sb("c2_parts", [KP, E1 * D], BF16)

        hT, msg, agg, adj32, gate_r, gate_z, cand = (pair(k) for k in (0, 2, 4, 6, 8, 10, 12))
        got = wide[:, 16:20, :].rearrange("p (b k) n -> p b (k n)", b=2).rearrange("p b (q k d) -> p b q k d", q=Q, k=2)
        near = sb("near", [P, 2, 2 * Q], U32)
        from_u = sb("from_u", [P, 2 * B], U32)
        gru_w_sb = sb("gru_w_sb", [P, LAYERS, D])
        gru_in = sb("gru_in", [P, 2, 3, D])
        gru_wT = sb("gru_wT", [P, 2, 3, D])
        gru_b = sb("gru_b", [P, 2, 3])
        bias_rz = sb("bias_rz", [P, 2])

        ring = ps("ring", [P, 3, QN])
        tp = ps("tp", [P, QN])
        tp3 = ps("tp3", [P, QN])
        heads = ps("heads", [P, 2, QN])
        small = ps("small", [P, QN])

        rows0 = nc.dram_tensor("rows0", (E0 * CAP + E0 * P, D), F32, kind="Internal").ap()
        outs0 = nc.dram_tensor("outs0", (T0 * P, D), F32, kind="Internal").ap()
        rows1 = nc.dram_tensor("rows1", (E1 * CAP + E1 * P, D), F32, kind="Internal").ap()
        outs1 = nc.dram_tensor("outs1", (T1 * P, D), F32, kind="Internal").ap()

        c_passed, c_consts, c_small, c_wa = sem("c_passed"), sem("c_consts"), sem("c_small"), sem("c_wa")
        x_in = [sem("x_in0"), sem("x_in1")]
        a_mask, a_edges = sem("a_mask"), sem("a_edges")
        a_chain, s_chain, v_chain, f_chain, f_chain2 = (sem(f"{n}_chain") for n in ("ln", "split", "max", "fin", "gate"))
        a_var, a_rstd, a_y, a_yTp, a_yT, a_whp, a_wh = (
            sem(n) for n in ("a_var", "a_rstd", "a_y", "a_yTp", "a_yT", "a_whp", "a_wh"))
        a_s2p, a_s1p, a_s2, a_s1, a_s2parts, a_s1parts = (
            sem(n) for n in ("a_s2p", "a_s1p", "a_s2", "a_s1", "a_s2parts", "a_s1parts"))
        a_maximg, a_rowmax, a_dup, a_maxT = (sem(n) for n in ("a_maximg", "a_rowmax", "a_dup", "a_maxT"))
        p_img1, p_img2, p_exp1, p_exp2, p_probs, p_heads = (
            sem(n) for n in ("p_img1", "p_img2", "p_exp1", "p_exp2", "p_probs", "p_heads"))
        f_divided, f_norm, f_affine, f_var, f_rstd, f_neg, f_exp, f_y, f_yTp, f_yT, f_lgp = (
            sem(n) for n in ("f_divided", "f_norm", "f_affine", "f_var", "f_rstd", "f_neg", "f_exp", "f_y", "f_yTp", "f_yT", "f_lgp"))
        g_gap, g_egap, g_chosen, g_rankp, g_slot = (
            sem(n) for n in ("g_gap", "g_egap", "g_chosen", "g_rankp", "g_slot"))
        sent = [sem("sent0"), sem("sent1")]
        stored = sem("stored")
        i_chain, m_from, r_near = sem("i_chain"), sem("m_from"), sem("r_near")
        c_zero, b_chain = sem("c_zero"), sem("b_chain")
        c_weights1 = sem("c_weights1")
        c_weights, c_gru, c_gruT, c_bias = sem("c_weights"), sem("c_gru"), sem("c_gruT"), sem("c_bias")
        m_count, m_pad, m_padded, m_table, m_chain = (
            sem(n) for n in ("m_count", "m_pad", "m_padded", "m_table", "m_chain"))
        T_SEMS = ("xTp", "xT", "hp", "act", "hid", "hidTp", "hidT", "yp", "y")
        tiles = [{n: sem(f"t{k}_{n}") for n in T_SEMS} for k in range(2)]
        for k in range(2):
            tiles[k]["in"] = [sem(f"t{k}_in{j}") for j in range(4)]
            tiles[k]["out"] = [sem(f"t{k}_out{j}") for j in range(4)]
        r_combined, r_yTp, r_h0, r_adj, r_mp, r_m, r_aggp, r_agg, r_rz, r_sig, r_t, r_n, r_backp = (
            sem(f"r_{n}") for n in ("combined", "yTp", "h0", "adj", "mp", "m", "aggp", "agg", "rz", "sig", "t",
                                    "n", "backp"))
        r_h = [sem("r_hA"), sem("r_hB")]
        r_chain, r_chain2, r_xn, r_back = (sem(f"r_{n}") for n in ("chain", "chain2", "xn", "back"))
        got_in = [sem("got_in0"), sem("got_in1")]
        last_in = [sem("last_in0"), sem("last_in1")]
        last_done, last_chain = sem("last_done"), sem("last_chain")
        GATE = ("chain", "var", "rstd", "y", "yTp", "yT", "lgp", "gap", "egap", "chosen", "rankp", "slot")
        gates = [dict(zip(GATE, (f_chain2, f_var, f_rstd, f_y, f_yTp, f_yT, f_lgp, g_gap, g_egap, g_chosen, g_rankp,
                                 g_slot))),
                 {n: sem(f"g1_{n}") for n in GATE}]
        sents = [sent, [sem("sent2"), sem("sent3")]]
        rows, results = [rows0, rows1], [outs0, outs1]
        mixtures = [(E0, H0, T0), (E1, H1, T1)]

        block = ctx.enter_context(nc.Block())

        def attention_steps(eng, work):
            def step(G):
                groups = [G, G.prev(), G.prev().prev(), G.prev().prev().prev()]
                work(*(a if not isinstance(a.g, int) or 0 <= a.g < NG else None for a in groups))

            for g in range(4):
                step(Group(g // 2, g % 2))
            with eng.Fori(2, NG // 2) as u:
                step(Group(u, 0))
                step(Group(u, 1))
            for g in range(NG, NG + 3):
                step(Group(g // 2, g % 2))

        def tile_steps(eng, T, work):
            for s in range(8):
                work(Tile(0, s), T)
            with eng.Fori(1, T // 8) as i:
                for c in range(8):
                    work(Tile(i, c), T)
            for s in range(T, T + 6):
                work(Tile(0, s), T)

        def recurrence_steps(eng, work):
            work(0, True)
            with eng.Fori(1, NG // 2 - 1) as u:
                work(u, True)
            work(NG // 2 - 1, False)

        def turn(G, l):
            return G.u * (2 * LAYERS) + (2 * l + G.b + 1)

        def norm(G, layer, n):
            return G.g * 2 + n if layer == 0 else G.u * 4 + (2 * (n - 1) + G.b + 1)

        def last_steps(eng, work):
            work(Group(0, 0))
            work(Group(0, 1))
            with eng.Fori(1, NG // 2) as u:
                work(Group(u, 0))
                work(Group(u, 1))

        def apart(eng):
            eng.sem_inc(c_passed, 1)

        def graphs(t, g):
            return t[:, bass.ds(g * Q, Q)]

        @block.sync
        def _(sp):
            for dst, src in (
                    (gat_w_sb[:, :], gat_w), (gate0_sb[:, :], gate0_w), (gate1_sb[:, :], gate1_w),
                    (a_rows[:, 0, :], gat_a1.partition_broadcast(P)), (a_rows[:, 1, :], gat_a2.partition_broadcast(P)),
                    (gamma[:, :], gat_gamma.partition_broadcast(P)), (beta[:, :], gat_beta.partition_broadcast(P)),
                    (gate0_bias[:, :], gate0_b.partition_broadcast(P)),
                    (gate1_bias[:, :], gate1_b.partition_broadcast(P))):
                sp.dma_start(dst, src).then_inc(c_small, 16)
            sp.wait_ge(c_zero, 1)
            for c in range(PARTS):
                sp.dma_start(wide[32 * c:32 * c + 1, 8:8 + E1 * D // QN, :].rearrange("p k n -> p (k n)"),
                             c2.rearrange("(a e) d -> a (e d)", a=1)).then_inc(c_bias, 16)
                sp.dma_start(bias_rows[32 * c:32 * c + 1, :], c1.rearrange("(a e) h -> a (e h)", a=1)).then_inc(c_bias, 16)
            sp.wait_ge(c_consts, 1)
            for c in range(PARTS):
                for k in range(2):
                    r = 32 * c + H * k
                    sp.dma_start(emb[r:r + H, :], gat_emb[1:2, :].rearrange("a h -> h a"),
                                 allow_slow_non_contiguous=True).then_inc(c_small, 16)

            def load(G, M, A, F):
                if G:
                    if not early(G, 2):
                        sp.wait_ge(a_mask, G.g - 1)
                    sp.dma_start(graphs(xs, G.g), x[bass.ds(G.g * Q, Q)].rearrange("q n f -> n q f")).then_inc(
                        x_in[G.b], 16)
                    sp.dma_start(adj_in[:, G.b], adj[bass.ds(G.g * Q, Q)].rearrange("q i j -> i q j")).then_inc(
                        x_in[G.b], 16)

            attention_steps(sp, load)

            def mixture(k):
                E, HID, T = mixtures[k]
                t_ = tiles[k]
                sp.wait_ge(m_table, k + 1)
                for b in range(2):
                    sp.wait_ge(sents[k][b], NG // 2 * 2 * Q * 16)
                sp.wait_ge(m_padded, 16 * (E0 + (E1 if k else 0) + 2))

                def work(t, T):
                    a = t.back(0, T)
                    if a:
                        if not early(a, 4):
                            sp.wait_ge(t_["xTp"], a.g - 3)
                        row = sp.value_load(tile_row[0:1, bass.ds(a.g, 1)], min_val=0, max_val=E * CAP + (E - 1) * P)
                        sp.dma_start(x_tile[:, a.m % 4, :], rows[k][bass.ds(row, P), :]).then_inc(
                            t_["in"][a.m % 4], 16)
                    a = t.back(5, T)
                    if a:
                        sp.wait_ge(t_["y"], a.g + 1)
                        sp.dma_start(results[k][bass.ds(a.g * P, P), :], y_tile[:, a.m % 4, :]).then_inc(
                            t_["out"][a.m % 4], 16)

                tile_steps(sp, T, work)

            mixture(0)
            mixture(1)

            def store(G):
                sp.wait_ge(last_done, G.g + 1)
                apart(sp)
                sp.dma_start(out[bass.ds(G.g * Q, Q)].rearrange("q n f -> n q f"), graphs(xs, G.g)).then_inc(
                    stored, 16)

            last_steps(sp, store)
            sp.wait_ge(stored, NG * 16)

        @block.gpsimd
        def _(pool):
            pool.memset(emb[:, :], 0.0).then_inc(c_consts, 1)
            k = [1]

            def after(ins):
                k[0] += 1
                ins.then_inc(c_consts, 1)
                pool.wait_ge(c_consts, k[0])

            def choose(t, pattern, base_, mult, op, fill):
                after(pool.affine_select(out=t, in_=t, pattern=pattern, compare_op=op, fill=fill, base=base_,
                                         channel_multiplier=mult))

            after(pool.memset(ident[:, :], 0.0))
            choose(ident[:, :], [[-1, P]], 0, 1, ALU.not_equal, 1.0)
            after(pool.tensor_copy(identb[:, :], ident[:, :]))
            after(pool.memset(before[:, :], 0.0))
            choose(before[:, :], [[-1, P]], 0, 1, ALU.is_ge, 1.0)
            after(pool.memset(onesb[:, :], 1.0))
            after(pool.memset(sel[:, :, :], 0.0))
            for c in range(PARTS):
                choose(sel[:, :, :], [[-1, 2 * H], [0, P]], -32 * c, 1, ALU.not_equal, 1.0)
            after(pool.iota(rev[:, :], [[-1, E0]], base=E0, channel_multiplier=0, allow_small_or_imprecise_dtypes=True))
            after(pool.iota(base[:, :], [[CAP, E0]], base=0, channel_multiplier=0, allow_small_or_imprecise_dtypes=True))
            after(pool.iota(lane[:, :], [[0, 1]], base=0, channel_multiplier=1, allow_small_or_imprecise_dtypes=True))
            after(pool.iota(tile_no[:, :], [[1, T0]], base=0, channel_multiplier=0, allow_small_or_imprecise_dtypes=True))
            after(pool.memset(not_hi[:, :], -1.0))
            choose(not_hi[:, :], [[0, 1]], -32, 1, ALU.is_ge, 0.0)
            after(pool.memset(is_lo[:, :], -1.0))
            choose(is_lo[:, :], [[0, 1]], -64, 1, ALU.is_ge, 0.0)
            after(pool.memset(slope[:, :], 1.0))
            for c in range(PARTS):
                choose(slope[:, :], [[0, 1]], 32 * c + H, -1, ALU.is_gt, 0.2)
                choose(slope[:, :], [[0, 1]], 32 * c + 32, -1, ALU.is_gt, 1.0)
            after(pool.memset(minus_half[:, :], -0.5))
            after(pool.memset(zeros[:, :], 0.0))
            after(pool.memset(wa_dup[:, :, :], 0.0))
            after(pool.memset(rowmax_dup[:, :, :], 0.0))
            after(pool.memset(seen[:, 0, :], 0.0))
            after(pool.memset(values[:, :, :, :, :], 1.0))
            assert k[0] == CONSTS, k[0]

            def work(G, M, A, F):
                if F:
                    power(F, 0, 1)
                    pool.wait_ge(f_norm, F.g + 1)
                    pool.tensor_tensor(hn[:, :, :], hn[:, :, :], gamma[:, :].rearrange("p (a f) -> p a f", a=1)
                                       .broadcast_to([P, Q, D]), ALU.mult).then_inc(f_affine, 1)
                    pool.wait_ge(f_affine, F.g * 2 + 1)
                    pool.tensor_tensor(hn[:, :, :], hn[:, :, :], beta[:, :].rearrange("p (a f) -> p a f", a=1)
                                       .broadcast_to([P, Q, D]), ALU.add).then_inc(f_affine, 1)
                if G:
                    pool.wait_ge(a_var, G.g + 1)
                    pool.tensor_tensor(rstd[:, :], var_eps[:, :], minus_half[:, :], ALU.pow).then_inc(a_rstd, 1)
                if F:
                    power(F, 0, 2)
                    if not early(F, 1):
                        send(F.prev(), 0)

            def power(G, k, n):
                pool.wait_ge(gates[k]["var"], norm(G, k, n))
                pool.tensor_tensor(rstd3[:, :], var_eps3[:, :], minus_half[:, :], ALU.pow).then_inc(
                    gates[k]["rstd"], 1)

            def send(G, layer):
                pool.wait_ge(gates[layer]["slot"], G.g + 1)
                apart(pool)
                for q in range(Q):
                    for k in range(2):
                        pool.indirect_dma_start(
                            rows[layer], bass.IndirectOffsetOnAxis(ap=slot_u[:, G.b, q, k:k + 1], axis=0),
                            yg[:, G.b, q, :], None).then_inc(sents[layer][G.b], 16)

            def fetch(G, layer, combined, sems):
                if not early(G, 2):
                    pool.wait_ge(combined, G.g - 1)
                    apart(pool)
                pool.tensor_copy(near[:, G.b], from_u[:, bass.ds(G.g * (2 * Q), 2 * Q)]).then_inc(
                    r_near, 1)
                pool.wait_ge(r_near, G.g + (layer * NG + 1))
                apart(pool)
                for q in range(Q):
                    for k in range(2):
                        pool.indirect_dma_start(
                            got[:, G.b, q, k, :], None, results[layer],
                            bass.IndirectOffsetOnAxis(ap=near[:, G.b, 2 * q + k:2 * q + k + 1], axis=0)).then_inc(sems[G.b], 16)

            def pad(k):
                pool.wait_ge(m_pad, k + 1)
                for e in range(mixtures[k][0]):
                    pool.indirect_dma_start(rows[k], bass.IndirectOffsetOnAxis(ap=pad_u[:, e:e + 1], axis=0),
                                            zeros[:, :], None).then_inc(m_padded, 16)

            def results_stored(k):
                T = mixtures[k][2]
                pool.wait_ge(m_from, k + 1)
                for j in range(4):
                    pool.wait_ge(tiles[k]["out"][j], T // 4 * 16)

            for k in range(2):
                E = mixtures[k][0]
                pool.dma_start(rows[k][E * CAP:, :].rearrange("(e p) d -> p e d", p=P),
                               zeros[:, :].rearrange("p (e d) -> p e d", e=1).broadcast_to([P, E, D])).then_inc(
                    m_padded, 16)
            attention_steps(pool, work)
            send(Group(NG // 2 - 1, 1), 0)
            pad(0)
            results_stored(0)
            def recurrence(u, more):
                if isinstance(u, int) and u == 0:
                    for b in range(2):
                        fetch(Group(u, b), 0, r_combined, got_in)
                for b in range(2):
                    power(Group(u, b), 1, 1)
                if more:
                    for b in range(2):
                        fetch(Group(u + 1, b), 0, r_combined, got_in)
                for b in range(2):
                    power(Group(u, b), 1, 2)
                    send(Group(u, b), 1)

            recurrence_steps(pool, recurrence)
            for b in range(2):
                pool.wait_ge(sents[1][b], NG // 2 * 2 * Q * 16)
            pad(1)
            results_stored(1)
            last_steps(pool, lambda G: fetch(G, 1, last_done, last_in))

        @block.tensor
        def _(pe):
            pe.wait_ge(c_consts, CONSTS)
            pe.wait_ge(c_wa, 8)

            def transpose_x(G):
                pe.wait_ge(a_y, G.g + 1)
                if not early(G, 1):
                    pe.wait_ge(a_wh, G.g)
                for q in range(Q):
                    ins = pe.transpose(tp[:, q * P:(q + 1) * P], y[:, q, :], ident[:, :])
                ins.then_inc(a_yTp, 1)

            def score_s2(G):
                pe.wait_ge(a_yT, G.g + 1)
                pe.matmul(tp[0:KP, :], wa_dup[:, 1, :], yT[:, :], start=True, stop=True).then_inc(a_s2p, 1)

            def score_s1(G):
                pe.wait_ge(a_s2, G.g + 1)
                pe.matmul(tp[0:KP, :], wa_dup[:, 0, :], yT[:, :], start=True, stop=True).then_inc(a_s1p, 1)

            def product(G):
                pe.wait_ge(a_s1, G.g + 1)
                for q in range(Q):
                    ins = pe.matmul(tp[:, q * P:(q + 1) * P], yT[:, q * P:(q + 1) * P], gat_w_sb[:, :],
                                    start=True, stop=True)
                ins.then_inc(a_whp, 1)

            def max_image(G, h):
                if h == 0:
                    pe.wait_ge(a_s2parts, G.g + 1)
                    pe.wait_ge(a_mask, G.g + 1)
                    if not early(G, 1):
                        pe.wait_ge(a_s1parts, G.g)
                else:
                    pe.wait_ge(a_rowmax, H * G.g + h)
                pe.matmul(ring[:, 2, :], sel[:, h, :], s2_parts[:, G.b, :], start=True, stop=False)
                pe.matmul(ring[:, 2, :], identb[:, :], mask[:, G.b].rearrange("p q n -> p (q n)"),
                          start=False, stop=True).then_inc(a_maximg, 1)

            def image(G, h, k):
                bank = ring[:, k, :]
                row = sel[:, H * k + h, :]
                if not (h == 0 and early(G, 1)):
                    pe.wait_ge((p_exp1, p_exp2)[k], H * G.g + h)
                pe.matmul(bank, row, s1_parts[:, :], start=True, stop=False)
                for q in range(Q):
                    cols = slice(q * P, (q + 1) * P)
                    pe.matmul(bank[:, cols], s2_parts[:, G.b, cols], row, start=False, stop=False)
                    ins = pe.matmul(bank[:, cols], mask[:, G.b, q, :], identb[:, :], start=False, stop=(q == Q - 1))
                ins.then_inc((p_img1, p_img2)[k], 1)

            def attend_head(G, h):
                pe.wait_ge(p_probs, H * G.g + h + 1)
                if h == 0:
                    pe.wait_ge(a_wh, G.g + 1)
                    if not early(G, 1):
                        pe.wait_ge(f_divided, 2 * G.g)
                for q in range(Q):
                    c = (q % 2) * H * (HD + 1) + h * (HD + 1)
                    ins = pe.matmul(heads[:, q // 2, c:c + HD + 1], probs[:, h % 2, q * P:(q + 1) * P],
                                    values[:, G.b, q, h, :], start=True, stop=True, skip_group_check=True)
                ins.then_inc(p_heads, 1)

            def transpose_yg(G, k):
                gs = gates[k]
                pe.wait_ge(gs["y"], G.g + 1)
                for q in range(Q):
                    ins = pe.transpose(tp3[:, q * P:(q + 1) * P], yg[:, G.b, q, :], ident[:, :])
                ins.then_inc(gs["yTp"], 1)

            def logits(G, k):
                E, gs, gate_w = mixtures[k][0], gates[k], (gate0_sb, gate1_sb)[k]
                pe.wait_ge(gs["yT"], G.g + 1)
                if not early(G, 1):
                    pe.wait_ge(gs["slot"], G.g)
                for q in range(Q):
                    ins = pe.matmul(small[:, q * E:(q + 1) * E], ygT[:, q * P:(q + 1) * P], gate_w[:, :],
                                    start=True, stop=True)
                ins.then_inc(gs["lgp"], 1)

            def ranks(G, k):
                E, gs = mixtures[k][0], gates[k]
                pe.wait_ge(gs["chosen"], G.g + 1)
                pe.matmul(small[:, 0:Q * E], before[:, :], chosen[:, :, 0:E], start=True, stop=False)
                pe.matmul(small[:, 0:Q * E], onesb[:, :], seen[:, 0:Q, 0:E], start=False, stop=True).then_inc(
                    gs["rankp"], 1)

            def work(G, M, A, F):
                if A:
                    pe.wait_ge(a_s1parts, A.g + 1)
                for h in range(H + 1):
                    if A and h < H:
                        image(A, h, 0)
                        image(A, h, 1)
                    if M and h > 0:
                        max_image(M, h - 1)
                    if A and h > 0:
                        attend_head(A, h - 1)
                    if G:
                        {4: transpose_x, 5: score_s2, 6: score_s1, 7: product}.get(h, lambda G: None)(G)
                    if F:
                        {5: transpose_yg, 6: logits}.get(h, lambda G, k: None)(F, 0)
                if M:
                    pe.wait_ge(a_dup, M.g + 1)
                    for q in range(Q):
                        ins = pe.transpose(ring[0:KP, 2, q * P:(q + 1) * P], rowmax_dup[:, q, :], ident[:, :])
                    ins.then_inc(a_maxT, 1)
                if F:
                    ranks(F, 0)

            def count(k):
                E = mixtures[k][0]
                pe.wait_ge(gates[k]["slot"], NG)
                pe.matmul(small[:, 0:E], onesb[:, :], seen[:, Q, 0:E], start=True, stop=True).then_inc(m_count, 1)

            def mixture(k):
                E, HID, T = mixtures[k]
                C = HID // P
                t_ = tiles[k]
                w_in, w_out = ((w12_sb, w3_sb), (v1_sb, v2_sb))[k]
                pe.wait_ge(m_table, k + 1)
                pe.wait_ge(*((c_weights, WEIGHTS), (c_weights1, WEIGHTS1))[k])
                xT_banks, h_banks, hT_banks, y_banks = (tp, tp3), (ring[:, 0], ring[:, 1]), (ring[:, 2], small), (
                    heads[:, 0], heads[:, 1])

                experts = {}

                def expert(a):
                    key = (id(a.i), a.off)
                    if key not in experts:
                        experts[key] = pe.value_load(tile_expert[0:1, bass.ds(a.g, 1)], min_val=0, max_val=E - 1)
                    return experts[key]

                def work(t, T):
                    a = t.back(2, T)
                    if a:
                        expert(a)
                    a = t.back(1, T)
                    if a:
                        pe.wait_ge(t_["in"][a.m % 4], 16 * a.uses(4))
                        if not early(a, 2):
                            pe.wait_ge(t_["xT"], a.g - 1)
                        pe.transpose(xT_banks[a.m % 2][:, 0:P], x_tile[:, a.m % 4, :], ident[:, :]).then_inc(
                            t_["xTp"], 1)
                    a = t.back(2, T)
                    if a:
                        e = expert(a)
                        bank = h_banks[a.m % 2]
                        pe.wait_ge(t_["xT"], a.g + 1)
                        if not early(a, 2):
                            pe.wait_ge(t_["hid"], a.g - 1)
                        ins = pe.matmul(bank, xT_tile[:, a.m % 4, :], w_in[:, bass.ds(e, 1), :], start=True,
                                        stop=(k == 0))
                        if k:
                            ins = pe.matmul(bank, onesb[0:KP, :], c1_parts[:, bass.ds(e * H1, H1)], start=False,
                                            stop=True)
                        ins.then_inc(t_["hp"], 1)
                    a = t.back(3, T)
                    if a:
                        pe.wait_ge(t_["hid"], a.g + 1)
                        if not early(a, 2):
                            pe.wait_ge(t_["hidT"], a.g - 1)
                        for c in range(C):
                            ins = pe.transpose(hT_banks[a.m % 2][:, c * P:(c + 1) * P],
                                               hid[:, a.m % 2, c * P:(c + 1) * P], ident[:, :])
                        ins.then_inc(t_["hidTp"], 1)
                    a = t.back(4, T)
                    if a:
                        e = expert(a)
                        bank = y_banks[a.m % 2][:, 0:D]
                        pe.wait_ge(t_["hidT"], a.g + 1)
                        if not early(a, 2):
                            pe.wait_ge(t_["y"], a.g - 1)
                        for c in range(C):
                            ins = pe.matmul(bank, hidT[:, a.m % 2, c * P:(c + 1) * P],
                                            w_out[:, bass.ds(e, 1), c, :], start=(c == 0),
                                            stop=(k == 0 and c == C - 1))
                        if k:
                            ins = pe.matmul(bank, onesb[0:KP, :], c2_parts[:, bass.ds(e * D, D)], start=False,
                                            stop=True)
                        ins.then_inc(t_["yp"], 1)

                tile_steps(pe, T, work)

            def recurrence(u, more):
                groups = [Group(u, b) for b in range(2)]
                for G in groups:
                    pe.wait_ge(r_xn, G.g + 1)
                    for q in range(Q):
                        ins = pe.transpose(tp[:, q * P:(q + 1) * P], yg[:, G.b, q, :], ident[:, :])
                    ins.then_inc(r_yTp, 1)
                    pe.wait_ge(r_h0, G.g + 1)
                for l in range(LAYERS):
                    for G in groups:
                        n = turn(G, l)
                        bank = heads[:, G.b, :]
                        state = hT[:, G.b, :]
                        if l:
                            pe.wait_ge(r_h[G.b], G.u * LAYERS + l)
                        for q in range(Q):
                            ins = pe.matmul(bank[:, q * P:(q + 1) * P], state[:, q * P:(q + 1) * P], gru_w_sb[:, l, :],
                                            start=True, stop=True)
                        ins.then_inc(r_mp, 1)
                        if not (isinstance(n, int) and n == 1):
                            pe.wait_ge(r_t, n - 1)
                        pe.matmul(ring[:, 0, :], gru_wT[:, 1, 0, :], state, start=True, stop=False)
                        pe.matmul(ring[:, 1, :], gru_wT[:, 1, 1, :], state, start=True, stop=False)
                        pe.matmul(small[:, :], gru_wT[:, 1, 2, :], state, start=True, stop=True)
                        pe.wait_ge(r_m, turn(G, l))
                        for q in range(Q):
                            ins = pe.matmul(bank[:, q * P:(q + 1) * P], msg[:, G.b, q * P:(q + 1) * P],
                                            adj32[:, G.b, q * P:(q + 1) * P], start=True, stop=True)
                        ins.then_inc(r_aggp, 1)
                        pe.wait_ge(r_agg, turn(G, l))
                        pe.matmul(ring[:, 0, :], gru_wT[:, 0, 0, :], agg[:, G.b, :], start=False, stop=True)
                        pe.matmul(ring[:, 1, :], gru_wT[:, 0, 1, :], agg[:, G.b, :], start=False, stop=True)
                        pe.matmul(ring[:, 2, :], gru_wT[:, 0, 2, :], agg[:, G.b, :], start=True, stop=True).then_inc(
                            r_rz, 1)
                for G in groups:
                    pe.wait_ge(r_h[G.b], (G.u + 1) * LAYERS)
                    for q in range(Q):
                        ins = pe.transpose(tp[:, q * P:(q + 1) * P], hT[:, G.b, q * P:(q + 1) * P], ident[:, :])
                    ins.then_inc(r_backp, 1)
                    transpose_yg(G, 1)
                    logits(G, 1)
                    ranks(G, 1)

            pe.wait_ge(c_gru, GRU)
            for k in range(2):
                for c in range(3):
                    ins = pe.transpose((tp, tp3)[k][:, c * P:(c + 1) * P], gru_in[:, k, c, :], ident[:, :])
            ins.then_inc(c_gruT, 1)
            pe.wait_ge(c_gruT, 3)
            attention_steps(pe, work)
            count(0)
            mixture(0)
            recurrence_steps(pe, recurrence)
            count(1)
            mixture(1)

        @block.scalar
        def _(act):
            act.wait_ge(c_consts, CONSTS)
            act.wait_ge(c_small, SMALL)

            def copy_yT(G):
                act.wait_ge(a_yTp, G.g + 1)
                act.copy(yT[:, :], tp[:, :]).then_inc(a_yT, 1)

            def scale_s2(G):
                act.wait_ge(a_s2p, G.g + 1)
                if not early(G, 1):
                    act.wait_ge(a_s2parts, G.g)
                act.activation(s2[:, :], tp[0:KP, :], ACT.Copy, scale=slope[:, 0:1]).then_inc(a_s2, 1)

            def copy_s1(G):
                act.wait_ge(a_s1p, G.g + 1)
                if not early(G, 2):
                    act.wait_ge(a_s1parts, G.g - 1)
                act.activation(s1[G.b][:, :], tp[0:KP, :], ACT.Identity, bias=emb[:, 0:1]).then_inc(a_s1, 1)

            def edge_masks(G):
                act.wait_ge(x_in[G.b], 32 * G.u + 32)
                apart(act)
                act.copy(graphs(edges, G.g), adj_in[:, G.b]).then_inc(a_edges, 1)
                act.activation(mask[:, G.b], adj_in[:, G.b], ACT.Copy, scale=-MASKED, bias=MASKED).then_inc(a_mask, 1)

            def work(G, M, A, F):
                for h in range(H):
                    if A:
                        if not (early(A, 1) and h < 2):
                            act.wait_ge(p_probs, H * A.g + h - 1)
                        act.wait_ge(p_img1, H * A.g + h + 1)
                        act.activation(exp1[:, h % 2, :], ring[:, 0, :], ACT.Exp).then_inc(p_exp1, 1)
                        act.wait_ge(p_img2, H * A.g + h + 1)
                        act.activation(exp2[:, h % 2, :], ring[:, 1, :], ACT.Exp).then_inc(p_exp2, 1)
                    if G:
                        {4: copy_yT, 5: scale_s2, 6: copy_s1}.get(h, lambda G: None)(G)
                    if F and h == 3:
                        act.wait_ge(f_neg, F.g + 1)
                        act.activation(hexp[:, :, :], hneg[:, :, :], ACT.Exp).then_inc(f_exp, 1)
                    if F and h == 5:
                        copy_ygT(F, 0)
                if G:
                    edge_masks(G)
                    act.wait_ge(a_whp, G.g + 1)
                    if A:
                        act.wait_ge(p_heads, H * (A.g + 1))
                    act.copy(values[:, G.b, :, :, 0:HD].rearrange("p q h d -> p (q h) d"),
                             tp[:, :].rearrange("p (a d) -> p a d", d=HD)).then_inc(a_wh, 1)
                if F:
                    gap_exp(F, 0)

            def copy_ygT(G, k):
                gs = gates[k]
                act.wait_ge(gs["yTp"], G.g + 1)
                act.copy(ygT[:, :], tp3[:, :]).then_inc(gs["yT"], 1)

            def gap_exp(G, k):
                gs = gates[k]
                act.wait_ge(gs["gap"], G.g + 1)
                act.activation(egap[:, :], gap[:, :], (ACT.Exp, ACT.Sigmoid)[k]).then_inc(gs["egap"], 1)

            def mixture(k):
                t_ = tiles[k]
                HID, T = mixtures[k][1:]

                def work(t, T):
                    a = t.back(2, T)
                    if a:
                        act.wait_ge(t_["hp"], a.g + 1)
                        bank = ring[:, a.m % 2, :]
                        if k == 0:
                            if not early(a, 2):
                                act.wait_ge(t_["hid"], a.g - 1)
                            act.activation(silu[:, a.m % 2, 0:H0], bank[:, 0:H0], ACT.Silu).then_inc(t_["act"], 1)
                        else:
                            if not early(a, 2):
                                act.wait_ge(t_["hidTp"], a.g - 1)
                            act.activation(hid[:, a.m % 2, :], bank, ACT.Gelu).then_inc(t_["hid"], 1)
                    a = t.back(3, T)
                    if a and k == 0:
                        act.wait_ge(t_["hidTp"], a.g + 1)
                        if not early(a, 2):
                            act.wait_ge(t_["yp"], a.g - 1)
                        act.copy(hidT[:, a.m % 2, 0:HID], (ring[:, 2, :], small)[a.m % 2][:, 0:HID]).then_inc(
                            t_["hidT"], 1)

                tile_steps(act, T, work)

            def recurrence(u, more):
                groups = [Group(u, b) for b in range(2)]
                for G in groups:
                    act.wait_ge(r_yTp, G.g + 1)
                    act.copy(hT[:, G.b, :], tp[:, :]).then_inc(r_h0, 1)
                for l in range(LAYERS):
                    for G in groups:
                        n = turn(G, l)
                        act.wait_ge(r_mp, n)
                        act.copy(msg[:, G.b, :], heads[:, G.b, :]).then_inc(r_m, 1)
                        act.wait_ge(r_aggp, n)
                        act.copy(agg[:, G.b, :], heads[:, G.b, :]).then_inc(r_agg, 1)
                        act.wait_ge(r_rz, n)
                        act.activation(gate_r[:, G.b, :], ring[:, 0, :], ACT.Sigmoid, bias=bias_rz[:, 0:1]).then_inc(
                            r_sig, 1)
                        act.activation(gate_z[:, G.b, :], ring[:, 1, :], ACT.Sigmoid, bias=bias_rz[:, 1:2]).then_inc(
                            r_sig, 1)
                        act.wait_ge(r_t, n)
                        act.activation(cand[:, G.b, :], cand[:, G.b, :], ACT.Tanh, bias=gru_b[:, 0, 2:3]).then_inc(
                            r_n, 1)
                for G in groups:
                    copy_ygT(G, 1)
                    gap_exp(G, 1)

            act.dma_start(gru_w_sb[:, :, :], gru_w.rearrange("l d e -> d l e")).then_inc(c_gru, 16)
            for k, w in enumerate((w_ih, w_hh)):
                act.dma_start(gru_in[:, k], w.rearrange("(c e) d -> e c d", c=3)).then_inc(c_gru, 16)
            for k, w in enumerate((b_ih, b_hh)):
                act.dma_start(gru_b[:, k, :], w.rearrange("(c e) -> e c", c=3),
                              allow_slow_non_contiguous=True).then_inc(c_gru, 16)
            act.dma_start(w12_sb[:, :, 0:H0], w1.rearrange("e d h -> d e h")).then_inc(c_weights, 16)
            act.dma_start(w12_sb[:, :, H0:2 * H0], w2.rearrange("e d h -> d e h")).then_inc(c_weights, 16)
            for c in range(H0 // P):
                act.dma_start(w3_sb[:, :, c, :], w3[:, c * P:(c + 1) * P, :].rearrange("e k o -> k e o")).then_inc(
                    c_weights, 16)
            act.wait_ge(c_gruT, 1)
            for k in range(2):
                act.copy(gru_wT[:, k].rearrange("p c e -> p (c e)"), (tp, tp3)[k][:, 0:3 * P]).then_inc(c_gruT, 1)
            attention_steps(act, work)
            mixture(0)
            act.wait_ge(tiles[0]["yp"], T0)
            act.dma_start(v1_sb, v1.rearrange("e d h -> d e h")).then_inc(c_weights1, 16)
            for c in range(H1 // P):
                act.dma_start(v2_sb[:, :, c, :], v2[:, c * P:(c + 1) * P, :].rearrange("e k o -> k e o")).then_inc(
                    c_weights1, 16)
            recurrence_steps(act, recurrence)
            mixture(1)

        @block.vector
        def _(dve):
            dve.memset(wide[0:KP, 8:20, :], 0.0).then_inc(c_zero, 1)
            dve.wait_ge(c_consts, CONSTS)
            dve.wait_ge(c_small, SMALL)
            for k in range(2):
                dve.tensor_tensor(prod[:, :].rearrange("p (h d) -> p h d", d=HD),
                                  gat_w_sb[:, :].rearrange("p (h d) -> p h d", d=HD),
                                  a_rows[:, k:k + 1, :].broadcast_to([P, H, HD]), ALU.mult).then_inc(c_wa, 1)
                dve.wait_ge(c_wa, 2 * k + 1)
                dve.tensor_reduce(wa[:, k, :], prod[:, :].rearrange("p (h d) -> p h d", d=HD), AX.X,
                                  ALU.add).then_inc(c_wa, 1)
                dve.wait_ge(c_wa, 2 * k + 2)
            for k in range(2):
                for c in range(2):
                    view = wa_dup[:, k, H * c:H * c + H]
                    dst = bass.AP(view.tensor, view.offset, [view.ap[0], [32, PARTS], [1, H]])
                    dve.tensor_copy(dst, wa[:, k:k + 1, :].broadcast_to([P, PARTS, H])).then_inc(c_wa, 1)

            def features(G):
                if isinstance(G.g, int):
                    return lambda q: xs[:, G.g * Q + q, :]
                return lambda q: xs[:, bass.ds(G.g * Q + q, 1), :].rearrange("p a f -> p (a f)")

            def moments_of(ch, src, stats_, moments_):
                for q in range(Q):
                    ins = dve.bn_stats(stats_[:, q, :], src(q))
                ch.step(ins, apart)
                for q in range(Q):
                    ins = dve.bn_aggr(moments_[:, q, :], stats_[:, q, :])
                ch.step(ins)

            def split(ch, src, dst):
                ch.step(dve.tensor_copy(part_a[:, :], src))
                ch.step(dve.scalar_tensor_tensor(part_b[:, :], part_a[:, :], not_hi[:, 0:1], src, ALU.mult, ALU.add))
                ch.step(dve.tensor_copy(part_c[:, :], part_b[:, :]))
                return dve.scalar_tensor_tensor(dst, part_c[:, :], is_lo[:, 0:1], part_b[:, :], ALU.mult, ALU.add)

            def normal_x_a(G):
                ch = Chain(dve, a_chain, 2, G.g)
                dve.wait_ge(x_in[G.b], 32 * G.u + 32)
                apart(dve)
                moments_of(ch, features(G), stats, moments)
                ch.end()
                dve.tensor_scalar(var_eps[:, :], moments[:, :, 1], EPS, None, ALU.add).then_inc(a_var, 1)

            def normal_x_b(G):
                dve.wait_ge(a_rstd, G.g + 1)
                for q in range(Q):
                    ins = dve.tensor_scalar(y[:, q, :], features(G)(q), moments[:, q, 0:1], rstd[:, q:q + 1],
                                            ALU.subtract, ALU.mult)
                ins.then_inc(a_y, 1)

            def split_s2(G):
                sc = Chain(dve, s_chain, 3, G.g)
                dve.wait_ge(a_s2, G.g + 1)
                split(sc, s2[:, :], s2_parts[:, G.b, :]).then_inc(a_s2parts, 1)
                sc.end()

            def spread_maxima(G):
                dve.wait_ge(a_rowmax, H * G.g + H)
                for c in range(PARTS):
                    view = rowmax_dup[:, :, 32 * c:32 * c + 2 * H].rearrange("p q (k h) -> p q k h", k=2)
                    ins = dve.tensor_copy(view, rowmax[:, :, :].rearrange("p q (k h) -> p q k h", k=1).broadcast_to(
                        [P, Q, 2, H]))
                ins.then_inc(a_dup, 1)

            def subtract_maxima(G):
                ch = Chain(dve, v_chain, 6, G.g)
                s1_ = s1[G.b]
                dve.wait_ge(a_maxT, G.g + 1)
                dve.wait_ge(a_s1, G.g + 1)
                ch.step(dve.tensor_tensor(top[:, :], s1_[:, :], ring[0:KP, 2, :], ALU.add))
                ch.step(dve.scalar_tensor_tensor(top[:, :], top[:, :], 0.2, top[:, :], ALU.mult, ALU.max))
                ch.step(dve.scalar_tensor_tensor(top[:, :], s1_[:, :], slope[:, 0:1], top[:, :], ALU.mult,
                                                 ALU.subtract))
                split(ch, top[:, :], s1_parts[:, :]).then_inc(a_s1parts, 1)
                ch.end()

            def divide(G, ch):
                dve.wait_ge(p_heads, H * (G.g + 1))
                view = heads[:, :, 0:2 * H * (HD + 1)].rearrange("p a (h d) -> p a h d", d=HD + 1)
                dve.reciprocal(rden[:, :, :], view[:, :, :, HD]).then_inc(f_divided, 1)
                dve.wait_ge(f_divided, 2 * G.g + 1)
                dve.tensor_tensor(hn[:, :, :].rearrange("p (a b) (h d) -> p a (b h) d", a=2, d=HD),
                                  view[:, :, :, 0:HD],
                                  rden[:, :, :].rearrange("p a (h d) -> p a h d", d=1).broadcast_to(
                                      [P, 2, 2 * H, HD]), ALU.mult).then_inc(f_divided, 1)
                dve.wait_ge(f_divided, 2 * G.g + 2)
                apart(dve)
                moments_of(ch, lambda q: hn[:, q, :], stats3, moments3)
                dve.tensor_scalar(var_eps3[:, :], moments3[:, :, 1], EPS, None, ALU.add).then_inc(f_var, 1)

            def normal_h(G, ch):
                dve.wait_ge(f_rstd, norm(G, 0, 1))
                for q in range(Q):
                    ins = dve.tensor_scalar(hn[:, q, :], hn[:, q, :], moments3[:, q, 0:1], rstd3[:, q:q + 1],
                                            ALU.subtract, ALU.mult)
                ins.then_inc(f_norm, 1)

            def elu_a(G, ch):
                dve.wait_ge(f_affine, 2 * G.g + 2)
                dve.tensor_scalar(hneg[:, :, :], hn[:, :, :], 0.0, None, ALU.min).then_inc(f_neg, 1)

            def elu_b(G, ch):
                dve.wait_ge(f_exp, G.g + 1)
                ch.step(dve.scalar_tensor_tensor(hn[:, :, :], hn[:, :, :], 0.0, hexp[:, :, :], ALU.max, ALU.add))
                ch.step(dve.scalar_tensor_tensor(graphs(xs, G.g), hn[:, :, :], -1.0, graphs(xs, G.g), ALU.add,
                                                 ALU.add), apart)
                ch.end()

            def normalise_and_gate(G, layer):
                ch = Chain(dve, gates[layer]["chain"], FIN2, G.g)
                normal_a(G, layer, ch)
                normal_b(G, layer, ch)
                choose(G, layer, ch)
                pick_slots(G, layer, ch)
                ch.end()

            def normal_a(G, layer, ch):
                moments_of(ch, features(G), stats3, moments3)
                dve.tensor_scalar(var_eps3[:, :], moments3[:, :, 1], EPS, None, ALU.add).then_inc(
                    gates[layer]["var"], 1)

            def normal_b(G, layer, ch):
                gs, sent, src = gates[layer], sents[layer], features(G)
                if not early(G, 2):
                    dve.wait_ge(sent[G.b], G.u * (2 * Q * 16))
                dve.wait_ge(gs["rstd"], norm(G, layer, 2))
                for q in range(Q):
                    ins = dve.tensor_scalar(yg[:, G.b, q, :], src(q), moments3[:, q, 0:1], rstd3[:, q:q + 1],
                                            ALU.subtract, ALU.mult)
                ins.then_inc(gs["y"], 1)

            def choose(G, layer, ch):
                gs, E, bias = gates[layer], mixtures[layer][0], (gate0_bias, gate1_bias)[layer]

                def wide(t):
                    return t.rearrange("p (q a) -> p q a", a=1).broadcast_to([P, Q, E])

                L, S, F1, F2 = lg[:, :, 0:E], score[:, :, 0:E], first[:, :, 0:E], second[:, :, 0:E]
                revs = rev[:, 0:E].rearrange("p (a e) -> p a e", a=1).broadcast_to([P, Q, E])
                dve.wait_ge(gs["lgp"], G.g + 1)
                ch.step(dve.tensor_tensor(L, small[:, 0:Q * E].rearrange("p (q e) -> p q e", e=E),
                                          bias[:, 0:E].rearrange("p (a e) -> p a e", a=1).broadcast_to([P, Q, E]),
                                          ALU.add))
                for k, (src_, one) in enumerate(((L, F1), (lg2[:, :, 0:E], F2))):
                    ch.step(dve.tensor_reduce(peak[:, :, k], src_, AX.X, ALU.max))
                    ch.step(dve.tensor_tensor(S, src_, peak[:, :, k:k + 1].broadcast_to([P, Q, E]), ALU.is_equal))
                    ch.step(dve.tensor_tensor(S, S, revs, ALU.mult))
                    ch.step(dve.tensor_reduce(rmax[:, :], S, AX.X, ALU.max))
                    ch.step(dve.tensor_tensor(one, S, wide(rmax[:, :]), ALU.is_equal))
                    if k == 0:
                        ch.step(dve.scalar_tensor_tensor(lg2[:, :, 0:E], one, -3e38, L, ALU.mult, ALU.add))
                dve.tensor_tensor(gap[:, :], peak[:, :, 1], peak[:, :, 0], ALU.subtract).then_inc(gs["gap"], 1)
                ch.step(dve.tensor_tensor(chosen[:, :, 0:E], F1, F2, ALU.add))
                if not early(G, 1):
                    ch.step(dve.tensor_copy(seen[:, 0, 0:E], seen[:, Q, 0:E]))
                else:
                    ch.step(dve.memset(seen[:, 0, 0:E], 0.0))
                for q in range(Q):
                    ins = dve.tensor_tensor(seen[:, q + 1, 0:E], seen[:, q, 0:E], chosen[:, q, 0:E], ALU.add)
                    if q < Q - 1:
                        ch.step(ins)
                ins.then_inc(gs["chosen"], 1)

            def pick_slots(G, layer, ch):
                gs, E = gates[layer], mixtures[layer][0]
                S, F1, F2 = score[:, :, 0:E], first[:, :, 0:E], second[:, :, 0:E]
                dve.wait_ge(gs["egap"], G.g + 1)
                if layer == 0:
                    ch.step(dve.tensor_scalar(rmax[:, :], egap[:, :], 1.0, None, ALU.add))
                    ch.step(dve.reciprocal(wgt[:, :, 0], rmax[:, :]))
                    ch.step(dve.tensor_tensor(wgt[:, :, 1], wgt[:, :, 0], egap[:, :], ALU.mult))
                else:
                    ch.step(dve.tensor_copy(wgt[:, :, 1], egap[:, :]))
                    ch.step(dve.tensor_scalar(wgt[:, :, 0], egap[:, :], -1.0, 1.0, ALU.mult, ALU.add))
                    ch.step(dve.tensor_copy(rmax[:, :], wgt[:, :, 0]))
                dve.tensor_scalar(graphs(gate_all, G.g), wgt[:, :, :], 1.0, None, ALU.mult)
                dve.wait_ge(gs["rankp"], G.g + 1)
                ch.step(dve.tensor_tensor(rank[:, :, 0:E], small[:, 0:Q * E].rearrange("p (q e) -> p q e", e=E),
                                          base[:, 0:E].rearrange("p (a e) -> p a e", a=1).broadcast_to([P, Q, E]),
                                          ALU.add))
                for k, one in enumerate((F1, F2)):
                    ch.step(dve.tensor_tensor(S, one, rank[:, :, 0:E], ALU.mult))
                    ch.step(dve.tensor_reduce(slot_f[:, :, k], S, AX.X, ALU.add))
                ch.step(dve.tensor_scalar(graphs(slot_all, G.g), slot_f[:, :, :], 1.0, None, ALU.mult))
                dve.tensor_copy(slot_u[:, G.b], slot_f[:, :, :]).then_inc(gs["slot"], 1)

            def work(G, M, A, F):
                if F:
                    fin = Chain(dve, f_chain, FIN, F.g)
                    gate = Chain(dve, gates[0]["chain"], FIN2, F.g)
                    divide(F, fin)
                for h in range(H + 1):
                    if A and h < H:
                        if not (early(A, 1) and h < 2):
                            dve.wait_ge(p_heads, H * A.g + h - 1)
                        dve.wait_ge(p_exp2, H * A.g + h + 1)
                        dve.tensor_tensor(probs[:, h % 2, :], exp1[:, h % 2, :], exp2[:, h % 2, :],
                                          ALU.max).then_inc(p_probs, 1)
                    if M and h > 0:
                        dve.wait_ge(a_maximg, H * M.g + h)
                        dve.tensor_reduce(rowmax[:, :, h - 1], ring[:, 2, :].rearrange("p (q n) -> p q n", q=Q), AX.X,
                                          ALU.max).then_inc(a_rowmax, 1)
                    if G and h == 2:
                        normal_x_a(G)
                    if F and h == 1:
                        normal_h(F, fin)
                    if F and h == 2:
                        elu_a(F, fin)
                    if F and h == 3:
                        elu_b(F, fin)
                        normal_a(F, 0, gate)
                    if G and h == 3:
                        normal_x_b(G)
                    if F and h == 4:
                        normal_b(F, 0, gate)
                    if F and h == 7:
                        choose(F, 0, gate)
                if M:
                    spread_maxima(M)
                if G:
                    split_s2(G)
                if M:
                    subtract_maxima(M)
                if F:
                    pick_slots(F, 0, gate)
                    gate.end()

            def plan(k):
                E, HID, T = mixtures[k]
                ch = Chain(dve, m_chain, PLAN, 0)
                ch.k = PLAN if k else 0
                dve.wait_ge(m_count, k + 1)
                if k:
                    dve.wait_ge(m_padded, 16 * (E0 + 2))
                ch.step(dve.tensor_copy(counts[:, 0:E], small[:, 0:E]))
                ch.step(dve.tensor_tensor(pad_f[:, 0:E], counts[:, 0:E], base[:, 0:E], ALU.add))
                dve.tensor_scalar(pad_u[:, 0:E], pad_f[:, 0:E], lane[:, 0:1], None, ALU.add).then_inc(m_pad, 1)
                ch.step(dve.tensor_scalar(tiles_i[:, 0, 0:E], counts[:, 0:E], float(P - 1), None, ALU.add))
                ch.step(dve.tensor_scalar(tiles_i[:, 1, 0:E], tiles_i[:, 0, 0:E], P.bit_length() - 1, None,
                                          ALU.logical_shift_right))
                ch.step(dve.tensor_copy(tiles_f[:, 0:E], tiles_i[:, 1, 0:E]))
                ch.step(dve.tensor_copy(ends[:, 0, 0:E], tiles_f[:, 0:E]))
                dve.memset(closer[:, 0:1], 0.0)
                dve.tensor_scalar(closer[:, 1:E], tiles_f[:, 0:E - 1], float(P), -float(CAP), ALU.mult, ALU.add)
                src, step = 0, 1
                while step < E:
                    dve.tensor_copy(ends[:, 1 - src, 0:step], ends[:, src, 0:step])
                    ch.step(dve.tensor_tensor(ends[:, 1 - src, step:E], ends[:, src, step:E],
                                              ends[:, src, 0:E - step], ALU.add))
                    src, step = 1 - src, 2 * step
                flat = wide[0:1, :, :].rearrange("p k n -> p (k n)")
                past = flat[:, 0:T * E].rearrange("p (t e) -> p t e", e=E)
                held = flat[:, T0 * E0:T0 * E0 + T * E].rearrange("p (t e) -> p t e", e=E)

                def per_tile(t):
                    return t.rearrange("p (a e) -> p a e", a=1).broadcast_to([1, T, E])

                ch.step(dve.tensor_tensor(past, tile_no[:, 0:T].rearrange("p (t a) -> p t a", a=1).broadcast_to(
                    [1, T, E]), per_tile(ends[0:1, src, 0:E]), ALU.is_ge))
                ch.step(dve.tensor_tensor(held, past, per_tile(tiles_f[0:1, 0:E]), ALU.mult))
                ch.step(dve.tensor_reduce(expert_f[:, 0:T], past, AX.X, ALU.add))
                ch.step(dve.tensor_reduce(start_f[:, 0:T], held, AX.X, ALU.add))
                ch.step(dve.tensor_tensor(start_f[:, 0:T], tile_no[:, 0:T], start_f[:, 0:T], ALU.subtract))
                ch.step(dve.tensor_scalar(start_f[:, 0:T], start_f[:, 0:T], float(P), None, ALU.mult))
                ch.step(dve.tensor_scalar(tile_expert[:, 0:T], expert_f[:, 0:T], float(E - 1), None, ALU.min))
                ch.step(dve.tensor_scalar(expert_f[:, 0:T], expert_f[:, 0:T], float(CAP), None, ALU.mult))
                dve.tensor_tensor(tile_row[:, 0:T], expert_f[:, 0:T], start_f[:, 0:T], ALU.add).then_inc(m_table, 1)

            def mixture(k):
                t_ = tiles[k]
                HID, T = mixtures[k][1:]

                def work(t, T):
                    a = t.back(1, T)
                    if a:
                        dve.wait_ge(t_["xTp"], a.g + 1)
                        if not early(a, 4):
                            dve.wait_ge(t_["hp"], a.g - 3)
                        dve.tensor_copy(xT_tile[:, a.m % 4, :], (tp, tp3)[a.m % 2][:, 0:P]).then_inc(t_["xT"], 1)
                    a = t.back(2, T)
                    if a and k == 0:
                        dve.wait_ge(t_["act"], a.g + 1)
                        if not early(a, 2):
                            dve.wait_ge(t_["hidTp"], a.g - 1)
                        dve.tensor_tensor(hid[:, a.m % 2, 0:H0], silu[:, a.m % 2, 0:H0],
                                          ring[:, a.m % 2, H0:2 * H0], ALU.mult).then_inc(t_["hid"], 1)
                    a = t.back(3, T)
                    if a and k == 1:
                        dve.wait_ge(t_["hidTp"], a.g + 1)
                        if not early(a, 2):
                            dve.wait_ge(t_["yp"], a.g - 1)
                        dve.tensor_copy(hidT[:, a.m % 2, :], (ring[:, 2, :], small)[a.m % 2][:, 0:HID]).then_inc(
                            t_["hidT"], 1)
                    a = t.back(4, T)
                    if a:
                        dve.wait_ge(t_["yp"], a.g + 1)
                        if not early(a, 4):
                            dve.wait_ge(t_["out"][a.m % 4], 16 * (a.uses(4) - 1))
                        dve.tensor_copy(y_tile[:, a.m % 4, :], heads[:, a.m % 2, 0:D]).then_inc(t_["y"], 1)

                tile_steps(dve, T, work)

            def index(k):
                E = mixtures[k][0]
                ch = Chain(dve, i_chain, 3, k)
                slots = slot_all[:, :, :].rearrange("p g k -> p (g k)")
                cmp = wide[:, 12:12 + 2 * B * E // QN, :].rearrange("p k n -> p (k n)").rearrange("p (g e) -> p g e", e=E)

                def every(t):
                    return t[:, 0:E].rearrange("p (a e) -> p a e", a=1).broadcast_to([P, 2 * B, E])

                ch.step(dve.tensor_tensor(cmp, slots.rearrange("p (g a) -> p g a", a=1).broadcast_to([P, 2 * B, E]),
                                          every(base), ALU.is_ge))
                ch.step(dve.tensor_tensor(cmp, cmp, every(closer), ALU.mult))
                ch.step(dve.tensor_reduce(moved[:, :], cmp, AX.X, ALU.add))
                ch.end()
                dve.tensor_tensor(from_u[:, :], slots, moved[:, :], ALU.add).then_inc(m_from, 1)

            def weight(G, q, k):
                return gate_all[:, bass.ds(G.g * Q + q, 1), k:k + 1].rearrange("p a c -> p (a c)")

            def combine(G, ch, sems):
                dve.wait_ge(sems[G.b], G.u * (2 * Q * 16) + 2 * Q * 16)
                x_of = features(G)
                for k in range(2):
                    for q in range(Q):
                        ins = dve.scalar_tensor_tensor(x_of(q), got[:, G.b, q, k, :], weight(G, q, k), x_of(q), ALU.mult,
                                                       ALU.add)
                    if k == 0:
                        ch.step(ins)
                return ins

            def recurrence(u, more):
                groups = [Group(u, b) for b in range(2)]
                for G in groups:
                    ch = Chain(dve, r_chain, 3, G.g)
                    combine(G, ch, got_in).then_inc(r_combined, 1)
                    dve.wait_ge(r_combined, G.g + 1)
                    apart(dve)
                    moments_of(ch, features(G), stats3, moments3)
                    ch.end()
                    dve.tensor_scalar(var_eps3[:, :], moments3[:, :, 1], EPS, None, ALU.add).then_inc(
                        gates[1]["var"], 1)
                    dve.tensor_scalar(by_graph(adj32[:, G.b, :]), graphs(edges, G.g), 1.0, None, ALU.mult)
                    dve.wait_ge(gates[1]["rstd"], norm(G, 1, 1))
                    if not early(G, 2):
                        dve.wait_ge(sents[1][G.b], G.u * (2 * Q * 16))
                    for q in range(Q):
                        ins = dve.tensor_scalar(yg[:, G.b, q, :], features(G)(q), moments3[:, q, 0:1], rstd3[:, q:q + 1],
                                                ALU.subtract, ALU.mult)
                    ins.then_inc(r_xn, 1)
                for l in range(LAYERS):
                    for G in groups:
                        n = turn(G, l)
                        state, c, z = hT[:, G.b, :], cand[:, G.b, :], gate_z[:, G.b, :]
                        ch = Chain(dve, r_chain2, 3, n - 1)
                        dve.wait_ge(r_sig, 2 * n)
                        ch.step(dve.scalar_tensor_tensor(c, small[:, :], gru_b[:, 1, 2:3], gate_r[:, G.b, :], ALU.add,
                                                         ALU.mult))
                        dve.tensor_tensor(c, c, ring[:, 2, :], ALU.add).then_inc(r_t, 1)
                        dve.wait_ge(r_n, n)
                        ch.step(dve.tensor_tensor(state, state, c, ALU.subtract))
                        ch.step(dve.tensor_tensor(state, state, z, ALU.mult))
                        ch.end()
                        dve.tensor_tensor(state, state, c, ALU.add).then_inc(r_h[G.b], 1)
                for G in groups:
                    dve.wait_ge(r_backp, G.g + 1)
                    dve.tensor_tensor(graphs(xs, G.g), graphs(xs, G.g), by_graph(tp[:, :]), ALU.add).then_inc(r_back, 1)
                    dve.wait_ge(r_back, G.g + 1)
                    apart(dve)
                    normalise_and_gate(G, 1)

            dve.wait_ge(c_bias, 16 * 2 * PARTS)
            bc = Chain(dve, b_chain, 4 * BIAS_STEPS, 0)
            for j in range(E1 * H1 // QN):
                bc.step(split(bc, wide[0:KP, 12 + j, :], c1_parts[:, j * QN:(j + 1) * QN]))
            for j in range(E1 * D // QN):
                bc.step(split(bc, wide[0:KP, 8 + j, :], c2_parts[:, j * QN:(j + 1) * QN]))
            bc.end()
            dve.wait_ge(c_gru, GRU)
            dve.tensor_tensor(bias_rz[:, :], gru_b[:, 0, 0:2], gru_b[:, 1, 0:2], ALU.add)
            attention_steps(dve, work)
            plan(0)
            index(0)
            mixture(0)
            recurrence_steps(dve, recurrence)
            plan(1)
            index(1)
            mixture(1)

            def last(G):
                ch = Chain(dve, last_chain, 1, G.g)
                combine(G, ch, last_in).then_inc(last_done, 1)
            last_steps(dve, last)


PLAN = 18
BIAS_STEPS = E1 * (H1 + D) // QN

WEIGHTS = 16 * (2 + H0 // P)
WEIGHTS1 = 16 * (1 + H1 // P)
GRU = 16 * 5
CONSTS = 32
FIN = 4
FIN2 = 28
SMALL = 16 * (9 + 2 * PARTS)

_INS = ['x', 'adj', 'L0_gnn_W', 'L0_gnn_a1', 'L0_gnn_a2', 'L0_gnn_edge_emb', 'L0_gnn_ln_gamma', 'L0_gnn_ln_beta',
        'L0_ffn_gate_w', 'L0_ffn_gate_b', 'L0_ffn_w1', 'L0_ffn_w2', 'L0_ffn_w3', 'L1_gnn_weight', 'L1_gnn_w_ih',
        'L1_gnn_w_hh', 'L1_gnn_b_ih', 'L1_gnn_b_hh', 'L1_ffn_Wg', 'L1_ffn_bg', 'L1_ffn_W1', 'L1_ffn_b1', 'L1_ffn_W2',
        'L1_ffn_b2']
_OUTS = [((64, 128, 128), 'float32')]


def kernel(**inputs):
    import numpy as _np
    import concourse.bacc as _bacc
    from concourse import mybir as _mybir
    from concourse.bass_utils import run_bass_kernel_spmd as _run

    nc = _bacc.Bacc("TRN2", target_bir_lowering=False, num_devices=1)
    arrays, args = {}, []
    for name in _INS:
        a = _np.ascontiguousarray(inputs[name])
        arrays[f"in_{name}_dram"] = a
        args.append(nc.dram_tensor(f"in_{name}_dram", a.shape, _mybir.dt.from_np(a.dtype), kind="ExternalInput").ap())
    for i, (shape, dtype) in enumerate(_OUTS):
        dt = _mybir.dt.from_np(_np.dtype(dtype))
        args.append(nc.dram_tensor(f"out_{i}_dram", shape, dt, kind="ExternalOutput").ap())
    two_layers(nc, *args)
    r = _run(nc, [arrays], core_ids=[0])
    return r.results[0]["out_0_dram"]
```

```python
import concourse.bass as bass
from concourse import mybir
from contextlib import ExitStack

F32 = mybir.dt.float32
BF16 = mybir.dt.bfloat16
I32 = mybir.dt.int32
U32 = mybir.dt.uint32
ALU = mybir.AluOpType
ACT = mybir.ActivationFunctionType
AX = mybir.AxisListType

P = 128
B = 64
N = 128
D = 128
Q = 4
NG = B // Q
QN = Q * N
H = 8
HD = D // H
PARTS = 3
KP = 32 * (PARTS - 1) + 2 * H
EPS = 1e-5
MASKED = -1e9
LAYERS = 3

E0, H0 = 16, 256
E1, H1 = 8, 512
PAIRS = 2 * B * N
CAP = B * N + P
T0 = PAIRS // P + E0
T1 = PAIRS // P + E1


class Group:

    def __init__(self, u, b):
        self.u, self.b, self.g = u, b, u * 2 + b

    def prev(self):
        return Group(self.u, 0) if self.b else Group(self.u - 1, 1)


class Tile:

    def __init__(self, i, off):
        self.i, self.off, self.g, self.m = i, off, i * 8 + off, off % 8

    def back(self, n, T):
        if isinstance(self.g, int) and not 0 <= self.g - n < T:
            return None
        return Tile(self.i, self.off - n)

    def uses(self, n):
        return self.i * (8 // n) + self.off // n + 1


def early(G, n):
    return isinstance(G.g, int) and G.g < n


class Chain:

    def __init__(self, eng, sem, n, g):
        self.eng, self.sem, self.n, self.g, self.k = eng, sem, n, g, 0

    def step(self, ins, apart=None):
        self.k += 1
        ins.then_inc(self.sem, 1)
        self.eng.wait_ge(self.sem, self.g * self.n + self.k)
        if apart:
            apart(self.eng)

    def end(self):
        assert self.k == self.n, (self.sem, self.k, self.n)


def two_layers(nc, x, adj, gat_w, gat_a1, gat_a2, gat_emb, gat_gamma, gat_beta, gate0_w, gate0_b, w1, w2, w3,
               gru_w, w_ih, w_hh, b_ih, b_hh, gate1_w, gate1_b, v1, c1, v2, c2, out):
    with ExitStack() as ctx:
        def sb(name, shape, dt=F32):
            return ctx.enter_context(nc.sbuf_tensor(name, shape, dt))

        def ps(name, shape, dt=F32):
            return ctx.enter_context(nc.psum_tensor(name, shape, dt))

        def sem(name):
            return ctx.enter_context(nc.semaphore(name))

        ident = sb("ident", [P, P])
        identb = sb("identb", [P, P], BF16)
        before = sb("before", [P, P], BF16)
        onesb = sb("onesb", [P, P], BF16)
        sel = sb("sel", [KP, 2 * H, P], BF16)
        rev = sb("rev", [P, E0])
        base = sb("base", [P, E0])
        not_hi = sb("not_hi", [KP, 1])
        is_lo = sb("is_lo", [KP, 1])
        slope = sb("slope", [KP, 1])
        ones_q = sb("ones_q", [P, Q])
        minus_one = sb("minus_one", [P, Q])
        minus_half = sb("minus_half", [P, Q])
        lane = sb("lane", [P, 1])
        zeros = sb("zeros", [P, D])
        tile_no = sb("tile_no", [1, T0])

        gat_w_sb = sb("gat_w_sb", [P, D])
        a_rows = sb("a_rows", [P, 2, HD])
        wa = sb("wa", [P, 2, H])
        prod = sb("prod", [P, D])
        wa_dup = sb("wa_dup", [P, 2, KP])
        emb = sb("emb", [KP, 1])
        gamma = sb("gamma", [P, D])
        beta = sb("beta", [P, D])
        gate0_sb = sb("gate0_sb", [P, E0])
        gate0_bias = sb("gate0_bias", [P, E0])
        gate1_sb = sb("gate1_sb", [P, E1])
        gate1_bias = sb("gate1_bias", [P, E1])

        xs = sb("xs", [P, B, D])
        edges = sb("edges", [P, B, N], BF16)
        slot_all = sb("slot_all", [P, B, 2])
        gate_all = sb("gate_all", [P, B, 2])

        adj_in = sb("adj_in", [P, 2, Q, N], I32)
        mask = sb("mask", [P, 2, Q, N], BF16)
        stats = sb("stats", [P, Q, 6])
        moments = sb("moments", [P, Q, 2])
        var_eps = sb("var_eps", [P, Q])
        rstd = sb("rstd", [P, Q])
        less_mean = sb("less_mean", [P, Q])
        less_mean3 = sb("less_mean3", [P, Q])
        shift = sb("shift", [P, Q])
        shift3 = sb("shift3", [P, Q])
        stats3 = sb("stats3", [P, Q, 6])
        moments3 = sb("moments3", [P, Q, 2])
        var_eps3 = sb("var_eps3", [P, Q])
        rstd3 = sb("rstd3", [P, Q])
        wide = sb("wide", [P, 20, QN])

        def one(k):
            return wide[:, k, :]

        def pair(k):
            return wide[:, k:k + 2, :]

        def by_graph(t):
            return t.rearrange("p (q d) -> p q d", q=Q)

        y, yT = by_graph(one(0)), one(1)
        values = sb("values", [P, 2, Q, H, HD + 1])
        s2, top, part_b = (wide[0:KP, k, :] for k in (3, 4, 5))
        s1 = [wide[0:KP, k, :] for k in (2, 16)]
        part_a = sb("part_a", [KP, QN], BF16)
        part_c = sb("part_c", [KP, QN], BF16)
        s2_parts = sb("s2_parts", [KP, 2, QN], BF16)
        s1_parts = sb("s1_parts", [KP, 2, QN], BF16)
        rowmax = sb("rowmax", [P, Q, H])
        rowmax_dup = sb("rowmax_dup", [P, Q, KP])
        exp1, exp2, probs = pair(6), pair(8), pair(10)
        rden = sb("rden", [P, 2, Q // 2 * H])
        hn, hneg, hexp, ygT = by_graph(one(12)), by_graph(one(13)), by_graph(one(14)), one(15)
        yg = sb("yg", [P, 2, Q, D])
        lg = sb("lg", [P, Q, E0])
        lg2 = sb("lg2", [P, Q, E0])
        score = sb("score", [P, Q, E0])
        first = sb("first", [P, Q, E0])
        second = sb("second", [P, Q, E0])
        peak = sb("peak", [P, Q, 2])
        rmax = sb("rmax", [P, Q])
        gap = sb("gap", [P, Q])
        egap = sb("egap", [P, Q])
        chosen = sb("chosen", [P, Q, E0], BF16)
        seen = sb("seen", [P, Q + 1, E0], BF16)
        rank = sb("rank", [P, Q, E0])
        slot_f = sb("slot_f", [P, Q, 2])
        slot_u = sb("slot_u", [P, 2, Q, 2], U32)
        wgt = sb("wgt", [P, Q, 2])
        wsum = sb("wsum", [P, Q])

        x_tile = one(0).rearrange("p (k d) -> p k d", k=4)
        xT_tile = one(1).rearrange("p (k d) -> p k d", k=4)
        silu, hid, hidT = pair(2), pair(4), pair(6)
        y_tile = one(8).rearrange("p (k d) -> p k d", k=4)
        counts = sb("counts", [P, E0])
        pad_f = sb("pad_f", [P, E0])
        pad_u = sb("pad_u", [P, E0], U32)
        tiles_i = sb("tiles_i", [P, 2, E0], I32)
        tiles_f = sb("tiles_f", [P, E0])
        ends = sb("ends", [P, 2, E0])
        closer = sb("closer", [P, E0])
        moved = sb("moved", [P, 2 * B])
        expert_f = sb("expert_f", [1, T0])
        start_f = sb("start_f", [1, T0])
        tile_row = sb("tile_row", [1, T0], I32)
        tile_expert = sb("tile_expert", [1, T0], I32)
        w12_sb = sb("w12_sb", [P, E0, 2 * H0])
        w3_sb = sb("w3_sb", [P, E0, H0 // P, D])
        v1_sb = w12_sb[:, 0:E1, :]
        v2_sb = w12_sb[:, E1:2 * E1, :].rearrange("p e (c d) -> p e c d", d=D)
        bias_rows = wide[0:KP, 6:16, :].rearrange("p k n -> p (k n)")
        c1_parts = sb("c1_parts", [KP, E1 * H1], BF16)
        c2_parts = sb("c2_parts", [KP, E1 * D], BF16)

        hT, msg, agg, adj32, gate_r, gate_z, cand = (pair(k) for k in (0, 2, 4, 6, 8, 10, 12))
        xn = values[:, :, :, :, :].rearrange("p b q h d -> p b (q h d)")[:, :, 0:QN].rearrange("p b (q d) -> p b q d", q=Q)
        back = one(14)
        got = wide[:, 16:20, :].rearrange("p (b k) n -> p b (k n)", b=2).rearrange("p b (q k d) -> p b q k d", q=Q, k=2)
        near = sb("near", [P, 2, 2 * Q], U32)
        from_u = sb("from_u", [P, 2 * B], U32)
        gru_w_sb = sb("gru_w_sb", [P, LAYERS, D])
        gru_in = sb("gru_in", [P, 2, 3, D])
        gru_wT = sb("gru_wT", [P, 2, 3, D])
        gru_b = sb("gru_b", [P, 2, 3])
        bias_rz = sb("bias_rz", [P, 2])

        ring = ps("ring", [P, 3, QN])
        tp = ps("tp", [P, QN])
        tp3 = ps("tp3", [P, QN])
        heads = ps("heads", [P, 2, QN])
        small = ps("small", [P, QN])

        rows0 = nc.dram_tensor("rows0", (E0 * CAP + E0 * P, D), F32, kind="Internal").ap()
        outs0 = nc.dram_tensor("outs0", (T0 * P, D), F32, kind="Internal").ap()
        rows1 = nc.dram_tensor("rows1", (E1 * CAP + E1 * P, D), F32, kind="Internal").ap()
        outs1 = nc.dram_tensor("outs1", (T1 * P, D), F32, kind="Internal").ap()

        c_passed, c_consts, c_small, c_wa = sem("c_passed"), sem("c_consts"), sem("c_small"), sem("c_wa")
        x_in = [sem("x_in0"), sem("x_in1")]
        a_mask, a_shift = sem("a_mask"), sem("a_shift")
        a_chain, s_chain, v_chain, f_chain, f_chain2 = (sem(f"{n}_chain") for n in ("ln", "split", "max", "fin", "gate"))
        a_var, a_rstd, a_y, a_yTp, a_yT, a_whp, a_wh = (
            sem(n) for n in ("a_var", "a_rstd", "a_y", "a_yTp", "a_yT", "a_whp", "a_wh"))
        a_s2p, a_s1p, a_s2, a_s1, a_s2parts, a_s1parts = (
            sem(n) for n in ("a_s2p", "a_s1p", "a_s2", "a_s1", "a_s2parts", "a_s1parts"))
        a_maximg, a_rowmax, a_dup, a_maxT = (sem(n) for n in ("a_maximg", "a_rowmax", "a_dup", "a_maxT"))
        p_img1, p_img2, p_exp1, p_exp2, p_probs, p_heads = (
            sem(n) for n in ("p_img1", "p_img2", "p_exp1", "p_exp2", "p_probs", "p_heads"))
        f_divided, f_norm, f_affine, f_shift, f_var, f_rstd, f_neg, f_exp, f_y, f_yTp, f_yT, f_lgp = (
            sem(n) for n in ("f_divided", "f_norm", "f_affine", "f_shift", "f_var", "f_rstd", "f_neg", "f_exp", "f_y", "f_yTp", "f_yT", "f_lgp"))
        g_gap, g_egap, g_chosen, g_rankp, g_slot = (
            sem(n) for n in ("g_gap", "g_egap", "g_chosen", "g_rankp", "g_slot"))
        sent = [sem("sent0"), sem("sent1")]
        stored = sem("stored")
        w_chain, w_ready = sem("w_chain"), sem("w_ready")
        i_chain, m_from, r_near = sem("i_chain"), sem("m_from"), sem("r_near")
        c_zero, b_chain = sem("c_zero"), sem("b_chain")
        c_weights1 = sem("c_weights1")
        c_weights, c_gru, c_gruT, c_bias = sem("c_weights"), sem("c_gru"), sem("c_gruT"), sem("c_bias")
        m_count, m_pad, m_padded, m_table, m_chain = (
            sem(n) for n in ("m_count", "m_pad", "m_padded", "m_table", "m_chain"))
        T_SEMS = ("xTp", "xT", "hp", "act", "hid", "hidTp", "hidT", "yp", "y")
        tiles = [{n: sem(f"t{k}_{n}") for n in T_SEMS} for k in range(2)]
        for k in range(2):
            tiles[k]["in"] = [sem(f"t{k}_in{j}") for j in range(4)]
            tiles[k]["out"] = [sem(f"t{k}_out{j}") for j in range(4)]
        r_combined, r_yTp, r_h0, r_adj, r_mp, r_m, r_aggp, r_agg, r_rz, r_np, r_sig, r_t, r_n, r_backp, r_backc = (
            sem(f"r_{n}") for n in ("combined", "yTp", "h0", "adj", "mp", "m", "aggp", "agg", "rz", "np", "sig", "t",
                                    "n", "backp", "backc"))
        r_h = [sem("r_hA"), sem("r_hB")]
        r_chain, r_chain2, r_xn, r_back = (sem(f"r_{n}") for n in ("chain", "chain2", "xn", "back"))
        got_in = [sem("got_in0"), sem("got_in1")]
        last_done = sem("last_done")
        GATE = ("lg", "ranked", "chain", "var", "rstd", "y", "yTp", "yT", "lgp", "gap", "egap", "chosen", "rankp",
                "slot")
        gates = [dict(zip(GATE, (sem("f_lg"), sem("f_ranked"), f_chain2, f_var, f_rstd, f_y, f_yTp, f_yT, f_lgp, g_gap,
                                 g_egap, g_chosen, g_rankp, g_slot))),
                 {n: sem(f"g1_{n}") for n in GATE}]
        n_var, n_rstd, n_shift, g1_shift = sem("n_var"), sem("n_rstd"), sem("n_shift"), sem("g1_shift")
        n_moments = sem("n_moments")
        h_moments, f_moments, g1_moments = sem("h_moments"), sem("f_moments"), sem("g1_moments")
        sents = [sent, [sem("sent2"), sem("sent3")]]
        rows, results = [rows0, rows1], [outs0, outs1]
        mixtures = [(E0, H0, T0), (E1, H1, T1)]

        block = ctx.enter_context(nc.Block())

        def attention_steps(eng, work):
            def step(G):
                groups = [G]
                for _ in range(4):
                    groups.append(groups[-1].prev())
                work(*(a if not isinstance(a.g, int) or 0 <= a.g < NG else None for a in groups))

            for g in range(6):
                step(Group(g // 2, g % 2))
            with eng.Fori(3, NG // 2) as u:
                step(Group(u, 0))
                step(Group(u, 1))
            for g in range(NG, NG + 4):
                step(Group(g // 2, g % 2))

        def tile_steps(eng, T, work):
            for s in range(8):
                work(Tile(0, s), T)
            with eng.Fori(1, T // 8) as i:
                for c in range(8):
                    work(Tile(i, c), T)
            for s in range(T, T + 6):
                work(Tile(0, s), T)

        def recurrence_steps(eng, work):
            def step(u):
                work(*([Group(v, b) for b in range(2)] if not isinstance(v, int) or 0 <= v < NG // 2 else None
                       for v in (u, u + 1, u - 1, u - 2)))

            for u in range(-1, 3):
                step(u)
            with eng.Fori(3, NG // 2 - 1) as u:
                step(u)
            for u in range(NG // 2 - 1, NG // 2 + 2):
                step(u)

        def turn(G, l):
            return G.u * (2 * LAYERS) + (2 * l + G.b + 1)

        def norm(G, n):
            return G.g * 2 + n

        def last_steps(eng, work):
            work(Group(0, 0))
            work(Group(0, 1))
            with eng.Fori(1, NG // 2) as u:
                work(Group(u, 0))
                work(Group(u, 1))

        def apart(eng):
            eng.sem_inc(c_passed, 1)

        def graphs(t, g):
            return t[:, bass.ds(g * Q, Q)]

        def features(G):
            if isinstance(G.g, int):
                return lambda q: xs[:, G.g * Q + q, :]
            return lambda q: xs[:, bass.ds(G.g * Q + q, 1), :].rearrange("p a f -> p (a f)")

        @block.sync
        def _(sp):
            for dst, src in (
                    (gat_w_sb[:, :], gat_w), (gate0_sb[:, :], gate0_w), (gate1_sb[:, :], gate1_w),
                    (a_rows[:, 0, :], gat_a1.partition_broadcast(P)), (a_rows[:, 1, :], gat_a2.partition_broadcast(P)),
                    (gamma[:, :], gat_gamma.partition_broadcast(P)), (beta[:, :], gat_beta.partition_broadcast(P)),
                    (gate0_bias[:, :], gate0_b.partition_broadcast(P)),
                    (gate1_bias[:, :], gate1_b.partition_broadcast(P))):
                sp.dma_start(dst, src).then_inc(c_small, 16)
            sp.wait_ge(c_consts, 1)
            for c in range(PARTS):
                for k in range(2):
                    r = 32 * c + H * k
                    sp.dma_start(emb[r:r + H, :], gat_emb[1:2, :].rearrange("a h -> h a"),
                                 allow_slow_non_contiguous=True).then_inc(c_small, 16)

            def load(G, M, A, F, S):
                if G:
                    if not early(G, 2):
                        sp.wait_ge(a_mask, G.g - 1)
                    sp.dma_start(graphs(xs, G.g), x[bass.ds(G.g * Q, Q)].rearrange("q n f -> n q f")).then_inc(
                        x_in[G.b], 16)
                    sp.dma_start(adj_in[:, G.b], adj[bass.ds(G.g * Q, Q)].rearrange("q i j -> i q j")).then_inc(
                        x_in[G.b], 16)

            attention_steps(sp, load)

            def mixture(k):
                E, HID, T = mixtures[k]
                t_ = tiles[k]
                sp.wait_ge(m_table, k + 1)
                for b in range(2):
                    sp.wait_ge(sents[k][b], NG // 2 * 2 * Q * 16)
                sp.wait_ge(m_padded, 16 * (E0 + (E1 if k else 0) + 2))

                def work(t, T):
                    a = t.back(0, T)
                    if a:
                        if not early(a, 4):
                            sp.wait_ge(t_["xTp"], a.g - 3)
                        row = sp.value_load(tile_row[0:1, bass.ds(a.g, 1)], min_val=0, max_val=E * CAP + (E - 1) * P)
                        sp.dma_start(x_tile[:, a.m % 4, :], rows[k][bass.ds(row, P), :]).then_inc(
                            t_["in"][a.m % 4], 16)
                    a = t.back(5, T)
                    if a:
                        sp.wait_ge(t_["y"], a.g + 1)
                        sp.dma_start(results[k][bass.ds(a.g * P, P), :], y_tile[:, a.m % 4, :]).then_inc(
                            t_["out"][a.m % 4], 16)

                tile_steps(sp, T, work)

            mixture(0)
            sp.wait_ge(c_zero, 1)
            for c in range(PARTS):
                sp.dma_start(bias_rows[32 * c:32 * c + 1, 0:E1 * H1],
                             c1.rearrange("(a e) h -> a (e h)", a=1)).then_inc(c_bias, 16)
                sp.dma_start(bias_rows[32 * c:32 * c + 1, E1 * H1:],
                             c2.rearrange("(a e) d -> a (e d)", a=1)).then_inc(c_bias, 16)
            mixture(1)

            def store(G):
                sp.wait_ge(last_done, G.g + 1)
                apart(sp)
                sp.dma_start(out[bass.ds(G.g * Q, Q)].rearrange("q n f -> n q f"), graphs(xs, G.g)).then_inc(
                    stored, 16)

            last_steps(sp, store)
            sp.wait_ge(stored, NG * 16)

        @block.gpsimd
        def _(pool):
            pool.memset(emb[:, :], 0.0).then_inc(c_consts, 1)
            k = [1]

            def after(ins):
                k[0] += 1
                ins.then_inc(c_consts, 1)
                pool.wait_ge(c_consts, k[0])

            def choose(t, pattern, base_, mult, op, fill):
                after(pool.affine_select(out=t, in_=t, pattern=pattern, compare_op=op, fill=fill, base=base_,
                                         channel_multiplier=mult))

            after(pool.memset(ident[:, :], 0.0))
            choose(ident[:, :], [[-1, P]], 0, 1, ALU.not_equal, 1.0)
            after(pool.tensor_copy(identb[:, :], ident[:, :]))
            after(pool.memset(before[:, :], 0.0))
            choose(before[:, :], [[-1, P]], 0, 1, ALU.is_ge, 1.0)
            after(pool.memset(onesb[:, :], 1.0))
            after(pool.memset(sel[:, :, :], 0.0))
            for c in range(PARTS):
                choose(sel[:, :, :], [[-1, 2 * H], [0, P]], -32 * c, 1, ALU.not_equal, 1.0)
            after(pool.iota(rev[:, :], [[-1, E0]], base=E0, channel_multiplier=0, allow_small_or_imprecise_dtypes=True))
            after(pool.iota(base[:, :], [[CAP, E0]], base=0, channel_multiplier=0, allow_small_or_imprecise_dtypes=True))
            after(pool.iota(lane[:, :], [[0, 1]], base=0, channel_multiplier=1, allow_small_or_imprecise_dtypes=True))
            after(pool.iota(tile_no[:, :], [[1, T0]], base=0, channel_multiplier=0, allow_small_or_imprecise_dtypes=True))
            after(pool.memset(not_hi[:, :], -1.0))
            choose(not_hi[:, :], [[0, 1]], -32, 1, ALU.is_ge, 0.0)
            after(pool.memset(is_lo[:, :], -1.0))
            choose(is_lo[:, :], [[0, 1]], -64, 1, ALU.is_ge, 0.0)
            after(pool.memset(slope[:, :], 1.0))
            for c in range(PARTS):
                choose(slope[:, :], [[0, 1]], 32 * c + H, -1, ALU.is_gt, 0.2)
                choose(slope[:, :], [[0, 1]], 32 * c + 32, -1, ALU.is_gt, 1.0)
            after(pool.memset(minus_half[:, :], -0.5))
            after(pool.memset(ones_q[:, :], 1.0))
            after(pool.memset(minus_one[:, :], -1.0))
            after(pool.memset(zeros[:, :], 0.0))
            after(pool.memset(wa_dup[:, :, :], 0.0))
            after(pool.memset(rowmax_dup[:, :, :], 0.0))
            after(pool.memset(seen[:, 0, :], 0.0))
            after(pool.memset(values[:, :, :, :, :], 1.0))
            assert k[0] == CONSTS, k[0]

            def work(G, M, A, F, S):
                if F:
                    if not early(F, 1):
                        pool.wait_ge(f_y, F.g)
                    power(F, 0, norm(F, 1))
                    pool.wait_ge(f_rstd, norm(F, 1))
                    pool.tensor_tensor(shift3[:, :], less_mean3[:, :], rstd3[:, :], ALU.mult).then_inc(f_shift, 1)
                    pool.wait_ge(f_norm, F.g + 1)
                    ch = Chain(pool, f_affine, 2, F.g)
                    for t, op in ((gamma, ALU.mult), (beta, ALU.add)):
                        ch.step(pool.tensor_tensor(hn[:, :, :], hn[:, :, :], t[:, :].rearrange("p (a f) -> p a f", a=1)
                                                   .broadcast_to([P, Q, D]), op), apart)
                    ch.end()
                    pool.tensor_scalar(hneg[:, :, :], hn[:, :, :], 0.0, None, ALU.min).then_inc(f_neg, 1)
                if G:
                    pool.wait_ge(a_var, G.g + 1)
                    if not early(G, 1):
                        pool.wait_ge(a_y, G.g)
                    pool.tensor_tensor(rstd[:, :], var_eps[:, :], minus_half[:, :], ALU.pow).then_inc(a_rstd, 1)
                    pool.wait_ge(a_rstd, G.g + 1)
                    pool.tensor_tensor(shift[:, :], less_mean[:, :], rstd[:, :], ALU.mult).then_inc(a_shift, 1)
                if S and not early(S, 1):
                    send(S.prev(), 0)
                if F:
                    power(F, 0, norm(F, 2))
                    pool.wait_ge(f_rstd, norm(F, 2))
                    pool.tensor_tensor(shift3[:, :], less_mean3[:, :], rstd3[:, :], ALU.mult).then_inc(f_shift, 1)

            def power(G, k, n):
                pool.wait_ge(gates[k]["var"], n)
                pool.tensor_tensor(rstd3[:, :], var_eps3[:, :], minus_half[:, :], ALU.pow).then_inc(
                    gates[k]["rstd"], 1)

            def weights(G, layer):
                ch = Chain(pool, w_chain, 3, G.g + layer * NG)
                pool.wait_ge(gates[layer]["egap"], G.g + 1)
                apart(pool)
                if layer == 0:
                    ch.step(pool.tensor_tensor(wsum[:, :], egap[:, :], ones_q[:, :], ALU.add))
                    ch.step(pool.tensor_tensor(wgt[:, :, 0], wsum[:, :], minus_one[:, :], ALU.pow))
                    pool.tensor_tensor(wgt[:, :, 1], wgt[:, :, 0], egap[:, :], ALU.mult).then_inc(w_ready, 1)
                else:
                    ch.step(pool.tensor_copy(wgt[:, :, 1], egap[:, :]))
                    ch.step(pool.tensor_tensor(wgt[:, :, 0], ones_q[:, :], egap[:, :], ALU.subtract), apart)
                    pool.tensor_copy(wsum[:, :], wgt[:, :, 0]).then_inc(w_ready, 1)
                pool.wait_ge(w_ready, G.g + (layer * NG + 1))
                apart(pool)
                ch.step(pool.tensor_copy(graphs(gate_all, G.g), wgt[:, :, :]))
                ch.end()

            def send(G, layer):
                weights(G, layer)
                pool.wait_ge(gates[layer]["slot"], G.g + 1)
                apart(pool)
                for q in range(Q):
                    for k in range(2):
                        pool.indirect_dma_start(
                            rows[layer], bass.IndirectOffsetOnAxis(ap=slot_u[:, G.b, q, k:k + 1], axis=0),
                            yg[:, G.b, q, :], None).then_inc(sents[layer][G.b], 16)

            def fetch(G, layer, combined):
                if not early(G, 2):
                    pool.wait_ge(combined, G.g - 1)
                    apart(pool)
                pool.tensor_copy(near[:, G.b], from_u[:, bass.ds(G.g * (2 * Q), 2 * Q)]).then_inc(
                    r_near, 1)
                pool.wait_ge(r_near, G.g + (layer * NG + 1))
                apart(pool)
                for q in range(Q):
                    for k in range(2):
                        pool.indirect_dma_start(
                            got[:, G.b, q, k, :], None, results[layer],
                            bass.IndirectOffsetOnAxis(ap=near[:, G.b, 2 * q + k:2 * q + k + 1], axis=0)).then_inc(got_in[G.b], 16)

            def pad(k):
                pool.wait_ge(m_pad, k + 1)
                for e in range(mixtures[k][0]):
                    pool.indirect_dma_start(rows[k], bass.IndirectOffsetOnAxis(ap=pad_u[:, e:e + 1], axis=0),
                                            zeros[:, :], None).then_inc(m_padded, 16)

            def results_stored(k):
                T = mixtures[k][2]
                pool.wait_ge(m_from, k + 1)
                for j in range(4):
                    pool.wait_ge(tiles[k]["out"][j], T // 4 * 16)

            for k in range(2):
                E = mixtures[k][0]
                pool.dma_start(rows[k][E * CAP:, :].rearrange("(e p) d -> p e d", p=P),
                               zeros[:, :].rearrange("p (e d) -> p e d", e=1).broadcast_to([P, E, D])).then_inc(
                    m_padded, 16)
            attention_steps(pool, work)
            send(Group(NG // 2 - 1, 1), 0)
            pad(0)
            results_stored(0)
            def recurrence(R, N, C, L):
                def scale(G):
                    if not early(G, 1):
                        pool.wait_ge(gates[1]["y"], G.g)
                    power(G, 1, G.g + 1)
                    pool.wait_ge(gates[1]["rstd"], G.g + 1)
                    pool.tensor_tensor(shift3[:, :], less_mean3[:, :], rstd3[:, :], ALU.mult).then_inc(g1_shift, 1)

                def scale_n(G):
                    pool.wait_ge(n_var, G.g + 1)
                    if not early(G, 1):
                        pool.wait_ge(r_xn, G.g)
                    pool.tensor_tensor(rstd[:, :], var_eps[:, :], minus_half[:, :], ALU.pow).then_inc(n_rstd, 1)
                    pool.wait_ge(n_rstd, G.g + 1)
                    pool.tensor_tensor(shift[:, :], less_mean[:, :], rstd[:, :], ALU.mult).then_inc(n_shift, 1)

                if L:
                    send(L[0], 1)
                if C:
                    scale(C[0])
                if N:
                    fetch(N[0], 0, r_combined)
                if L:
                    send(L[1], 1)
                if C:
                    scale(C[1])
                if N:
                    if R:
                        scale_n(N[0])
                        fetch(N[1], 0, r_combined)
                    else:
                        fetch(N[1], 0, r_combined)
                        scale_n(N[0])
                    scale_n(N[1])

            recurrence_steps(pool, recurrence)
            for b in range(2):
                pool.wait_ge(sents[1][b], NG // 2 * 2 * Q * 16)
            pad(1)
            results_stored(1)
            last_steps(pool, lambda G: fetch(G, 1, last_done))

        @block.tensor
        def _(pe):
            pe.wait_ge(c_consts, CONSTS)
            pe.wait_ge(c_wa, 8)

            def transpose_x(G):
                pe.wait_ge(a_y, G.g + 1)
                if not early(G, 1):
                    pe.wait_ge(a_wh, G.g)
                for q in range(Q):
                    ins = pe.transpose(tp[:, q * P:(q + 1) * P], y[:, q, :], ident[:, :])
                ins.then_inc(a_yTp, 1)

            def score_s2(G):
                pe.wait_ge(a_yT, G.g + 1)
                pe.matmul(tp[0:KP, :], wa_dup[:, 1, :], yT[:, :], start=True, stop=True).then_inc(a_s2p, 1)

            def score_s1(G):
                pe.wait_ge(a_s2, G.g + 1)
                pe.matmul(tp[0:KP, :], wa_dup[:, 0, :], yT[:, :], start=True, stop=True).then_inc(a_s1p, 1)

            def product(G):
                pe.wait_ge(a_s1, G.g + 1)
                for q in range(Q):
                    ins = pe.matmul(tp[:, q * P:(q + 1) * P], yT[:, q * P:(q + 1) * P], gat_w_sb[:, :],
                                    start=True, stop=True)
                ins.then_inc(a_whp, 1)

            def max_image(G, h):
                if h == 0:
                    pe.wait_ge(a_s2parts, G.g + 1)
                    pe.wait_ge(a_mask, G.g + 1)
                    if not early(G, 1):
                        pe.wait_ge(a_s1parts, G.g)
                elif h == 1:
                    if not early(G, 4):
                        pe.wait_ge(gates[0]["ranked"], G.g - 3)
                else:
                    pe.wait_ge(a_rowmax, H * G.g + h - 1)
                bank = (ring[:, 2, :], small[:, :])[h % 2]
                pe.matmul(bank, sel[:, h, :], s2_parts[:, G.b, :], start=True, stop=False)
                pe.matmul(bank, identb[:, :], mask[:, G.b].rearrange("p q n -> p (q n)"),
                          start=False, stop=True).then_inc(a_maximg, 1)

            def image(G, h, k):
                bank = ring[:, k, :]
                row = sel[:, H * k + h, :]
                if not (h == 0 and early(G, 1)):
                    pe.wait_ge((p_exp1, p_exp2)[k], H * G.g + h)
                pe.matmul(bank, row, s1_parts[:, G.b, :], start=True, stop=False)
                for q in range(Q):
                    cols = slice(q * P, (q + 1) * P)
                    pe.matmul(bank[:, cols], s2_parts[:, G.b, cols], row, start=False, stop=False)
                    ins = pe.matmul(bank[:, cols], mask[:, G.b, q, :], identb[:, :], start=False, stop=(q == Q - 1))
                ins.then_inc((p_img1, p_img2)[k], 1)

            def attend_head(G, h):
                pe.wait_ge(p_probs, H * G.g + h + 1)
                if h == 0:
                    pe.wait_ge(a_wh, G.g + 1)
                    if not early(G, 1):
                        pe.wait_ge(f_divided, 2 * G.g)
                for q in range(Q):
                    c = (q % 2) * H * (HD + 1) + h * (HD + 1)
                    ins = pe.matmul(heads[:, q // 2, c:c + HD + 1], probs[:, h % 2, q * P:(q + 1) * P],
                                    values[:, G.b, q, h, :], start=True, stop=True, skip_group_check=True)
                ins.then_inc(p_heads, 1)

            def transpose_yg(G, k):
                gs = gates[k]
                pe.wait_ge(gs["y"], G.g + 1)
                if not early(G, 1):
                    pe.wait_ge(gs["lg"], G.g)
                for q in range(Q):
                    ins = pe.transpose(tp3[:, q * P:(q + 1) * P], yg[:, G.b, q, :], ident[:, :])
                ins.then_inc(gs["yTp"], 1)

            def logits(G, k):
                E, gs, gate_w = mixtures[k][0], gates[k], (gate0_sb, gate1_sb)[k]
                pe.wait_ge(gs["yT"], G.g + 1)
                for q in range(Q):
                    ins = pe.matmul(tp3[:, q * E:(q + 1) * E], ygT[:, q * P:(q + 1) * P], gate_w[:, :],
                                    start=True, stop=True)
                ins.then_inc(gs["lgp"], 1)

            def ranks(G, k):
                E, gs = mixtures[k][0], gates[k]
                bank = (small, tp)[k][:, 0:Q * E]
                pe.wait_ge(gs["chosen"], G.g + 1)
                if not early(G, 1):
                    pe.wait_ge(gs["ranked"], G.g)
                pe.matmul(bank, before[:, :], chosen[:, :, 0:E], start=True, stop=False)
                pe.matmul(bank, onesb[:, :], seen[:, 0:Q, 0:E], start=False, stop=True).then_inc(
                    gs["rankp"], 1)

            def work(G, M, A, F, S):
                if A:
                    pe.wait_ge(a_s1parts, A.g + 1)
                for h in range(H + 1):
                    if A and h < H:
                        image(A, h, 0)
                        image(A, h, 1)
                    if M and 1 <= h <= H // 2:
                        max_image(M, 2 * h - 2)
                        max_image(M, 2 * h - 1)
                    if A and h > 0:
                        attend_head(A, h - 1)
                    if M and h == 5:
                        pe.wait_ge(a_dup, M.g + 1)
                        for q in range(Q):
                            ins = pe.transpose(ring[0:KP, 2, q * P:(q + 1) * P], rowmax_dup[:, q, :], ident[:, :])
                        ins.then_inc(a_maxT, 1)
                    if G:
                        {4: transpose_x, 5: score_s2, 6: score_s1, 7: product}.get(h, lambda G: None)(G)
                    if F:
                        {7: transpose_yg, 8: logits}.get(h, lambda G, k: None)(F, 0)
                    if S and h == 6:
                        if M:
                            pe.wait_ge(a_rowmax, H * (M.g + 1))
                        ranks(S, 0)

            def count(k):
                E = mixtures[k][0]
                pe.wait_ge(gates[k]["slot"], NG)
                pe.matmul(small[:, 0:E], onesb[:, :], seen[:, Q, 0:E], start=True, stop=True).then_inc(m_count, 1)

            def mixture(k):
                E, HID, T = mixtures[k]
                C = HID // P
                t_ = tiles[k]
                w_in, w_out = ((w12_sb, w3_sb), (v1_sb, v2_sb))[k]
                pe.wait_ge(m_table, k + 1)
                pe.wait_ge(*((c_weights, WEIGHTS), (c_weights1, WEIGHTS1))[k])
                xT_banks, h_banks, hT_banks, y_banks = (tp, tp3), (ring[:, 0], ring[:, 1]), (ring[:, 2], small), (
                    heads[:, 0], heads[:, 1])

                experts = {}

                def expert(a):
                    key = (id(a.i), a.off)
                    if key not in experts:
                        experts[key] = pe.value_load(tile_expert[0:1, bass.ds(a.g, 1)], min_val=0, max_val=E - 1)
                    return experts[key]

                def work(t, T):
                    a = t.back(2, T)
                    if a:
                        expert(a)
                    a = t.back(1, T)
                    if a:
                        pe.wait_ge(t_["in"][a.m % 4], 16 * a.uses(4))
                        if not early(a, 2):
                            pe.wait_ge(t_["xT"], a.g - 1)
                        pe.transpose(xT_banks[a.m % 2][:, 0:P], x_tile[:, a.m % 4, :], ident[:, :]).then_inc(
                            t_["xTp"], 1)
                    a = t.back(2, T)
                    if a:
                        e = expert(a)
                        bank = h_banks[a.m % 2]
                        pe.wait_ge(t_["xT"], a.g + 1)
                        if not early(a, 2):
                            pe.wait_ge(t_["hid"], a.g - 1)
                        ins = pe.matmul(bank, xT_tile[:, a.m % 4, :], w_in[:, bass.ds(e, 1), :], start=True,
                                        stop=(k == 0))
                        if k:
                            ins = pe.matmul(bank, onesb[0:KP, :], c1_parts[:, bass.ds(e * H1, H1)], start=False,
                                            stop=True)
                        ins.then_inc(t_["hp"], 1)
                    a = t.back(3, T)
                    if a:
                        pe.wait_ge(t_["hid"], a.g + 1)
                        if not early(a, 2):
                            pe.wait_ge(t_["hidT"], a.g - 1)
                        for c in range(C):
                            ins = pe.transpose(hT_banks[a.m % 2][:, c * P:(c + 1) * P],
                                               hid[:, a.m % 2, c * P:(c + 1) * P], ident[:, :])
                        ins.then_inc(t_["hidTp"], 1)
                    a = t.back(4, T)
                    if a:
                        e = expert(a)
                        bank = y_banks[a.m % 2][:, 0:D]
                        pe.wait_ge(t_["hidT"], a.g + 1)
                        if not early(a, 2):
                            pe.wait_ge(t_["y"], a.g - 1)
                        for c in range(C):
                            ins = pe.matmul(bank, hidT[:, a.m % 2, c * P:(c + 1) * P],
                                            w_out[:, bass.ds(e, 1), c, :], start=(c == 0),
                                            stop=(k == 0 and c == C - 1))
                        if k:
                            ins = pe.matmul(bank, onesb[0:KP, :], c2_parts[:, bass.ds(e * D, D)], start=False,
                                            stop=True)
                        ins.then_inc(t_["yp"], 1)

                tile_steps(pe, T, work)

            def turnover(R, C, L, b):
                if C:
                    G = C[b]
                    pe.wait_ge(r_h[b], (G.u + 1) * LAYERS)
                    for q in range(Q):
                        ins = pe.transpose(heads[:, b, q * P:(q + 1) * P], hT[:, b, q * P:(q + 1) * P], ident[:, :])
                    ins.then_inc(r_backp, 1)
                if R:
                    G = R[b]
                    pe.wait_ge(r_xn, G.g + 1)
                    for q in range(Q):
                        ins = pe.transpose(heads[:, 1 - b, q * P:(q + 1) * P], xn[:, b, q, :], ident[:, :])
                    ins.then_inc(r_yTp, 1)
                    pe.wait_ge(r_h0, G.g + 1)

            def layer(G, l):
                n = turn(G, l)
                first_one = isinstance(n, int) and n == 1
                bank, state = heads[:, G.b, :], hT[:, G.b, :]
                if l:
                    pe.wait_ge(r_h[G.b], G.u * LAYERS + l)
                for q in range(Q):
                    ins = pe.matmul(bank[:, q * P:(q + 1) * P], state[:, q * P:(q + 1) * P], gru_w_sb[:, l, :],
                                    start=True, stop=True)
                ins.then_inc(r_mp, 1)
                if not first_one:
                    pe.wait_ge(r_sig, 2 * n - 3)
                pe.matmul(ring[:, 0, :], gru_wT[:, 1, 0, :], state, start=True, stop=False)
                if not first_one:
                    pe.wait_ge(r_sig, 2 * n - 2)
                pe.matmul(ring[:, 1, :], gru_wT[:, 1, 1, :], state, start=True, stop=False)
                pe.wait_ge(r_m, n)
                if l == 0:
                    pe.wait_ge(r_adj, G.g + 1)
                for q in range(Q):
                    ins = pe.matmul(bank[:, q * P:(q + 1) * P], msg[:, G.b, q * P:(q + 1) * P],
                                    adj32[:, G.b, q * P:(q + 1) * P], start=True, stop=True)
                ins.then_inc(r_aggp, 1)
                if not first_one:
                    pe.wait_ge(r_t, n - 1)
                pe.matmul(small[:, :], gru_wT[:, 1, 2, :], state, start=True, stop=True)
                pe.wait_ge(r_agg, n)
                pe.matmul(ring[:, 0, :], gru_wT[:, 0, 0, :], agg[:, G.b, :], start=False, stop=True).then_inc(r_rz, 1)
                pe.matmul(ring[:, 1, :], gru_wT[:, 0, 1, :], agg[:, G.b, :], start=False, stop=True).then_inc(r_rz, 1)
                pe.matmul(ring[:, 2, :], gru_wT[:, 0, 2, :], agg[:, G.b, :], start=True, stop=True).then_inc(r_np, 1)

            def recurrence(R, N, C, L):
                for l in range(LAYERS):
                    for b in range(2):
                        if l == 0:
                            turnover(R, C, L, b)
                        if R:
                            layer(R[b], l)
                        if l == 0 and b == 1 and L:
                            ranks(L[1], 1)
                        if C and l == 1 and b == 0:
                            transpose_yg(C[0], 1)
                        if C and l == 1 and b == 1:
                            logits(C[0], 1)
                        if C and l == 2 and b == 0:
                            transpose_yg(C[1], 1)
                        if C and l == 2 and b == 1:
                            logits(C[1], 1)
                            ranks(C[0], 1)

            pe.wait_ge(c_gru, GRU)
            for k in range(2):
                for c in range(3):
                    ins = pe.transpose((tp, tp3)[k][:, c * P:(c + 1) * P], gru_in[:, k, c, :], ident[:, :])
            ins.then_inc(c_gruT, 1)
            pe.wait_ge(c_gruT, 3)
            attention_steps(pe, work)
            count(0)
            mixture(0)
            recurrence_steps(pe, recurrence)
            count(1)
            mixture(1)

        @block.scalar
        def _(act):
            act.wait_ge(c_consts, CONSTS)
            act.wait_ge(c_small, SMALL)

            def normal_x(G):
                act.wait_ge(a_shift, G.g + 1)
                apart(act)
                for q in range(Q):
                    ins = act.activation(y[:, q, :], features(G)(q), ACT.Identity, scale=rstd[:, q:q + 1],
                                         bias=shift[:, q:q + 1])
                ins.then_inc(a_y, 1)

            def normal_h(G):
                act.wait_ge(f_shift, 2 * G.g + 1)
                for q in range(Q):
                    ins = act.activation(hn[:, q, :], hn[:, q, :], ACT.Identity, scale=rstd3[:, q:q + 1],
                                         bias=shift3[:, q:q + 1])
                ins.then_inc(f_norm, 1)

            def normal_yg(G, k):
                act.wait_ge(*((f_shift, 2 * G.g + 2), (g1_shift, G.g + 1))[k])
                if not early(G, 2):
                    act.wait_ge(sents[k][G.b], G.u * (2 * Q * 16))
                apart(act)
                for q in range(Q):
                    ins = act.activation(yg[:, G.b, q, :], features(G)(q), ACT.Identity, scale=rstd3[:, q:q + 1],
                                         bias=shift3[:, q:q + 1])
                ins.then_inc(gates[k]["y"], 1)

            def copy_yT(G):
                act.wait_ge(a_yTp, G.g + 1)
                act.copy(yT[:, :], tp[:, :]).then_inc(a_yT, 1)

            def scale_s2(G):
                act.wait_ge(a_s2p, G.g + 1)
                if not early(G, 1):
                    act.wait_ge(a_s2parts, G.g)
                act.activation(s2[:, :], tp[0:KP, :], ACT.Copy, scale=slope[:, 0:1]).then_inc(a_s2, 1)

            def copy_s1(G):
                act.wait_ge(a_s1p, G.g + 1)
                if not early(G, 2):
                    act.wait_ge(a_s1parts, G.g - 1)
                act.activation(s1[G.b][:, :], tp[0:KP, :], ACT.Identity, bias=emb[:, 0:1]).then_inc(a_s1, 1)

            def edge_masks(G):
                act.wait_ge(x_in[G.b], 32 * G.u + 32)
                apart(act)
                act.copy(graphs(edges, G.g), adj_in[:, G.b])
                act.activation(mask[:, G.b], adj_in[:, G.b], ACT.Copy, scale=-MASKED, bias=MASKED).then_inc(a_mask, 1)

            def work(G, M, A, F, S):
                for h in range(H):
                    if A:
                        if not (early(A, 1) and h < 2):
                            act.wait_ge(p_probs, H * A.g + h - 1)
                        act.wait_ge(p_img1, H * A.g + h + 1)
                        act.activation(exp1[:, h % 2, :], ring[:, 0, :], ACT.Exp).then_inc(p_exp1, 1)
                        act.wait_ge(p_img2, H * A.g + h + 1)
                        act.activation(exp2[:, h % 2, :], ring[:, 1, :], ACT.Exp).then_inc(p_exp2, 1)
                    if G:
                        {4: copy_yT, 5: scale_s2, 6: copy_s1}.get(h, lambda G: None)(G)
                    if F and h == 3:
                        act.wait_ge(f_neg, F.g + 1)
                        act.activation(hexp[:, :, :], hneg[:, :, :], ACT.Exp).then_inc(f_exp, 1)
                    if F and h == 1:
                        normal_h(F)
                    if G and h == 3:
                        normal_x(G)
                    if F and h == 6:
                        normal_yg(F, 0)
                if F:
                    copy_ygT(F, 0)
                if G:
                    edge_masks(G)
                    act.wait_ge(a_whp, G.g + 1)
                    if A:
                        act.wait_ge(p_heads, H * (A.g + 1))
                    act.copy(values[:, G.b, :, :, 0:HD].rearrange("p q h d -> p (q h) d"),
                             tp[:, :].rearrange("p (a d) -> p a d", d=HD)).then_inc(a_wh, 1)
                if S:
                    gap_exp(S, 0)

            def copy_ygT(G, k):
                gs = gates[k]
                act.wait_ge(gs["yTp"], G.g + 1)
                act.copy(ygT[:, :], tp3[:, :]).then_inc(gs["yT"], 1)

            def gap_exp(G, k):
                gs = gates[k]
                if k or not early(G, 1):
                    act.wait_ge(w_ready, G.g + k * NG)
                act.wait_ge(gs["gap"], G.g + 1)
                act.activation(egap[:, :], gap[:, :], (ACT.Exp, ACT.Sigmoid)[k]).then_inc(gs["egap"], 1)

            def mixture(k):
                t_ = tiles[k]
                HID, T = mixtures[k][1:]

                def work(t, T):
                    a = t.back(2, T)
                    if a:
                        act.wait_ge(t_["hp"], a.g + 1)
                        bank = ring[:, a.m % 2, :]
                        if k == 0:
                            if not early(a, 2):
                                act.wait_ge(t_["hid"], a.g - 1)
                            act.activation(silu[:, a.m % 2, 0:H0], bank[:, 0:H0], ACT.Silu).then_inc(t_["act"], 1)
                        else:
                            if not early(a, 2):
                                act.wait_ge(t_["hidTp"], a.g - 1)
                            act.activation(hid[:, a.m % 2, :], bank, ACT.Gelu).then_inc(t_["hid"], 1)
                    a = t.back(3, T)
                    if a and k == 0:
                        act.wait_ge(t_["hidTp"], a.g + 1)
                        if not early(a, 2):
                            act.wait_ge(t_["yp"], a.g - 1)
                        act.copy(hidT[:, a.m % 2, 0:HID], (ring[:, 2, :], small)[a.m % 2][:, 0:HID]).then_inc(
                            t_["hidT"], 1)

                tile_steps(act, T, work)

            def messages(G, l):
                act.wait_ge(r_mp, turn(G, l))
                act.copy(msg[:, G.b, :], heads[:, G.b, :]).then_inc(r_m, 1)

            def layer(G, l):
                n = turn(G, l)
                act.wait_ge(r_aggp, n)
                act.copy(agg[:, G.b, :], heads[:, G.b, :]).then_inc(r_agg, 1)
                act.wait_ge(r_rz, 2 * n - 1)
                act.activation(gate_r[:, G.b, :], ring[:, 0, :], ACT.Sigmoid, bias=bias_rz[:, 0:1]).then_inc(r_sig, 1)
                act.wait_ge(r_rz, 2 * n)
                act.activation(gate_z[:, G.b, :], ring[:, 1, :], ACT.Sigmoid, bias=bias_rz[:, 1:2]).then_inc(r_sig, 1)
                act.wait_ge(r_t, n)
                act.activation(cand[:, G.b, :], cand[:, G.b, :], ACT.Tanh, bias=gru_b[:, 0, 2:3]).then_inc(r_n, 1)

            def normal_xn(G):
                act.wait_ge(n_shift, G.g + 1)
                apart(act)
                for q in range(Q):
                    ins = act.activation(xn[:, G.b, q, :], features(G)(q), ACT.Identity, scale=rstd[:, q:q + 1],
                                         bias=shift[:, q:q + 1])
                ins.then_inc(r_xn, 1)

            def recurrence(R, N, C, L):
                for l in range(LAYERS):
                    for b in range(2):
                        if C and l == 0:
                            act.wait_ge(r_backp, C[b].g + 1)
                            if not early(C[b], 1):
                                act.wait_ge(r_back, C[b].g)
                            act.copy(back[:, :], heads[:, b, :]).then_inc(r_backc, 1)
                        if R and l == 0:
                            G = R[b]
                            act.wait_ge(r_yTp, G.g + 1)
                            act.copy(hT[:, b, :], heads[:, 1 - b, :]).then_inc(r_h0, 1)
                            act.copy(by_graph(adj32[:, b, :]), graphs(edges, G.g)).then_inc(r_adj, 1)
                        if R:
                            messages(R[b], l)
                        if l == 0 and b == 0:
                            if R:
                                normal_xn(R[1])
                            if L:
                                gap_exp(L[0], 1)
                        if l == 1 and b == 0:
                            if L:
                                gap_exp(L[1], 1)
                            if C:
                                normal_yg(C[0], 1)
                        if C and l == 1 and b == 1:
                            copy_ygT(C[0], 1)
                        if C and l == 2 and b == 0:
                            normal_yg(C[1], 1)
                        if l == 2 and b == 1:
                            if N:
                                normal_xn(N[0])
                            if C:
                                copy_ygT(C[1], 1)
                        if R:
                            layer(R[b], l)

            act.dma_start(gru_w_sb[:, :, :], gru_w.rearrange("l d e -> d l e")).then_inc(c_gru, 16)
            for k, w in enumerate((w_ih, w_hh)):
                act.dma_start(gru_in[:, k], w.rearrange("(c e) d -> e c d", c=3)).then_inc(c_gru, 16)
            for k, w in enumerate((b_ih, b_hh)):
                act.dma_start(gru_b[:, k, :], w.rearrange("(c e) -> e c", c=3),
                              allow_slow_non_contiguous=True).then_inc(c_gru, 16)
            act.dma_start(w12_sb[:, :, 0:H0], w1.rearrange("e d h -> d e h")).then_inc(c_weights, 16)
            act.dma_start(w12_sb[:, :, H0:2 * H0], w2.rearrange("e d h -> d e h")).then_inc(c_weights, 16)
            for c in range(H0 // P):
                act.dma_start(w3_sb[:, :, c, :], w3[:, c * P:(c + 1) * P, :].rearrange("e k o -> k e o")).then_inc(
                    c_weights, 16)
            act.wait_ge(c_gruT, 1)
            for k in range(2):
                act.copy(gru_wT[:, k].rearrange("p c e -> p (c e)"), (tp, tp3)[k][:, 0:3 * P]).then_inc(c_gruT, 1)
            attention_steps(act, work)
            mixture(0)
            act.wait_ge(tiles[0]["yp"], T0)
            act.dma_start(v1_sb, v1.rearrange("e d h -> d e h")).then_inc(c_weights1, 16)
            for c in range(H1 // P):
                act.dma_start(v2_sb[:, :, c, :], v2[:, c * P:(c + 1) * P, :].rearrange("e k o -> k e o")).then_inc(
                    c_weights1, 16)
            recurrence_steps(act, recurrence)
            mixture(1)

        @block.vector
        def _(dve):
            dve.wait_ge(c_consts, CONSTS)
            dve.wait_ge(c_small, SMALL)
            for k in range(2):
                dve.tensor_tensor(prod[:, :].rearrange("p (h d) -> p h d", d=HD),
                                  gat_w_sb[:, :].rearrange("p (h d) -> p h d", d=HD),
                                  a_rows[:, k:k + 1, :].broadcast_to([P, H, HD]), ALU.mult).then_inc(c_wa, 1)
                dve.wait_ge(c_wa, 2 * k + 1)
                dve.tensor_reduce(wa[:, k, :], prod[:, :].rearrange("p (h d) -> p h d", d=HD), AX.X,
                                  ALU.add).then_inc(c_wa, 1)
                dve.wait_ge(c_wa, 2 * k + 2)
            for k in range(2):
                for c in range(2):
                    view = wa_dup[:, k, H * c:H * c + H]
                    dst = bass.AP(view.tensor, view.offset, [view.ap[0], [32, PARTS], [1, H]])
                    dve.tensor_copy(dst, wa[:, k:k + 1, :].broadcast_to([P, PARTS, H])).then_inc(c_wa, 1)

            def moments_of(ch, src, stats_, moments_):
                for q in range(Q):
                    ins = dve.bn_stats(stats_[:, q, :], src(q))
                ch.step(ins, apart)
                for q in range(Q):
                    ins = dve.bn_aggr(moments_[:, q, :], stats_[:, q, :])
                ch.step(ins)

            def split(ch, src):
                ch.step(dve.tensor_copy(part_a[:, :], src))
                ch.step(dve.scalar_tensor_tensor(part_b[:, :], part_a[:, :], not_hi[:, 0:1], src, ALU.mult, ALU.add))
                ch.step(dve.tensor_copy(part_c[:, :], part_b[:, :]))

            def last_part(dst):
                return dve.scalar_tensor_tensor(dst, part_c[:, :], is_lo[:, 0:1], part_b[:, :], ALU.mult, ALU.add)

            def normal_x_a(G):
                ch = Chain(dve, a_chain, 2, G.g)
                dve.wait_ge(x_in[G.b], 32 * G.u + 32)
                if not early(G, 1):
                    dve.wait_ge(a_shift, G.g)
                apart(dve)
                moments_of(ch, features(G), stats, moments)
                ch.end()
                dve.tensor_scalar(less_mean[:, :], moments[:, :, 0], -1.0, None, ALU.mult)
                dve.tensor_scalar(var_eps[:, :], moments[:, :, 1], EPS, None, ALU.add).then_inc(a_var, 1)

            def spread_maxima(G):
                dve.wait_ge(a_rowmax, H * G.g + H)
                for c in range(PARTS):
                    view = rowmax_dup[:, :, 32 * c:32 * c + 2 * H].rearrange("p q (k h) -> p q k h", k=2)
                    ins = dve.tensor_copy(view, rowmax[:, :, :].rearrange("p q (k h) -> p q k h", k=1).broadcast_to(
                        [P, Q, 2, H]))
                ins.then_inc(a_dup, 1)

            def subtract_maxima(G):
                ch = Chain(dve, v_chain, 6, G.g)
                s1_ = s1[G.b]
                dve.wait_ge(a_maxT, G.g + 1)
                dve.wait_ge(a_s1, G.g + 1)
                ch.step(dve.tensor_tensor(top[:, :], s1_[:, :], ring[0:KP, 2, :], ALU.add))
                ch.step(dve.scalar_tensor_tensor(top[:, :], top[:, :], 0.2, top[:, :], ALU.mult, ALU.max))
                ch.step(dve.scalar_tensor_tensor(top[:, :], s1_[:, :], slope[:, 0:1], top[:, :], ALU.mult,
                                                 ALU.subtract))
                split(ch, top[:, :])
                last_part(s1_parts[:, G.b, :]).then_inc(a_s1parts, 1)
                ch.end()

            def divide(G):
                dve.wait_ge(p_heads, H * (G.g + 1))
                view = heads[:, :, 0:2 * H * (HD + 1)].rearrange("p a (h d) -> p a h d", d=HD + 1)
                dve.reciprocal(rden[:, :, :], view[:, :, :, HD]).then_inc(f_divided, 1)
                dve.wait_ge(f_divided, 2 * G.g + 1)
                dve.tensor_tensor(hn[:, :, :].rearrange("p (a b) (h d) -> p a (b h) d", a=2, d=HD),
                                  view[:, :, :, 0:HD],
                                  rden[:, :, :].rearrange("p a (h d) -> p a h d", d=1).broadcast_to(
                                      [P, 2, 2 * H, HD]), ALU.mult).then_inc(f_divided, 1)
                if not early(G, 1):
                    dve.wait_ge(f_shift, 2 * G.g)
                dve.wait_ge(f_divided, 2 * G.g + 2)
                apart(dve)
                moments_of(Chain(dve, h_moments, 2, G.g), lambda q: hn[:, q, :], stats3, moments3)
                dve.tensor_scalar(less_mean3[:, :], moments3[:, :, 0], -1.0, None, ALU.mult)
                dve.tensor_scalar(var_eps3[:, :], moments3[:, :, 1], EPS, None, ALU.add).then_inc(f_var, 1)

            def elu(G):
                ch = Chain(dve, f_chain, FIN, G.g)
                dve.wait_ge(f_exp, G.g + 1)
                ch.step(dve.scalar_tensor_tensor(hn[:, :, :], hn[:, :, :], 0.0, hexp[:, :, :], ALU.max, ALU.add))
                ch.step(dve.scalar_tensor_tensor(graphs(xs, G.g), hn[:, :, :], -1.0, graphs(xs, G.g), ALU.add,
                                                 ALU.add), apart)
                ch.end()

            def normal_a(G, layer):
                if layer and not early(G, 1):
                    dve.wait_ge(g1_shift, G.g)
                    apart(dve)
                moments_of(Chain(dve, (f_moments, g1_moments)[layer], 2, G.g), features(G), stats3, moments3)
                dve.tensor_scalar(less_mean3[:, :], moments3[:, :, 0], -1.0, None, ALU.mult)
                dve.tensor_scalar(var_eps3[:, :], moments3[:, :, 1], EPS, None, ALU.add).then_inc(
                    gates[layer]["var"], 1)

            def wide_of(t, E):
                return t.rearrange("p (q a) -> p q a", a=1).broadcast_to([P, Q, E])

            def largest(ch, src, E, k, one):
                S = score[:, :, 0:E]
                ch.step(dve.tensor_reduce(peak[:, :, k], src, AX.X, ALU.max))
                ch.step(dve.tensor_tensor(S, src, peak[:, :, k:k + 1].broadcast_to([P, Q, E]), ALU.is_equal))
                ch.step(dve.tensor_tensor(S, S, rev[:, 0:E].rearrange("p (a e) -> p a e", a=1).broadcast_to([P, Q, E]),
                                          ALU.mult))
                ch.step(dve.tensor_reduce(rmax[:, :], S, AX.X, ALU.max))
                ch.step(dve.tensor_tensor(one, S, wide_of(rmax[:, :], E), ALU.is_equal))

            def choose_first(G, layer, ch):
                gs, E, bias = gates[layer], mixtures[layer][0], (gate0_bias, gate1_bias)[layer]
                L, F1 = lg[:, :, 0:E], first[:, :, 0:E]
                dve.wait_ge(gs["lgp"], G.g + 1)
                dve.tensor_tensor(L, tp3[:, 0:Q * E].rearrange("p (q e) -> p q e", e=E),
                                  bias[:, 0:E].rearrange("p (a e) -> p a e", a=1).broadcast_to([P, Q, E]),
                                  ALU.add).then_inc(gs["lg"], 1)
                dve.wait_ge(gs["lg"], G.g + 1)
                largest(ch, L, E, 0, F1)
                ch.step(dve.scalar_tensor_tensor(lg2[:, :, 0:E], F1, -3e38, L, ALU.mult, ALU.add))

            def choose_second(G, layer, ch):
                gs, E = gates[layer], mixtures[layer][0]
                F1, F2 = first[:, :, 0:E], second[:, :, 0:E]
                largest(ch, lg2[:, :, 0:E], E, 1, F2)
                if not early(G, 1):
                    dve.wait_ge(gs["egap"], G.g)
                dve.tensor_tensor(gap[:, :], peak[:, :, 1], peak[:, :, 0], ALU.subtract).then_inc(gs["gap"], 1)
                ch.step(dve.tensor_tensor(chosen[:, :, 0:E], F1, F2, ALU.add))
                if not early(G, 1):
                    ch.step(dve.tensor_copy(seen[:, 0, 0:E], seen[:, Q, 0:E]))
                else:
                    ch.step(dve.memset(seen[:, 0, 0:E], 0.0))
                for q in range(Q):
                    ins = dve.tensor_tensor(seen[:, q + 1, 0:E], seen[:, q, 0:E], chosen[:, q, 0:E], ALU.add)
                    if q < Q - 1:
                        ch.step(ins)
                ins.then_inc(gs["chosen"], 1)

            def pick_slots(G, layer, ch):
                gs, E = gates[layer], mixtures[layer][0]
                S, F1, F2 = score[:, :, 0:E], first[:, :, 0:E], second[:, :, 0:E]
                dve.wait_ge(gs["rankp"], G.g + 1)
                dve.tensor_tensor(rank[:, :, 0:E], (small, tp)[layer][:, 0:Q * E].rearrange("p (q e) -> p q e", e=E),
                                  base[:, 0:E].rearrange("p (a e) -> p a e", a=1).broadcast_to([P, Q, E]),
                                  ALU.add).then_inc(gs["ranked"], 1)
                dve.wait_ge(gs["ranked"], G.g + 1)
                for k, one in enumerate((F1, F2)):
                    ch.step(dve.tensor_tensor(S, one, rank[:, :, 0:E], ALU.mult))
                    ch.step(dve.tensor_reduce(slot_f[:, :, k], S, AX.X, ALU.add))
                ch.step(dve.tensor_scalar(graphs(slot_all, G.g), slot_f[:, :, :], 1.0, None, ALU.mult))
                if not early(G, 2):
                    dve.wait_ge(sents[layer][G.b], G.u * (2 * Q * 16))
                    apart(dve)
                dve.tensor_copy(slot_u[:, G.b], slot_f[:, :, :]).then_inc(gs["slot"], 1)

            def work(G, M, A, F, S):
                if S:
                    gate = Chain(dve, f_chain2, FIN2, S.g)
                for h in range(H + 1):
                    if A and h < H:
                        if not (early(A, 1) and h < 2):
                            dve.wait_ge(p_heads, H * A.g + h - 1)
                        dve.wait_ge(p_exp2, H * A.g + h + 1)
                        dve.tensor_tensor(probs[:, h % 2, :], exp1[:, h % 2, :], exp2[:, h % 2, :],
                                          ALU.max).then_inc(p_probs, 1)
                    if M and 1 <= h <= H // 2:
                        for k, bank in ((2 * h - 2, ring[:, 2, :]), (2 * h - 1, small[:, :])):
                            dve.wait_ge(a_maximg, H * M.g + k + 1)
                            dve.tensor_reduce(rowmax[:, :, k], bank.rearrange("p (q n) -> p q n", q=Q), AX.X,
                                              ALU.max).then_inc(a_rowmax, 1)
                    if G and h == 1:
                        normal_x_a(G)
                    if F and h == 3:
                        elu(F)
                    if F and h == 4:
                        normal_a(F, 0)
                    if M and h == 4:
                        spread_maxima(M)
                    if S and h == 1:
                        choose_first(S, 0, gate)
                    if S and h == 5:
                        choose_second(S, 0, gate)
                    if M and h == 6:
                        subtract_maxima(M)
                    if S and h == 7:
                        pick_slots(S, 0, gate)
                        gate.end()
                    if G and h == 7:
                        sc = Chain(dve, s_chain, 3, G.g)
                        dve.wait_ge(a_s2, G.g + 1)
                        split(sc, s2[:, :])
                if G:
                    last_part(s2_parts[:, G.b, :]).then_inc(a_s2parts, 1)
                    sc.end()
                if A:
                    divide(A)

            def plan(k):
                E, HID, T = mixtures[k]
                ch = Chain(dve, m_chain, PLAN, 0)
                ch.k = PLAN if k else 0
                dve.wait_ge(m_count, k + 1)
                if k:
                    dve.wait_ge(m_padded, 16 * (E0 + 2))
                ch.step(dve.tensor_copy(counts[:, 0:E], small[:, 0:E]))
                ch.step(dve.tensor_tensor(pad_f[:, 0:E], counts[:, 0:E], base[:, 0:E], ALU.add))
                dve.tensor_scalar(pad_u[:, 0:E], pad_f[:, 0:E], lane[:, 0:1], None, ALU.add).then_inc(m_pad, 1)
                ch.step(dve.tensor_scalar(tiles_i[:, 0, 0:E], counts[:, 0:E], float(P - 1), None, ALU.add))
                ch.step(dve.tensor_scalar(tiles_i[:, 1, 0:E], tiles_i[:, 0, 0:E], P.bit_length() - 1, None,
                                          ALU.logical_shift_right))
                ch.step(dve.tensor_copy(tiles_f[:, 0:E], tiles_i[:, 1, 0:E]))
                ch.step(dve.tensor_copy(ends[:, 0, 0:E], tiles_f[:, 0:E]))
                dve.memset(closer[:, 0:1], 0.0)
                dve.tensor_scalar(closer[:, 1:E], tiles_f[:, 0:E - 1], float(P), -float(CAP), ALU.mult, ALU.add)
                src, step = 0, 1
                while step < E:
                    dve.tensor_copy(ends[:, 1 - src, 0:step], ends[:, src, 0:step])
                    ch.step(dve.tensor_tensor(ends[:, 1 - src, step:E], ends[:, src, step:E],
                                              ends[:, src, 0:E - step], ALU.add))
                    src, step = 1 - src, 2 * step
                flat = wide[0:1, :, :].rearrange("p k n -> p (k n)")
                past = flat[:, 0:T * E].rearrange("p (t e) -> p t e", e=E)
                held = flat[:, T0 * E0:T0 * E0 + T * E].rearrange("p (t e) -> p t e", e=E)

                def per_tile(t):
                    return t.rearrange("p (a e) -> p a e", a=1).broadcast_to([1, T, E])

                ch.step(dve.tensor_tensor(past, tile_no[:, 0:T].rearrange("p (t a) -> p t a", a=1).broadcast_to(
                    [1, T, E]), per_tile(ends[0:1, src, 0:E]), ALU.is_ge))
                ch.step(dve.tensor_tensor(held, past, per_tile(tiles_f[0:1, 0:E]), ALU.mult))
                ch.step(dve.tensor_reduce(expert_f[:, 0:T], past, AX.X, ALU.add))
                ch.step(dve.tensor_reduce(start_f[:, 0:T], held, AX.X, ALU.add))
                ch.step(dve.tensor_tensor(start_f[:, 0:T], tile_no[:, 0:T], start_f[:, 0:T], ALU.subtract))
                ch.step(dve.tensor_scalar(start_f[:, 0:T], start_f[:, 0:T], float(P), None, ALU.mult))
                ch.step(dve.tensor_scalar(tile_expert[:, 0:T], expert_f[:, 0:T], float(E - 1), None, ALU.min))
                ch.step(dve.tensor_scalar(expert_f[:, 0:T], expert_f[:, 0:T], float(CAP), None, ALU.mult))
                dve.tensor_tensor(tile_row[:, 0:T], expert_f[:, 0:T], start_f[:, 0:T], ALU.add).then_inc(m_table, 1)

            def mixture(k):
                t_ = tiles[k]
                HID, T = mixtures[k][1:]

                def work(t, T):
                    a = t.back(1, T)
                    if a:
                        dve.wait_ge(t_["xTp"], a.g + 1)
                        if not early(a, 4):
                            dve.wait_ge(t_["hp"], a.g - 3)
                        dve.tensor_copy(xT_tile[:, a.m % 4, :], (tp, tp3)[a.m % 2][:, 0:P]).then_inc(t_["xT"], 1)
                    a = t.back(2, T)
                    if a and k == 0:
                        dve.wait_ge(t_["act"], a.g + 1)
                        if not early(a, 2):
                            dve.wait_ge(t_["hidTp"], a.g - 1)
                        dve.tensor_tensor(hid[:, a.m % 2, 0:H0], silu[:, a.m % 2, 0:H0],
                                          ring[:, a.m % 2, H0:2 * H0], ALU.mult).then_inc(t_["hid"], 1)
                    a = t.back(3, T)
                    if a and k == 1:
                        dve.wait_ge(t_["hidTp"], a.g + 1)
                        if not early(a, 2):
                            dve.wait_ge(t_["yp"], a.g - 1)
                        dve.tensor_copy(hidT[:, a.m % 2, :], (ring[:, 2, :], small)[a.m % 2][:, 0:HID]).then_inc(
                            t_["hidT"], 1)
                    a = t.back(4, T)
                    if a:
                        dve.wait_ge(t_["yp"], a.g + 1)
                        if not early(a, 4):
                            dve.wait_ge(t_["out"][a.m % 4], 16 * (a.uses(4) - 1))
                        dve.tensor_copy(y_tile[:, a.m % 4, :], heads[:, a.m % 2, 0:D]).then_inc(t_["y"], 1)

                tile_steps(dve, T, work)

            def index(k):
                E = mixtures[k][0]
                ch = Chain(dve, i_chain, 3, k)
                slots = slot_all[:, :, :].rearrange("p g k -> p (g k)")
                cmp = wide[:, 12:12 + 2 * B * E // QN, :].rearrange("p k n -> p (k n)").rearrange("p (g e) -> p g e", e=E)

                def every(t):
                    return t[:, 0:E].rearrange("p (a e) -> p a e", a=1).broadcast_to([P, 2 * B, E])

                ch.step(dve.tensor_tensor(cmp, slots.rearrange("p (g a) -> p g a", a=1).broadcast_to([P, 2 * B, E]),
                                          every(base), ALU.is_ge))
                ch.step(dve.tensor_tensor(cmp, cmp, every(closer), ALU.mult))
                ch.step(dve.tensor_reduce(moved[:, :], cmp, AX.X, ALU.add))
                ch.end()
                dve.tensor_tensor(from_u[:, :], slots, moved[:, :], ALU.add).then_inc(m_from, 1)

            def weight(G, q, k):
                return gate_all[:, bass.ds(G.g * Q + q, 1), k:k + 1].rearrange("p a c -> p (a c)")

            def combine(G, layer):
                ch = Chain(dve, r_chain, 1, G.g + layer * NG)
                dve.wait_ge(got_in[G.b], G.u * (2 * Q * 16) + (layer * (NG // 2) + 1) * 2 * Q * 16)
                x_of = features(G)
                for k in range(2):
                    for q in range(Q):
                        ins = dve.scalar_tensor_tensor(x_of(q), got[:, G.b, q, k, :], weight(G, q, k), x_of(q), ALU.mult,
                                                       ALU.add)
                    if k == 0:
                        ch.step(ins)
                return ins

            def combine_l0(G):
                combine(G, 0).then_inc(r_combined, 1)

            def normal_n(G):
                dve.wait_ge(r_combined, G.g + 1)
                if not early(G, 1):
                    dve.wait_ge(n_shift, G.g)
                apart(dve)
                moments_of(Chain(dve, n_moments, 2, G.g), features(G), stats, moments)
                dve.tensor_scalar(less_mean[:, :], moments[:, :, 0], -1.0, None, ALU.mult)
                dve.tensor_scalar(var_eps[:, :], moments[:, :, 1], EPS, None, ALU.add).then_inc(n_var, 1)

            def take_back(G):
                dve.wait_ge(r_backc, G.g + 1)
                dve.tensor_tensor(graphs(xs, G.g), graphs(xs, G.g), by_graph(back[:, :]), ALU.add).then_inc(r_back, 1)

            def layer(G, l):
                n = turn(G, l)
                state, c, z = hT[:, G.b, :], cand[:, G.b, :], gate_z[:, G.b, :]
                ch = Chain(dve, r_chain2, 3, n - 1)
                dve.wait_ge(r_sig, 2 * n - 1)
                ch.step(dve.scalar_tensor_tensor(c, small[:, :], gru_b[:, 1, 2:3], gate_r[:, G.b, :], ALU.add,
                                                 ALU.mult))
                dve.wait_ge(r_np, n)
                dve.tensor_tensor(c, c, ring[:, 2, :], ALU.add).then_inc(r_t, 1)
                dve.wait_ge(r_sig, 2 * n)
                ch.step(dve.tensor_tensor(state, state, z, ALU.mult))
                dve.wait_ge(r_n, n)
                ch.step(dve.scalar_tensor_tensor(c, z, 1.0, c, ALU.subtract, ALU.mult))
                ch.end()
                dve.tensor_tensor(state, state, c, ALU.subtract).then_inc(r_h[G.b], 1)

            def gate1(G, k):
                ch = Chain(dve, gates[1]["chain"], FIN2, G.g)
                ch.k = k
                return ch

            def recurrence(R, N, C, L):
                for l in range(LAYERS):
                    for b in range(2):
                        if C and l == 0:
                            take_back(C[b])
                        if R:
                            layer(R[b], l)
                        if C and l == 0:
                            dve.wait_ge(r_back, C[b].g + 1)
                            apart(dve)
                            normal_a(C[b], 1)
                        if L and l == 0 and b == 0:
                            choose_second(L[1], 1, gate1(L[1], CHOOSE1))
                        if L and l == 0 and b == 1:
                            ch = gate1(L[1], CHOOSE2)
                            pick_slots(L[1], 1, ch)
                            ch.end()
                        if N and l == 1 and b == 0:
                            combine_l0(N[0])
                            normal_n(N[0])
                            if not R:
                                bias_parts(5, 7)
                        if l == 1 and b == 1:
                            if C:
                                choose_first(C[0], 1, gate1(C[0], 0))
                        if l == 2 and b == 0:
                            if C:
                                choose_second(C[0], 1, gate1(C[0], CHOOSE1))
                            if N:
                                combine_l0(N[1])
                        if N and l == 2 and b == 1:
                            normal_n(N[1])
                            if not R:
                                bias_parts(7, BIAS_BLOCKS)
                        if C and l == 2 and b == 1:
                            pick_slots(C[0], 1, gate1(C[0], CHOOSE2))
                            choose_first(C[1], 1, gate1(C[1], 0))

            def load_bias():
                for j in range(4):
                    dve.wait_ge(tiles[0]["out"][j], T0 // 4 * 16)
                dve.memset(bias_rows[:, :], 0.0).then_inc(c_zero, 1)
                dve.wait_ge(c_bias, 16 * 2 * PARTS)

            def bias_parts(start, stop):
                for j in range(start, stop):
                    bc = Chain(dve, b_chain, 4, j)
                    cols = slice(j * QN, (j + 1) * QN)
                    split(bc, bias_rows[:, cols])
                    dst = c1_parts[:, cols] if j < C1_BLOCKS else c2_parts[:, (j - C1_BLOCKS) * QN:(j + 1 - C1_BLOCKS) * QN]
                    bc.step(last_part(dst))
                    bc.end()

            dve.wait_ge(c_gru, GRU)
            dve.tensor_tensor(bias_rz[:, :], gru_b[:, 0, 0:2], gru_b[:, 1, 0:2], ALU.add)
            attention_steps(dve, work)
            plan(0)
            index(0)
            mixture(0)
            load_bias()
            bias_parts(0, 5)
            recurrence_steps(dve, recurrence)
            plan(1)
            index(1)
            mixture(1)

            def last(G):
                combine(G, 1).then_inc(last_done, 1)
            last_steps(dve, last)


PLAN = 18
C1_BLOCKS = E1 * H1 // QN
BIAS_BLOCKS = E1 * (H1 + D) // QN

WEIGHTS = 16 * (2 + H0 // P)
WEIGHTS1 = 16 * (1 + H1 // P)
GRU = 16 * 5
CONSTS = 34
FIN = 2
FIN2 = 21
CHOOSE1 = 6
CHOOSE2 = 16
SMALL = 16 * (9 + 2 * PARTS)

_INS = ['x', 'adj', 'L0_gnn_W', 'L0_gnn_a1', 'L0_gnn_a2', 'L0_gnn_edge_emb', 'L0_gnn_ln_gamma', 'L0_gnn_ln_beta',
        'L0_ffn_gate_w', 'L0_ffn_gate_b', 'L0_ffn_w1', 'L0_ffn_w2', 'L0_ffn_w3', 'L1_gnn_weight', 'L1_gnn_w_ih',
        'L1_gnn_w_hh', 'L1_gnn_b_ih', 'L1_gnn_b_hh', 'L1_ffn_Wg', 'L1_ffn_bg', 'L1_ffn_W1', 'L1_ffn_b1', 'L1_ffn_W2',
        'L1_ffn_b2']
_OUTS = [((64, 128, 128), 'float32')]


def kernel(**inputs):
    import numpy as _np
    import concourse.bacc as _bacc
    from concourse import mybir as _mybir
    from concourse.bass_utils import run_bass_kernel_spmd as _run

    nc = _bacc.Bacc("TRN2", target_bir_lowering=False, num_devices=1)
    arrays, args = {}, []
    for name in _INS:
        a = _np.ascontiguousarray(inputs[name])
        arrays[f"in_{name}_dram"] = a
        args.append(nc.dram_tensor(f"in_{name}_dram", a.shape, _mybir.dt.from_np(a.dtype), kind="ExternalInput").ap())
    for i, (shape, dtype) in enumerate(_OUTS):
        dt = _mybir.dt.from_np(_np.dtype(dtype))
        args.append(nc.dram_tensor(f"out_{i}_dram", shape, dt, kind="ExternalOutput").ap())
    two_layers(nc, *args)
    r = _run(nc, [arrays], core_ids=[0])
    return r.results[0]["out_0_dram"]
```
